# Optimizing a Trainium2 kernel written in Bass

```python
import numpy as np
import jax
import jax.numpy as jnp

def _softmax(x, axis=-1):
    return jax.nn.softmax(x, axis=axis)

def _gelu(x):
    return jax.nn.gelu(x, approximate=True)

def _silu(x):
    return jax.nn.silu(x)

def _sigmoid(x):
    return jax.nn.sigmoid(x)

def _layernorm(x, axis=-1, eps=1e-05):
    m = jnp.mean(x, axis=axis, keepdims=True)
    v = jnp.var(x, axis=axis, keepdims=True)
    return (x - m) / jnp.sqrt(v + eps)

def _scatter_add(tgt, idx, src, axis=0):
    return tgt.at[idx].add(src)

def _segment_sum(src, seg, n):
    return jax.ops.segment_sum(src, seg, n)
kernel_name = 'mk_perceiver_d2_seqx_r8_3079ad'

def setup_inputs(seed: int=0):
    np.random.seed(seed)
    _w = jnp.asarray

    def _rec_inputs():
        import jax
        import jax.numpy as jnp
        _rk = jax.random.key(seed)
        x = -0.0003929 + 0.9999 * jax.random.normal(jax.random.fold_in(_rk, 1), (64, 32, 256), jnp.float32)
        _lenS = 32 - jax.random.randint(jax.random.fold_in(_rk, 7), (64,), 0, max(1, 32 // 4) + 1, jnp.int32)
        _lenS2 = 257 - jax.random.randint(jax.random.fold_in(_rk, 8), (64,), 0, max(1, 257 // 4) + 1, jnp.int32)
        _ctx_1024P = jax.random.normal(jax.random.fold_in(_rk, 11), (64, 16, 128), jnp.float32)
        _ctx_1024c = jax.random.dirichlet(jax.random.fold_in(_rk, 511), 0.3 * jnp.ones((16,), jnp.float32), (64, 257))
        _ctx_1024t = jnp.einsum('bsk,bkd->bsd', _ctx_1024c, _ctx_1024P)
        _ctx_1024t = _ctx_1024t * jax.lax.rsqrt(jnp.mean(jnp.square(_ctx_1024t)) + 1e-12) * 0.953939
        ctx_1024 = -0.000494167 + 1.00018 * (_ctx_1024t + 0.3 * jax.random.normal(jax.random.fold_in(_rk, 611), (64, 257, 128), jnp.float32))
        _validS = jnp.arange(32)[None, :] < _lenS[:, None]
        _validS2 = jnp.arange(257)[None, :] < _lenS2[:, None]
        _causal = jnp.tril(jnp.ones((32, 32), dtype=bool))
        mask_BxS2_bf1 = jnp.ones((64, 257), dtype=bool)
        return (x, ctx_1024, mask_BxS2_bf1)
    x, ctx_1024, mask_BxS2_bf1 = _rec_inputs()

    def _L0_xattn_setup():
        import jax, jax.numpy as jnp
        import numpy as np
        N_HEADS = 16
        N_KV_HEADS = 8
        HEAD_DIM = 128
        D_TEXT = 256
        D_VISION = 128
        GROUPS = N_HEADS // N_KV_HEADS
        key = jax.random.key(seed)
        ks = jax.random.split(key, 6)
        B, T_text, T_vis = (4, 256, 72)
        text_hidden = jax.random.normal(ks[0], (B, T_text, D_TEXT), dtype=jnp.float32)
        vision_tokens = jax.random.normal(ks[1], (B, T_vis, D_VISION), dtype=jnp.float32)
        vision_mask = jnp.ones((B, T_vis), dtype=bool)
        s = 0.02
        Wq = jax.random.normal(ks[2], (D_TEXT, N_HEADS * HEAD_DIM), dtype=jnp.float32) * s
        Wk = jax.random.normal(ks[3], (D_VISION, N_KV_HEADS * HEAD_DIM), dtype=jnp.float32) * s
        Wv = jax.random.normal(ks[4], (D_VISION, N_KV_HEADS * HEAD_DIM), dtype=jnp.float32) * s
        Wo = jax.random.normal(ks[5], (N_HEADS * HEAD_DIM, D_TEXT), dtype=jnp.float32) * s
        return {'text_hidden': text_hidden, 'vision_tokens': vision_tokens, 'vision_mask': vision_mask, 'Wq': Wq, 'Wk': Wk, 'Wv': Wv, 'Wo': Wo}
    _L0_xattn_all = _L0_xattn_setup()
    _L0_xattn_in = {k: v for k, v in _L0_xattn_all.items() if k in ('Wq', 'Wk', 'Wv', 'Wo')}
    del _L0_xattn_all

    def _L0_attn_setup():
        import jax, jax.numpy as jnp
        import numpy as np
        B, S, D, H = (2, 256, 256, 16)
        HD = D // H
        key = jax.random.key(seed)
        ks = jax.random.split(key, 5)
        scale = 0.02
        return {'hidden_states': jax.random.normal(ks[0], (B, S, D), dtype=jnp.float32), 'Wqkv_w': jax.random.normal(ks[1], (3 * D, D), dtype=jnp.float32) * scale, 'Wqkv_b': jax.random.normal(ks[2], (3 * D,), dtype=jnp.float32) * scale, 'out_w': jax.random.normal(ks[3], (D, D), dtype=jnp.float32) * scale, 'out_b': jax.random.normal(ks[4], (D,), dtype=jnp.float32) * scale}
    _L0_attn_all = _L0_attn_setup()
    _L0_attn_in = {k: v for k, v in _L0_attn_all.items() if k in ('Wqkv_w', 'Wqkv_b', 'out_w', 'out_b')}
    del _L0_attn_all

    def _L0_ffn_setup():
        import jax, jax.numpy as jnp
        import numpy as np
        B, S, H = (2, 128, 256)
        E, K, F = (64, 8, 96)
        CAP = 64
        key = jax.random.key(seed)
        k1, k2, k3, k4, k5 = jax.random.split(key, 5)
        scale_h = 1.0 / np.sqrt(H)
        scale_f = 1.0 / np.sqrt(F)
        return {'hidden_states': jax.random.normal(k1, (B, S, H), jnp.float32), 'router_w': jax.random.normal(k2, (E, H), jnp.float32) * scale_h, 'w_gate': jax.random.normal(k3, (E, H, F), jnp.float32) * scale_h, 'w_up': jax.random.normal(k4, (E, H, F), jnp.float32) * scale_h, 'w_down': jax.random.normal(k5, (E, F, H), jnp.float32) * scale_f}
    _L0_ffn_all = _L0_ffn_setup()
    _L0_ffn_in = {k: v for k, v in _L0_ffn_all.items() if k in ('router_w', 'w_gate', 'w_up', 'w_down')}
    del _L0_ffn_all

    def _L1_xattn_setup():
        import jax, jax.numpy as jnp
        import numpy as np
        EPS = 1e-05

        def rmsnorm(x, g, eps=EPS):
            var = jnp.mean(jnp.square(x), axis=-1, keepdims=True)
            return x * jax.lax.rsqrt(var + eps) * g
        key = jax.random.key(seed)
        ks = jax.random.split(key, 8)
        B, Sq, Skv = (2, 512, 64)
        dim, cdim, H, D = (256, 128, 16, 128)
        inner = H * D
        s = lambda f: 1.0 / np.sqrt(f)
        return {'hidden_states': jax.random.normal(ks[0], (B, Sq, dim), jnp.float32), 'encoder_hidden_states': jax.random.normal(ks[1], (B, Skv, cdim), jnp.float32), 'Wq': jax.random.normal(ks[2], (dim, inner), jnp.float32) * s(dim), 'Wk': jax.random.normal(ks[3], (cdim, inner), jnp.float32) * s(cdim), 'Wv': jax.random.normal(ks[4], (cdim, inner), jnp.float32) * s(cdim), 'Wo': jax.random.normal(ks[5], (inner, dim), jnp.float32) * s(inner), 'gq': jnp.ones((D,), jnp.float32), 'gk': jnp.ones((D,), jnp.float32)}
    _L1_xattn_all = _L1_xattn_setup()
    _L1_xattn_in = {k: v for k, v in _L1_xattn_all.items() if k in ('Wq', 'Wk', 'Wv', 'Wo', 'gq', 'gk')}
    del _L1_xattn_all

    def _L1_attn_setup():
        import jax, jax.numpy as jnp
        import numpy as np
        BLOCK = 32
        NUM_HEADS = 16
        HEAD_DIM = 128
        FP4_GRID = jnp.array([0.0, 0.5, 1.0, 1.5, 2.0, 3.0, 4.0, 6.0], dtype=jnp.float32)

        def quantize_to_mxfp4(w, block_size=BLOCK):
            D, F = w.shape
            blocks = w.reshape(D // block_size, block_size, F)
            amax = jnp.max(jnp.abs(blocks), axis=1)
            e = jnp.floor(jnp.log2(jnp.maximum(amax, 1e-12) / 6.0))
            scale = jnp.exp2(e)
            v = blocks / scale[:, None, :]
            idx = jnp.argmin(jnp.abs(jnp.abs(v)[..., None] - FP4_GRID), axis=-1)
            codes = jnp.sign(v) * FP4_GRID[idx]
            return (codes.reshape(D, F).astype(jnp.float32), scale.astype(jnp.float32))

        def _mxfp4_matmul(x, codes, scales, block_size=BLOCK):
            w = codes * jnp.repeat(scales, block_size, axis=0)
            return x @ w
        key = jax.random.key(seed)
        ks = jax.random.split(key, 9)
        B, S, D = (2, 256, 256)
        feat = NUM_HEADS * HEAD_DIM
        x = jax.random.normal(ks[0], (B, S, D), dtype=jnp.float32)

        def make_w(k, din, dout):
            w = jax.random.normal(k, (din, dout), dtype=jnp.float32) * (1.0 / np.sqrt(din))
            return quantize_to_mxfp4(w, BLOCK)
        wq_codes, wq_scales = make_w(ks[1], D, feat)
        wk_codes, wk_scales = make_w(ks[2], D, feat)
        wv_codes, wv_scales = make_w(ks[3], D, feat)
        wo_codes, wo_scales = make_w(ks[4], feat, D)
        bq = jnp.zeros((feat,), jnp.float32)
        bk = jnp.zeros((feat,), jnp.float32)
        bv = jnp.zeros((feat,), jnp.float32)
        bo = jnp.zeros((D,), jnp.float32)
        return {'x': x, 'wq_codes': wq_codes, 'wq_scales': wq_scales, 'bq': bq, 'wk_codes': wk_codes, 'wk_scales': wk_scales, 'bk': bk, 'wv_codes': wv_codes, 'wv_scales': wv_scales, 'bv': bv, 'wo_codes': wo_codes, 'wo_scales': wo_scales, 'bo': bo}
    _L1_attn_all = _L1_attn_setup()
    _L1_attn_in = {k: v for k, v in _L1_attn_all.items() if k in ('wq_codes', 'wq_scales', 'bq', 'wk_codes', 'wk_scales', 'bk', 'wv_codes', 'wv_scales', 'bv', 'wo_codes', 'wo_scales', 'bo')}
    del _L1_attn_all

    def _L1_ffn_setup():
        import jax, jax.numpy as jnp
        import numpy as np
        NUM_EXPERTS = 8
        HIDDEN = 256
        INTER = 256
        TOP_K = 2
        key = jax.random.key(seed)
        ks = jax.random.split(key, 7)
        hidden_states = jax.random.normal(ks[0], (4, 256, HIDDEN), dtype=jnp.float32)
        gate_w = jax.random.normal(ks[1], (HIDDEN, NUM_EXPERTS), dtype=jnp.float32) * 0.02
        fc1_w = jax.random.normal(ks[2], (NUM_EXPERTS, HIDDEN, INTER), dtype=jnp.float32) * 0.02
        fc1_b = jnp.zeros((NUM_EXPERTS, INTER), dtype=jnp.float32)
        fc2_w = jax.random.normal(ks[3], (NUM_EXPERTS, INTER, HIDDEN), dtype=jnp.float32) * 0.02
        fc2_b = jnp.zeros((NUM_EXPERTS, HIDDEN), dtype=jnp.float32)
        alpha = jax.random.normal(ks[4], (NUM_EXPERTS,), dtype=jnp.float32)
        return {'hidden_states': hidden_states, 'gate_w': gate_w, 'fc1_w': fc1_w, 'fc1_b': fc1_b, 'fc2_w': fc2_w, 'fc2_b': fc2_b, 'alpha': alpha}
    _L1_ffn_all = _L1_ffn_setup()
    _L1_ffn_in = {k: v for k, v in _L1_ffn_all.items() if k in ('gate_w', 'fc1_w', 'fc1_b', 'fc2_w', 'fc2_b', 'alpha')}
    del _L1_ffn_all
    return {'x': x, 'ctx_1024': ctx_1024, 'mask_BxS2_bf1': mask_BxS2_bf1, 'L0_xattn_Wq': _L0_xattn_in['Wq'], 'L0_xattn_Wk': _L0_xattn_in['Wk'], 'L0_xattn_Wv': _L0_xattn_in['Wv'], 'L0_xattn_Wo': _L0_xattn_in['Wo'], 'L0_attn_Wqkv_w': _L0_attn_in['Wqkv_w'], 'L0_attn_Wqkv_b': _L0_attn_in['Wqkv_b'], 'L0_attn_out_w': _L0_attn_in['out_w'], 'L0_attn_out_b': _L0_attn_in['out_b'], 'L0_ffn_router_w': _L0_ffn_in['router_w'], 'L0_ffn_w_gate': _L0_ffn_in['w_gate'], 'L0_ffn_w_up': _L0_ffn_in['w_up'], 'L0_ffn_w_down': _L0_ffn_in['w_down'], 'L1_xattn_Wq': _L1_xattn_in['Wq'], 'L1_xattn_Wk': _L1_xattn_in['Wk'], 'L1_xattn_Wv': _L1_xattn_in['Wv'], 'L1_xattn_Wo': _L1_xattn_in['Wo'], 'L1_xattn_gq': _L1_xattn_in['gq'], 'L1_xattn_gk': _L1_xattn_in['gk'], 'L1_attn_wq_codes': _L1_attn_in['wq_codes'], 'L1_attn_wq_scales': _L1_attn_in['wq_scales'], 'L1_attn_bq': _L1_attn_in['bq'], 'L1_attn_wk_codes': _L1_attn_in['wk_codes'], 'L1_attn_wk_scales': _L1_attn_in['wk_scales'], 'L1_attn_bk': _L1_attn_in['bk'], 'L1_attn_wv_codes': _L1_attn_in['wv_codes'], 'L1_attn_wv_scales': _L1_attn_in['wv_scales'], 'L1_attn_bv': _L1_attn_in['bv'], 'L1_attn_wo_codes': _L1_attn_in['wo_codes'], 'L1_attn_wo_scales': _L1_attn_in['wo_scales'], 'L1_attn_bo': _L1_attn_in['bo'], 'L1_ffn_gate_w': _L1_ffn_in['gate_w'], 'L1_ffn_fc1_w': _L1_ffn_in['fc1_w'], 'L1_ffn_fc1_b': _L1_ffn_in['fc1_b'], 'L1_ffn_fc2_w': _L1_ffn_in['fc2_w'], 'L1_ffn_fc2_b': _L1_ffn_in['fc2_b'], 'L1_ffn_alpha': _L1_ffn_in['alpha']}

def reference(x, ctx_1024, mask_BxS2_bf1, L0_xattn_Wq, L0_xattn_Wk, L0_xattn_Wv, L0_xattn_Wo, L0_attn_Wqkv_w, L0_attn_Wqkv_b, L0_attn_out_w, L0_attn_out_b, L0_ffn_router_w, L0_ffn_w_gate, L0_ffn_w_up, L0_ffn_w_down, L1_xattn_Wq, L1_xattn_Wk, L1_xattn_Wv, L1_xattn_Wo, L1_xattn_gq, L1_xattn_gk, L1_attn_wq_codes, L1_attn_wq_scales, L1_attn_bq, L1_attn_wk_codes, L1_attn_wk_scales, L1_attn_bk, L1_attn_wv_codes, L1_attn_wv_scales, L1_attn_bv, L1_attn_wo_codes, L1_attn_wo_scales, L1_attn_bo, L1_ffn_gate_w, L1_ffn_fc1_w, L1_ffn_fc1_b, L1_ffn_fc2_w, L1_ffn_fc2_b, L1_ffn_alpha):
    import jax
    import jax.numpy as jnp

    def _L0_xattn_ref(text_hidden, vision_tokens, vision_mask, Wq, Wk, Wv, Wo):
        import jax, jax.numpy as jnp
        import numpy as np
        N_HEADS = 16
        N_KV_HEADS = 8
        HEAD_DIM = 128
        D_TEXT = 256
        D_VISION = 128
        GROUPS = N_HEADS // N_KV_HEADS
        B, T_text, _ = text_hidden.shape
        T_vis = vision_tokens.shape[1]
        scale = jnp.float32(np.sqrt(HEAD_DIM))
        q = (text_hidden @ Wq).reshape(B, T_text, N_HEADS, HEAD_DIM).transpose(0, 2, 1, 3)
        k = (vision_tokens @ Wk).reshape(B, T_vis, N_KV_HEADS, HEAD_DIM).transpose(0, 2, 1, 3)
        v = (vision_tokens @ Wv).reshape(B, T_vis, N_KV_HEADS, HEAD_DIM).transpose(0, 2, 1, 3)
        k = jnp.repeat(k, GROUPS, axis=1)
        v = jnp.repeat(v, GROUPS, axis=1)
        scores = jnp.einsum('bhtd,bhsd->bhts', q, k) / scale
        mask = vision_mask[:, None, None, :]
        scores = jnp.where(mask, scores, -jnp.inf)
        attn = jax.nn.softmax(scores, axis=-1)
        attn = jnp.nan_to_num(attn, nan=0.0)
        out = jnp.einsum('bhts,bhsd->bhtd', attn, v)
        out = out.transpose(0, 2, 1, 3).reshape(B, T_text, N_HEADS * HEAD_DIM)
        return out @ Wo

    def _L0_attn_ref(hidden_states, Wqkv_w, Wqkv_b, out_w, out_b):
        import jax, jax.numpy as jnp
        import numpy as np
        B, S, D, H = (2, 256, 256, 16)
        HD = D // H
        b, s, d = hidden_states.shape
        qkv = hidden_states @ Wqkv_w.T + Wqkv_b
        qkv = qkv.reshape(b, s, 3, H, HD)
        q, k, v = (qkv[:, :, 0], qkv[:, :, 1], qkv[:, :, 2])
        softmax_scale = 1.0 / np.float32(np.sqrt(HD))
        scores = jnp.einsum('bthd,bshd->bhts', q, k) * softmax_scale
        attn = jax.nn.softmax(scores, axis=-1)
        ctx = jnp.einsum('bhts,bshd->bthd', attn, v)
        ctx = ctx.reshape(b, s, d)
        return ctx @ out_w.T + out_b

    def _L0_ffn_ref(hidden_states, router_w, w_gate, w_up, w_down):
        import jax, jax.numpy as jnp
        import numpy as np
        B, S, H = (2, 128, 256)
        E, K, F = (64, 8, 96)
        CAP = 64
        b, s, h = hidden_states.shape
        T = b * s
        xf = hidden_states.reshape(T, h)
        logits = xf @ router_w.T
        scores = jax.nn.softmax(logits.astype(jnp.float32), axis=-1)
        topk_w, topk_idx = jax.lax.top_k(scores, K)
        topk_w = topk_w / (topk_w.sum(axis=-1, keepdims=True) + 1e-20)
        slot_expert = topk_idx.reshape(-1)
        slot_token = jnp.repeat(jnp.arange(T), K)
        onehot = jax.nn.one_hot(slot_expert, E, dtype=jnp.int32)
        pos = (jnp.cumsum(onehot, axis=0) * onehot).sum(-1) - 1
        valid = pos < CAP
        dest = jnp.where(valid, slot_expert * CAP + pos, E * CAP)
        buf = jnp.zeros((E * CAP + 1, h), xf.dtype).at[dest].set(xf[slot_token])
        xb = buf[:E * CAP].reshape(E, CAP, h)
        gate = jnp.einsum('ech,ehf->ecf', xb, w_gate)
        up = jnp.einsum('ech,ehf->ecf', xb, w_up)
        hmid = jax.nn.silu(gate) * up
        yb = jnp.einsum('ecf,efh->ech', hmid, w_down).reshape(E * CAP, h)
        yb = jnp.concatenate([yb, jnp.zeros((1, h), yb.dtype)], axis=0)
        slot_out = yb[dest] * topk_w.reshape(-1)[:, None].astype(yb.dtype)
        out = jnp.zeros((T, h), yb.dtype).at[slot_token].add(slot_out)
        return out.reshape(b, s, h)

    def _L1_xattn_ref(hidden_states, encoder_hidden_states, Wq, Wk, Wv, Wo, gq, gk):
        import jax, jax.numpy as jnp
        import numpy as np
        EPS = 1e-05

        def rmsnorm(x, g, eps=EPS):
            var = jnp.mean(jnp.square(x), axis=-1, keepdims=True)
            return x * jax.lax.rsqrt(var + eps) * g
        B, Sq, _ = hidden_states.shape
        Skv = encoder_hidden_states.shape[1]
        D = gq.shape[0]
        H = Wq.shape[1] // D
        scale = 1.0 / np.sqrt(D)
        q = (hidden_states @ Wq).reshape(B, Sq, H, D)
        k = (encoder_hidden_states @ Wk).reshape(B, Skv, H, D)
        v = (encoder_hidden_states @ Wv).reshape(B, Skv, H, D)
        q = rmsnorm(q, gq)
        k = rmsnorm(k, gk)
        scores = jnp.einsum('bqhd,bkhd->bhqk', q, k) * scale
        attn = jax.nn.softmax(scores, axis=-1)
        out = jnp.einsum('bhqk,bkhd->bqhd', attn, v)
        out = out.reshape(B, Sq, H * D)
        return out @ Wo

    def _L1_attn_ref(x, wq_codes, wq_scales, bq, wk_codes, wk_scales, bk, wv_codes, wv_scales, bv, wo_codes, wo_scales, bo):
        import jax, jax.numpy as jnp
        import numpy as np
        BLOCK = 32
        NUM_HEADS = 16
        HEAD_DIM = 128
        FP4_GRID = jnp.array([0.0, 0.5, 1.0, 1.5, 2.0, 3.0, 4.0, 6.0], dtype=jnp.float32)

        def quantize_to_mxfp4(w, block_size=BLOCK):
            D, F = w.shape
            blocks = w.reshape(D // block_size, block_size, F)
            amax = jnp.max(jnp.abs(blocks), axis=1)
            e = jnp.floor(jnp.log2(jnp.maximum(amax, 1e-12) / 6.0))
            scale = jnp.exp2(e)
            v = blocks / scale[:, None, :]
            idx = jnp.argmin(jnp.abs(jnp.abs(v)[..., None] - FP4_GRID), axis=-1)
            codes = jnp.sign(v) * FP4_GRID[idx]
            return (codes.reshape(D, F).astype(jnp.float32), scale.astype(jnp.float32))

        def _mxfp4_matmul(x, codes, scales, block_size=BLOCK):
            w = codes * jnp.repeat(scales, block_size, axis=0)
            return x @ w
        B, S, D = x.shape
        q = _mxfp4_matmul(x, wq_codes, wq_scales) + bq
        k = _mxfp4_matmul(x, wk_codes, wk_scales) + bk
        v = _mxfp4_matmul(x, wv_codes, wv_scales) + bv
        q = q.reshape(B, S, NUM_HEADS, HEAD_DIM)
        k = k.reshape(B, S, NUM_HEADS, HEAD_DIM)
        v = v.reshape(B, S, NUM_HEADS, HEAD_DIM)
        scores = jnp.einsum('bqhd,bkhd->bhqk', q, k) / jnp.sqrt(jnp.float32(HEAD_DIM))
        attn = jax.nn.softmax(scores, axis=-1)
        out = jnp.einsum('bhqk,bkhd->bqhd', attn, v).reshape(B, S, NUM_HEADS * HEAD_DIM)
        return _mxfp4_matmul(out, wo_codes, wo_scales) + bo

    def _L1_ffn_ref(hidden_states, gate_w, fc1_w, fc1_b, fc2_w, fc2_b, alpha):
        import jax, jax.numpy as jnp
        import numpy as np
        NUM_EXPERTS = 8
        HIDDEN = 256
        INTER = 256
        TOP_K = 2
        B, S, H = hidden_states.shape
        x = hidden_states.reshape(-1, H)
        probs = jax.nn.softmax(x @ gate_w, axis=-1)
        gate_score, gate_idx = jax.lax.top_k(probs, TOP_K)
        gate_score = gate_score / jnp.sum(gate_score, axis=-1, keepdims=True)
        onehot = jax.nn.one_hot(gate_idx, NUM_EXPERTS, dtype=x.dtype)
        combine = jnp.einsum('tk,tke->te', gate_score, onehot) * alpha[None, :]
        h = jnp.einsum('th,ehi->eti', x, fc1_w) + fc1_b[:, None, :]
        h = jax.nn.gelu(h, approximate=False)
        y = jnp.einsum('eti,eih->eth', h, fc2_w) + fc2_b[:, None, :]
        out = jnp.einsum('eth,te->th', y, combine)
        return out.reshape(B, S, H)
    x = x + _L0_xattn_ref(_layernorm(x, axis=-1), ctx_1024, mask_BxS2_bf1, L0_xattn_Wq, L0_xattn_Wk, L0_xattn_Wv, L0_xattn_Wo)
    x = x + _L0_attn_ref(_layernorm(x, axis=-1), L0_attn_Wqkv_w, L0_attn_Wqkv_b, L0_attn_out_w, L0_attn_out_b)
    x = x + _L0_ffn_ref(_layernorm(x, axis=-1), L0_ffn_router_w, L0_ffn_w_gate, L0_ffn_w_up, L0_ffn_w_down)
    x = x + _L1_xattn_ref(_layernorm(x, axis=-1), ctx_1024, L1_xattn_Wq, L1_xattn_Wk, L1_xattn_Wv, L1_xattn_Wo, L1_xattn_gq, L1_xattn_gk)
    x = x + _L1_attn_ref(_layernorm(x, axis=-1), L1_attn_wq_codes, L1_attn_wq_scales, L1_attn_bq, L1_attn_wk_codes, L1_attn_wk_scales, L1_attn_bk, L1_attn_wv_codes, L1_attn_wv_scales, L1_attn_bv, L1_attn_wo_codes, L1_attn_wo_scales, L1_attn_bo)
    x = x + _L1_ffn_ref(_layernorm(x, axis=-1), L1_ffn_gate_w, L1_ffn_fc1_w, L1_ffn_fc1_b, L1_ffn_fc2_w, L1_ffn_fc2_b, L1_ffn_alpha)
    return x

_drawn_inputs = setup_inputs


def setup_inputs(seed=0):
    import zlib

    import numpy as np

    out = dict(_drawn_inputs(seed))
    spreads = {'L1_xattn_gq': (1.0, 0.2),
     'L1_xattn_gk': (1.0, 0.2),
     'L1_attn_bq': (0.0, 0.602),
     'L1_attn_bk': (0.0, 0.8),
     'L1_attn_bv': (0.0, 0.1),
     'L1_attn_bo': (0.0, 0.1),
     'L1_ffn_fc1_b': (0.0, 0.743),
     'L1_ffn_fc2_b': (0.0, 0.1)}
    factors = {'L0_xattn_Wq': 6.276, 'L0_xattn_Wk': 7.875, 'L0_attn_Wqkv_b': 3.755}
    for name, (base, spread) in spreads.items():
        noise = np.random.default_rng([zlib.crc32(name.encode()), seed]).standard_normal(out[name].shape)
        drawn = base * np.exp(spread * noise) if base else spread * noise
        out[name] = jnp.asarray(drawn.astype(out[name].dtype))
    for name, factor in factors.items():
        out[name] = (out[name] * factor).astype(out[name].dtype)
    return out
```

```python
from contextlib import ExitStack

import concourse.bass as bass
from concourse import mybir

ALU = mybir.AluOpType
ACT = mybir.ActivationFunctionType
F32 = mybir.dt.float32
U32 = mybir.dt.uint32
AX_X = mybir.AxisListType.X

P = 128
B, T, D = 64, 32, 256
S2, DC = 257, 128
H, HD = 16, 128
KVH = 8
AH, AD = 16, 16
E0, K0, F0, CAP = 64, 8, 96, 64
FP4_ROWS = 32
E1, F1 = 8, 256
NC = D // P
NT = B * T // P
BT = P // T
KEYS = B * S2
LN_EPS = 1e-5
SCALE = float(HD) ** -0.5
SLOTS = E0 * CAP
FOLDED = NC * P + D
RK_AHEAD = 512
RK_COPIES = 4
NOWHERE = 2 * SLOTS


class Chain:

    def __init__(self, eng, sem, base=0, passed=None):
        self.eng, self.sem, self.base, self.passed, self.n = eng, sem, base, passed, 0

    def __call__(self, ins, alone=False):
        self.n += 1
        ins.then_inc(self.sem, 1)
        self.eng.wait_ge(self.sem, self.base + self.n)
        if alone:
            apart(self.eng, self.passed)


def apart(eng, passed):
    eng.sem_inc(passed, 1)


class Scope:

    def __init__(self, nc, ctx, name):
        self.nc, self.ctx, self.name, self.sems = nc, ctx, name, []

    def sb(self, name, shape, dt=F32):
        return self.ctx.enter_context(self.nc.sbuf_tensor(f"{self.name}_{name}", shape, dt))

    def ps(self, name, shape=(P, 512), dt=F32):
        return self.ctx.enter_context(self.nc.psum_tensor(f"{self.name}_{name}_ps", list(shape), dt))

    def sem(self, name):
        handle = self.ctx.enter_context(self.nc.semaphore(f"{self.name}_{name}"))
        self.sems.append(handle)
        return handle

    def pool_dma_sem(self, name):
        return self.nc.alloc_semaphore(name=f"{self.name}_{name}")

    def block(self):
        with self.nc.Block() as block:
            @block.sync
            def _(sp):
                for handle in self.sems:
                    sp.sem_clear(handle)
        return self.ctx.enter_context(self.nc.Block())


def load_inputs(nc, I, x_sb, ident):
    with ExitStack() as ctx:
        sc = Scope(nc, ctx, "in")
        x_loaded, padded, zeroed, made = sc.sem("x_loaded"), sc.sem("padded"), sc.sem("zeroed"), sc.sem("made")
        block = sc.block()

        @block.sync
        def _(sp):
            sp.dma_start(x_sb[:, 0:NT, :], I["x"].rearrange("(n b) t d -> (b t) n d", b=BT)).then_inc(x_loaded, 16)
            sp.wait_ge(x_loaded, 16)

        @block.vector
        def _(dve):
            dve.memset(x_sb[:, NT:, :], 0.0).then_inc(padded, 1)
            dve.wait_ge(padded, 1)

        @block.gpsimd
        def _(pool):
            pool.memset(ident[:, :], 0.0).then_inc(zeroed, 1)
            pool.wait_ge(zeroed, 1)
            pool.affine_select(out=ident[:, :], in_=ident[:, :], compare_op=ALU.not_equal, fill=1.0, base=0,
                               pattern=[[-1, P]], channel_multiplier=1).then_inc(made, 1)


def fold_weights(nc, I, ident, folded, folded_dram):
    with ExitStack() as ctx:
        sc = Scope(nc, ctx, "fold")
        UNITS, SLOT = KVH, 2
        wq = [sc.sb(f"wq{l}", [P, SLOT, NC, 2 * HD]) for l in range(2)]
        wk = [sc.sb(f"wk{l}", [P, SLOT, (l + 1) * HD]) for l in range(2)]
        wv = [sc.sb(f"wv{l}", [P, SLOT, (l + 1) * HD]) for l in range(2)]
        wo = [sc.sb(f"wo{l}", [P, SLOT, 2, D]) for l in range(2)]
        wT = sc.sb("wT", [P, 2, 4 * P])
        stage = sc.sb("stage", [P, 2, FOLDED])
        gains = sc.sb("gains", [P, 2])
        gain = sc.sb("gain", [P, 1])
        turned_ps = [sc.ps(f"turned{n}") for n in range(2)]
        prod_ps = [sc.ps(f"prod{n}") for n in range(2)]
        loaded = [sc.sem(f"loaded{p}") for p in range(SLOT)]
        gains_loaded, gain_ready = sc.sem("gains_loaded"), sc.sem("gain_ready")
        passed, stored = sc.sem("passed"), [sc.pool_dma_sem(f"stored{j}") for j in range(2)]
        turned, wT_ready, multiplied, kept = sc.sem("turned"), sc.sem("wT_ready"), sc.sem("multiplied"), sc.sem("kept")
        block = sc.block()
        DMAS = 8
        ITERS = UNITS // SLOT
        STEPS = 4 * SLOT

        def step(k):
            return k // 4, (k % 4) // 2, k % 2

        names = ["L0_xattn_", "L1_xattn_"]

        @block.sync
        def _(sp):
            sp.dma_start(gains[:, 0:1], I["L1_xattn_gq"].rearrange("(d a) -> d a", a=1)).then_inc(gains_loaded, 16)
            sp.dma_start(gains[:, 1:2], I["L1_xattn_gk"].rearrange("(d a) -> d a", a=1)).then_inc(gains_loaded, 16)
            with sp.Fori(0, ITERS) as i:
                for p in range(SLOT):
                    u = i * SLOT + p
                    sp.wait_ge(multiplied, i * STEPS)
                    for l in range(2):
                        n, w = names[l], (l + 1) * HD
                        sp.dma_start(wq[l][:, p], I[n + "Wq"].rearrange("(c p) n -> p c n", p=P)[
                            :, :, bass.ds(u * (2 * HD), 2 * HD)]).then_inc(loaded[p], 16)
                        sp.dma_start(wk[l][:, p], I[n + "Wk"][:, bass.ds(u * w, w)]).then_inc(loaded[p], 16)
                        sp.dma_start(wv[l][:, p], I[n + "Wv"][:, bass.ds(u * w, w)]).then_inc(loaded[p], 16)
                        sp.dma_start(wo[l][:, p], I[n + "Wo"].rearrange("(h d) n -> d h n", d=HD)[
                            :, bass.ds(u * 2, 2), :]).then_inc(loaded[p], 16)

        @block.tensor
        def _(pe):
            def turn(i, k):
                p, l, j = step(k)
                kv = j * HD if l else 0
                if k % 4 == 0:
                    pe.wait_ge(loaded[p], i * (16 * DMAS) + 16 * DMAS)
                pe.wait_ge(wT_ready, i * STEPS + max(k - 1, 0))
                ps = turned_ps[k % 2]
                for c in range(NC):
                    pe.transpose(ps[:, c * P:(c + 1) * P], wq[l][:, p, c, j * HD:(j + 1) * HD], ident[:, :])
                pe.transpose(ps[:, 2 * P:3 * P], wk[l][:, p, kv:kv + HD], ident[:, :])
                pe.transpose(ps[:, 3 * P:4 * P], wv[l][:, p, kv:kv + HD], ident[:, :]).then_inc(turned, 1)

            def product(i, k):
                p, l, j = step(k)
                pe.wait_ge(wT_ready, i * STEPS + k + 1)
                pe.wait_ge(kept, i * STEPS + max(k - 1, 0))
                w, ps = wT[:, k % 2], prod_ps[k % 2]
                for c in range(NC):
                    pe.matmul(ps[:, c * P:(c + 1) * P], w[:, c * P:(c + 1) * P], w[:, 2 * P:3 * P], start=True, stop=True)
                pe.matmul(ps[:, 2 * P:2 * P + D], w[:, 3 * P:4 * P], wo[l][:, p, j, :],
                          start=True, stop=True).then_inc(multiplied, 1)

            with pe.Fori(0, ITERS) as i:
                turn(i, 0)
                for k in range(STEPS):
                    if k + 1 < STEPS:
                        turn(i, k + 1)
                    product(i, k)

        @block.vector
        def _(dve):
            dve.wait_ge(gains_loaded, 32)
            dve.tensor_tensor(gain[:, :], gains[:, 0:1], gains[:, 1:2], ALU.mult).then_inc(gain_ready, 1)
            dve.wait_ge(gain_ready, 1)
            with dve.Fori(0, ITERS) as i:
                for k in range(STEPS):
                    _, l, _ = step(k)
                    dve.wait_ge(multiplied, i * STEPS + max(k - 1, 0))
                    dve.wait_ge(turned, i * STEPS + k + 1)
                    w, ps = wT[:, k % 2], turned_ps[k % 2]
                    dve.tensor_scalar(w[:, 0:2 * P], ps[:, 0:2 * P], gain[:, 0:1] if l else SCALE,
                                      None, ALU.mult)
                    dve.tensor_copy(w[:, 2 * P:4 * P], ps[:, 2 * P:4 * P]).then_inc(wT_ready, 1)

        @block.scalar
        def _(act):
            with act.Fori(0, ITERS) as i:
                for k in range(STEPS):
                    p, l, j = step(k)
                    h = i * (2 * SLOT) + (2 * p + j)
                    act.wait_ge(multiplied, i * STEPS + k + 1)
                    if l:
                        act.wait_ge(stored[j], i * (16 * SLOT) + 16 * p)
                        to = stage[:, j, :]
                    else:
                        to = folded[:, bass.ds(h, 1), :].rearrange("p a n -> p (a n)")
                    act.activation(to, prod_ps[k % 2][:, 0:FOLDED], ACT.Copy).then_inc(kept, 1)

        @block.gpsimd
        def _(pool):
            with pool.Fori(0, ITERS) as i:
                for k in range(STEPS):
                    p, l, j = step(k)
                    if l:
                        pool.wait_ge(kept, i * STEPS + k + 1)
                        apart(pool, passed)
                        pool.dma_start(folded_dram[:, bass.ds(i * (2 * SLOT) + (2 * p + j), 1), :],
                                       stage[:, j, :]).then_inc(stored[j], 16)
            for j in range(2):
                pool.wait_ge(stored[j], 16 * UNITS)


def context_pass(nc, I, ident, ctxT, rk_dram):
    with ExitStack() as ctx:
        sc = Scope(nc, ctx, "ctx")
        U = 4
        FULL = KEYS // P
        ITERS = FULL // U
        REST = KEYS - FULL * P
        assert FULL % U == 0 and 0 < REST < P and U * P == RK_AHEAD
        NQ = H * HD // 512
        HQ = H // NQ
        wk = sc.sb("wk", [P, H * HD])
        rows = sc.sb("rows", [P, U, DC])
        stage = sc.sb("stage", [P, 2, P])
        squares = sc.sb("squares", [P, 2, 512])
        sums = sc.sb("sums", [P, U, H])
        root = sc.sb("root", [P, U, H])
        rk = sc.sb("rk", [P, U, H])
        rkT = sc.sb("rkT", [H, 1, U * P])
        eps = sc.sb("eps", [P, 1])
        turned_ps = [sc.ps(f"turned{n}") for n in range(2)]
        key_ps = [sc.ps(f"key{n}") for n in range(NQ)]
        rk_ps = sc.ps("rk")
        wk_loaded, eps_set, rk_zeroed = sc.sem("wk_loaded"), sc.sem("eps_set"), sc.sem("rk_zeroed")
        loaded = [sc.sem(f"loaded{u}") for u in range(U)]
        turned, staged, moved = sc.sem("turned"), sc.sem("staged"), sc.sem("moved")
        keyed, squared, summed = sc.sem("keyed"), sc.sem("squared"), sc.sem("summed")
        rooted, rk_ready = sc.sem("rooted"), sc.sem("rk_ready")
        passed = sc.sem("passed")
        rk_turned, rk_kept, rk_stored = sc.sem("rk_turned"), sc.sem("rk_kept"), sc.sem("rk_stored")
        block = sc.block()
        flat = I["ctx_1024"].rearrange("b s d -> (b s) d")

        @block.sync
        def _(sp):
            sp.dma_start(wk[:, :], I["L1_xattn_Wk"]).then_inc(wk_loaded, 16)
            with sp.Fori(0, ITERS) as i:
                for u in range(U):
                    sp.wait_ge(turned, i * U)
                    sp.dma_start(rows[:, u, :], flat[bass.ds((i * U + u) * P, P), :]).then_inc(loaded[u], 16)
            sp.wait_ge(turned, FULL)
            sp.dma_start(rows[0:REST, 0, :], flat[FULL * P:KEYS, :]).then_inc(loaded[0], 16)

        @block.tensor
        def _(pe):
            def turn(i, u, n):
                k = i * U + u
                if isinstance(k, int):
                    pe.wait_ge(loaded[u], 16 * (i + 1))
                else:
                    pe.wait_ge(loaded[u], i * 16 + 16)
                pe.wait_ge(staged, i * U + max(u - 1, 0))
                pe.transpose(turned_ps[u % 2][:, 0:n], rows[0:n, u, :], ident[0:n, 0:n]).then_inc(turned, 1)

            def keys(i, u, n):
                pe.wait_ge(staged, i * U + u + 1)
                for q in range(NQ):
                    pe.wait_ge(squared, i * (U * NQ) + ((u - 1) * NQ + q + 1 if u else 0))
                    pe.matmul(key_ps[q][0:n, :], stage[:, u % 2, 0:n], wk[:, q * 512:(q + 1) * 512],
                              start=True, stop=True).then_inc(keyed, 1)

            def turn_rk(i):
                pe.wait_ge(rk_ready, i * U)
                pe.wait_ge(rk_kept, i)
                for u in range(U):
                    ins = pe.transpose(rk_ps[0:H, u * P:(u + 1) * P], rk[:, u, :], ident[:, :])
                ins.then_inc(rk_turned, 1)

            pe.wait_ge(wk_loaded, 16)
            pe.wait_ge(rk_zeroed, 1)
            with pe.Fori(0, ITERS) as i:
                turn(i, 0, P)
                for u in range(U):
                    if u + 1 < U:
                        turn(i, u + 1, P)
                    keys(i, u, P)
                    if u == 0:
                        turn_rk(i)
            turn(ITERS, 0, REST)
            keys(ITERS, 0, REST)
            turn_rk(ITERS)
            pe.wait_ge(rk_ready, FULL + 1)
            pe.wait_ge(rk_kept, ITERS + 1)
            pe.transpose(rk_ps[0:H, 0:REST], rk[0:REST, 0, :], ident[0:REST, 0:REST]).then_inc(rk_turned, 1)

        @block.scalar
        def _(act):
            def square(i, u, n):
                for q in range(NQ):
                    act.wait_ge(summed, i * (U * NQ) + max(u * NQ + q - 1, 0))
                    act.wait_ge(keyed, i * (U * NQ) + (u * NQ + q + 1))
                    act.activation(squares[0:n, q % 2, :], key_ps[q][0:n, :], ACT.Square).then_inc(squared, 1)

            def take_root(i, u, n):
                act.wait_ge(rk_ready, i * U)
                act.wait_ge(summed, i * (U * NQ) + (u + 1) * NQ)
                act.activation(root[0:n, u, :], sums[0:n, u, :], ACT.Sqrt, bias=eps[0:n, 0:1],
                               scale=1.0 / HD).then_inc(rooted, 1)

            act.wait_ge(eps_set, 1)
            def store_rk(i, n):
                act.wait_ge(rk_kept, i + 1)
                to = rk_dram.rearrange("(h c) n -> h c n", c=RK_COPIES)
                act.dma_start(to[:, :, bass.ds(i * (U * P), n)],
                              rkT[:, :, 0:n].broadcast_to([H, RK_COPIES, n])).then_inc(rk_stored, 16)

            with act.Fori(0, ITERS) as i:
                for u in range(U):
                    square(i, u, P)
                    take_root(i, u, P)
                    if u == 2:
                        store_rk(i, U * P)
            square(ITERS, 0, REST)
            take_root(ITERS, 0, REST)
            store_rk(ITERS, U * P)
            store_rk(ITERS + 1, REST)
            act.wait_ge(rk_stored, 16 * (ITERS + 2))

        @block.vector
        def _(dve):
            dve.memset(eps[:, :], LN_EPS).then_inc(eps_set, 1)
            dve.memset(rk[:, :, :], 0.0).then_inc(rk_zeroed, 1)
            dve.wait_ge(rk_zeroed, 1)

            def put_stage(i, u, n):
                dve.wait_ge(moved, i * U + max(u - 1, 0))
                dve.wait_ge(keyed, i * (U * NQ) + max(u - 1, 0) * NQ)
                dve.wait_ge(turned, i * U + u + 1)
                dve.tensor_copy(stage[:, u % 2, 0:n], turned_ps[u % 2][:, 0:n]).then_inc(staged, 1)

            def sum_squares(i, u, n):
                for q in range(NQ):
                    dve.wait_ge(rooted, i * U)
                    dve.wait_ge(squared, i * (U * NQ) + (u * NQ + q + 1))
                    dve.tensor_reduce(sums[0:n, u, q * HQ:(q + 1) * HQ],
                                      squares[0:n, q % 2, :].rearrange("p (h d) -> p h d", h=HQ), AX_X, ALU.add
                                      ).then_inc(summed, 1)

            def invert(i, u, n):
                dve.wait_ge(rk_turned, i + 1)
                dve.wait_ge(rooted, i * U + u + 1)
                dve.reciprocal(rk[0:n, u, :], root[0:n, u, :]).then_inc(rk_ready, 1)

            def keep_rk(i):
                dve.wait_ge(rk_stored, i * 16)
                dve.wait_ge(rk_turned, i + 1)
                dve.tensor_copy(rkT[:, 0, :], rk_ps[0:H, :]).then_inc(rk_kept, 1)

            with dve.Fori(0, ITERS) as i:
                put_stage(i, 0, P)
                for u in range(U):
                    if u + 1 < U:
                        put_stage(i, u + 1, P)
                    sum_squares(i, u, P)
                    if u == 0:
                        keep_rk(i)
                    invert(i, u, P)
            put_stage(ITERS, 0, REST)
            sum_squares(ITERS, 0, REST)
            keep_rk(ITERS)
            invert(ITERS, 0, REST)
            dve.wait_ge(rk_stored, (ITERS + 1) * 16)
            dve.wait_ge(rk_turned, ITERS + 2)
            dve.tensor_copy(rkT[:, 0, 0:REST], rk_ps[0:H, 0:REST]).then_inc(rk_kept, 1)

        @block.gpsimd
        def _(pool):
            with pool.Fori(0, ITERS) as i:
                for u in range(U):
                    pool.wait_ge(staged, i * U + u + 1)
                    apart(pool, passed)
                    pool.tensor_copy(ctxT[:, bass.ds((i * U + u) * P, P)], stage[:, u % 2, :]).then_inc(moved, 1)
            pool.wait_ge(staged, FULL + 1)
            pool.tensor_copy(ctxT[:, FULL * P:KEYS], stage[:, 0, 0:REST]).then_inc(moved, 1)


def cross_attention(nc, I, layer, x_sb, ident, ctxT, folded, folded_dram, rk_dram):
    with ExitStack() as ctx:
        sc = Scope(nc, ctx, f"xa{layer}")
        G = 2
        NB = G * BT
        R = H * T // P
        HR = H // R
        ST = NB * R
        ITERS = NT // G
        N = G * P
        HP = H // 2
        RING = 4
        SR = 6
        EARLY = 2
        AHEAD = 4
        KB = S2 // P
        assert S2 == KB * P + 1
        NQ = H * HD // 512

        stats, mv = sc.sb("stats", [P, G, 6]), sc.sb("mv", [P, G, 2])
        rstd, minus_half = sc.sb("rstd", [P, G]), sc.sb("minus_half", [P, G * H])
        xn, xnT = sc.sb("xn", [P, G, D]), sc.sb("xnT", [P, NC, N])
        qT = sc.sb("qT", [P, NB, H, T])
        keys = sc.sb("keys", [P, RING, KB, DC])
        last_key = sc.sb("last_key", [1, RING, DC])
        probs = sc.sb("probs", [P, SR, S2])
        top, shift = sc.sb("top", [P, 8]), sc.sb("shift", [P, 8])
        total, share = sc.sb("total", [P, 8]), sc.sb("share", [P, 8])
        probsT, last_probsT = sc.sb("probsT", [P, 2, KB, H * T]), sc.sb("last_probsT", [1, 2, H * T])
        mixT = sc.sb("mixT", [P, H, N])
        if layer == 0:
            mask = sc.sb("mask", [P, B, S2], mybir.dt.uint8)
            any_key = sc.sb("any_key", [P, B])
            valid, bias = sc.sb("valid", [P, S2]), sc.sb("bias", [P, 2, S2])
        else:
            wq = sc.sb("wq", [P, NC, H * HD])
            squares = sc.sb("squares", [P, 2, 512])
            q_sum, q_rms = sc.sb("q_sum", [P, G, H]), sc.sb("q_rms", [P, G, H])
            row_scale = sc.sb("row_scale", [P, G, BT, R])
            key_scale = sc.sb("key_scale", [P, 2, R, S2])
        misc_ps = [sc.ps(f"misc{n}") for n in range(2)]
        score_ps = [sc.ps(f"score{n}") for n in range(2)]
        probsT_ps = [sc.ps(f"probsT{n}") for n in range(2)]
        last_ps, mix_ps = sc.ps("last"), sc.ps("mix")

        begun, passed, pre_loaded, any_ready = sc.sem("begun"), sc.sem("passed"), sc.sem("pre_loaded"), sc.sem("any_ready")
        keys_loaded = [sc.sem(f"keys_loaded{n}") for n in range(RING)]
        kscale_loaded = [sc.sem(f"kscale_loaded{n}") for n in range(2)]
        dve_chain, pool_chain = sc.sem("dve_chain"), sc.sem("pool_chain")
        var_ready, rstd_ready, normed = sc.sem("var_ready"), sc.sem("rstd_ready"), sc.sem("normed")
        x_turned, xnT_ready = sc.sem("x_turned"), sc.sem("xnT_ready")
        q_made, q_kept_act, q_kept_dve = sc.sem("q_made"), sc.sem("q_kept_act"), sc.sem("q_kept_dve")
        n_made, n_squared, n_summed, rows_ready = sc.sem("n_made"), sc.sem("n_squared"), sc.sem("n_summed"), sc.sem("rows_ready")
        bias_ready = sc.sem("bias_ready")
        scored, shifted, exped = sc.sem("scored"), sc.sem("shifted"), sc.sem("exped")
        probs_ready, turned, turned_kept = sc.sem("probs_ready"), sc.sem("turned"), sc.sem("turned_kept")
        last_kept, mixed, mix_kept = sc.sem("last_kept"), sc.sem("mixed"), sc.sem("mix_kept")
        projected, added = sc.sem("projected"), sc.sem("added")
        block = sc.block()
        ctx_in = I["ctx_1024"]

        @block.sync
        def _(sp):
            if layer == 0:
                sp.dma_start(mask[:, :, :], I["mask_BxS2_bf1"].partition_broadcast(P)).then_inc(pre_loaded, 16)
            else:
                sp.dma_start(wq[:, :, :], I["L1_xattn_Wq"].rearrange("(c p) n -> p c n", p=P)).then_inc(pre_loaded, 16)
                sp.dma_start(folded[:, :, :], folded_dram).then_inc(pre_loaded, 16)
            with sp.Fori(0, ITERS) as i:
                for b in range(NB):
                    item = i * NB + b
                    sp.wait_ge(mixed, i * NB + max(b - RING + 1, 0))
                    sp.dma_start(keys[:, b % RING], ctx_in[bass.ds(item, 1), 0:KB * P, :].rearrange(
                        "a (k p) d -> p (a k) d", p=P)).then_inc(keys_loaded[b % RING], 16)
                    sp.dma_start(last_key[:, b % RING, :], ctx_in[bass.ds(item, 1), KB * P, :]
                                 ).then_inc(keys_loaded[b % RING], 16)
                    if layer == 1:
                        sp.wait_ge(shifted, i * ST + max(b - 1, 0) * R)
                        for r in range(R):
                            src = rk_dram[r * HR * RK_COPIES:(r + 1) * HR * RK_COPIES,
                                          bass.ds(item * S2 + RK_AHEAD, S2)]
                            sp.dma_start(key_scale[:, b % 2, r, :], src.unsqueeze(1).broadcast_to(
                                [HR * RK_COPIES, T // RK_COPIES, S2])).then_inc(kscale_loaded[b % 2], 16)

        @block.tensor
        def _(pe):
            def score(i, s):
                b, r = s // R, s % R
                pe.wait_ge(shifted, i * ST + max(s - 1, 0))
                pe.matmul(score_ps[s % 2][:, 0:S2], qT[:, b, r * HR:(r + 1) * HR, :].rearrange("p h t -> p (h t)"),
                          ctxT[:, bass.ds((i * NB + b) * S2, S2)], start=True, stop=True).then_inc(scored, 1)

            def turn(i, s):
                b, r = s // R, s % R
                pe.wait_ge(probs_ready, i * ST + s + 1)
                pe.wait_ge(turned_kept, i * ST + max(s - 1, 0))
                if r == 0:
                    pe.wait_ge(last_kept, i * NB + b)
                for k in range(KB):
                    pe.transpose(probsT_ps[s % 2][:, k * P:(k + 1) * P], probs[:, s % SR, k * P:(k + 1) * P], ident[:, :])
                pe.transpose(last_ps[0:1, r * P:(r + 1) * P], probs[:, s % SR, KB * P:S2], ident[:, :]).then_inc(turned, 1)

            def mix(i, b, k):
                if k == 0:
                    pe.wait_ge(turned_kept, i * ST + (b + 1) * R)
                    pe.wait_ge(mix_kept, i * NB + b)
                    pe.wait_ge(keys_loaded[b % RING], i * (32 * NB // RING) + 32 * (b // RING + 1))
                if k < KB:
                    pe.matmul(mix_ps[:, :], keys[:, b % RING, k, :], probsT[:, b % 2, k, :], start=(k == 0), stop=False)
                else:
                    pe.wait_ge(last_kept, i * NB + b + 1)
                    pe.matmul(mix_ps[:, :], last_key[0:1, b % RING, :], last_probsT[0:1, b % 2, :],
                              start=False, stop=True).then_inc(mixed, 1)

            pe.wait_ge(pre_loaded, 32 if layer else 16)
            with pe.Fori(0, ITERS) as i:
                pe.wait_ge(added, i * G)
                pe.wait_ge(normed, i * G + G)
                for t in range(G):
                    for c in range(NC):
                        ins = pe.transpose(misc_ps[0][:, c * N + t * P:c * N + (t + 1) * P],
                                           xn[:, t, c * P:(c + 1) * P], ident[:, :])
                ins.then_inc(x_turned, 1)
                pe.wait_ge(xnT_ready, i + 1)
                if layer == 1:
                    for m in range(G * NQ):
                        pe.wait_ge(n_squared, i * (G * NQ) + max(m - 1, 0))
                        for c in range(NC):
                            ins = pe.matmul(misc_ps[m % 2][:, :], xnT[:, c, (m // NQ) * P:(m // NQ + 1) * P],
                                            wq[:, c, (m % NQ) * 512:(m % NQ + 1) * 512], start=(c == 0), stop=(c == NC - 1))
                        ins.then_inc(n_made, 1)
                    pe.wait_ge(n_squared, i * (G * NQ) + G * NQ)
                for hp in range(HP):
                    if hp >= 2:
                        pe.wait_ge(q_kept_dve if hp % 2 else q_kept_act, i * (HP // 2) + hp // 2)
                    for j in range(2):
                        for c in range(NC):
                            ins = pe.matmul(misc_ps[hp % 2][:, j * N:(j + 1) * N], folded[:, 2 * hp + j, c * P:(c + 1) * P], xnT[:, c, :],
                                            start=(c == 0), stop=(c == NC - 1))
                    ins.then_inc(q_made, 1)
                pe.wait_ge(q_kept_act, i * (HP // 2) + HP // 2)
                pe.wait_ge(q_kept_dve, i * (HP // 2) + HP // 2)
                for s in range(AHEAD):
                    score(i, s)
                for s in range(ST):
                    turn(i, s)
                    if s + AHEAD < ST:
                        score(i, s + AHEAD)
                    if s >= R and s % R:
                        mix(i, s // R - 1, s % R - 1)
                for k in range(KB + 1):
                    mix(i, NB - 1, k)
                for t in range(G):
                    pe.wait_ge(mix_kept, i * NB + (t + 1) * BT)
                    for h in range(H):
                        ins = pe.matmul(misc_ps[t][:, 0:D], mixT[:, h, t * P:(t + 1) * P], folded[:, h, NC * P:FOLDED],
                                        start=(h == 0), stop=(h == H - 1))
                    ins.then_inc(projected, 1)

        @block.scalar
        def _(act):
            def exp(i, s):
                act.wait_ge(shifted, i * ST + s + 1)
                b = s // R
                scale = 1.0 if layer == 0 else row_scale[:, b // BT, b % BT, s % R:s % R + 1]
                act.activation(probs[:, s % SR, :], probs[:, s % SR, :], ACT.Exp, bias=shift[:, s % 8:s % 8 + 1],
                               scale=scale, accum_out=total[:, s % 8:s % 8 + 1]).then_inc(exped, 1)

            def keep_turned(i, s):
                b, r = s // R, s % R
                if r == 0:
                    act.wait_ge(mixed, i * NB + max(b - 1, 0))
                act.wait_ge(turned, i * ST + s + 1)
                act.activation(probsT[:, b % 2, :, r * P:(r + 1) * P],
                               probsT_ps[s % 2][:, 0:KB * P].rearrange("p (k n) -> p k n", k=KB), ACT.Copy
                               ).then_inc(turned_kept, 1)
                if r == R - 1:
                    act.activation(last_probsT[0:1, b % 2, :], last_ps[0:1, :], ACT.Copy).then_inc(last_kept, 1)

            with act.Fori(0, ITERS) as i:
                act.wait_ge(x_turned, i + 1)
                act.activation(xnT[:, :, :], misc_ps[0][:, :].rearrange("p (c n) -> p c n", c=NC), ACT.Copy
                               ).then_inc(xnT_ready, 1)
                if layer == 1:
                    for m in range(G * NQ):
                        act.wait_ge(n_summed, i * (G * NQ) + max(m - 1, 0))
                        act.wait_ge(n_made, i * (G * NQ) + m + 1)
                        act.activation(squares[:, m % 2, :], misc_ps[m % 2][:, :], ACT.Square).then_inc(n_squared, 1)
                for hp in range(0, HP, 2):
                    act.wait_ge(q_made, i * HP + hp + 1)
                    act.activation(qT[:, :, 2 * hp:2 * hp + 2, :].rearrange("p b h t -> p h b t"),
                                   misc_ps[0][:, :].rearrange("p (h b t) -> p h b t", h=2, t=T), ACT.Copy
                                   ).then_inc(q_kept_act, 1)
                if layer == 1:
                    act.wait_ge(rows_ready, i + 1)
                for s in range(AHEAD):
                    exp(i, s)
                for s in range(ST):
                    keep_turned(i, s)
                    if s + AHEAD < ST:
                        exp(i, s + AHEAD)

        @block.vector
        def _(dve):
            LINKS = 1 + 2 * ST

            def row_stats(g, link):
                for t in range(G):
                    ins = dve.bn_stats(stats[:, t, :], x_sb[:, bass.ds(g * G + t, 1), :])
                link(ins, alone=True)
                for t in range(G):
                    ins = dve.bn_aggr(mv[:, t, :], stats[:, t, :])
                ins.then_inc(var_ready, 1)

            def normalize(g):
                dve.wait_ge(rstd_ready, g + 1)
                dve.wait_ge(x_turned, g)
                for t in range(G):
                    dve.tensor_scalar(xn[:, t, :], x_sb[:, bass.ds(g * G + t, 1), :], mv[:, t, 0:1], rstd[:, t:t + 1],
                                      ALU.subtract, ALU.mult).then_inc(normed, 1)

            def weigh(i, s, link):
                b, r = s // R, s % R
                if layer == 0:
                    if r == 0:
                        dve.wait_ge(bias_ready, i * NB + b + 1)
                    other, op = bias[:, b % 2, :], ALU.add
                else:
                    if s == 0:
                        dve.wait_ge(rows_ready, i + 1)
                    if r == 0:
                        dve.wait_ge(kscale_loaded[b % 2], i * (16 * R * NB // 2) + 16 * R * (b // 2 + 1))
                    other, op = key_scale[:, b % 2, r, :], ALU.mult
                dve.wait_ge(turned, i * ST + max(s - SR + 1, 0))
                dve.wait_ge(scored, i * ST + s + 1)
                apart(dve, passed)
                col = slice(s % 8, s % 8 + 1)
                link(dve.tensor_tensor_reduce(out=probs[:, s % SR, :], in0=score_ps[s % 2][:, 0:S2], in1=other, scale=1.0,
                                              scalar=-3.4e38, op0=op, op1=ALU.max, accum_out=top[:, col]))
                if layer == 0:
                    dve.tensor_scalar(shift[:, col], top[:, col], -1.0, None, ALU.mult).then_inc(shifted, 1)
                else:
                    dve.tensor_scalar(shift[:, col], top[:, col], row_scale[:, b // BT, b % BT, r:r + 1], -1.0,
                                      ALU.mult, ALU.mult).then_inc(shifted, 1)

            def share_out(i, s, link):
                dve.wait_ge(exped, i * ST + s + 1)
                col = slice(s % 8, s % 8 + 1)
                link(dve.reciprocal(share[:, col], total[:, col]))
                dve.tensor_scalar(probs[:, s % SR, :], probs[:, s % SR, :], share[:, col], None, ALU.mult
                                  ).then_inc(probs_ready, 1)

            def keep_mix(i, b):
                if b == 0:
                    dve.wait_ge(projected, i * G)
                dve.wait_ge(mixed, i * NB + b + 1)
                to, mix = mixT[:, :, b * T:(b + 1) * T], mix_ps[:, :].rearrange("p (h t) -> p h t", h=H)
                if layer == 0:
                    dve.tensor_scalar(to, mix, any_key[:, bass.ds(i * NB + b, 1)], None, ALU.mult).then_inc(mix_kept, 1)
                else:
                    dve.tensor_copy(to, mix).then_inc(mix_kept, 1)

            if layer == 0:
                dve.wait_ge(pre_loaded, 16)
                dve.tensor_reduce(any_key[:, :], mask[:, :, :], AX_X, ALU.max).then_inc(any_ready, 1)
                dve.wait_ge(any_ready, 1)
            row_stats(0, Chain(dve, dve_chain, 0, passed))
            normalize(0)
            with dve.Fori(0, ITERS) as i:
                link = Chain(dve, dve_chain, i * LINKS + 1, passed)
                if layer == 1:
                    for m in range(G * NQ):
                        dve.wait_ge(n_squared, i * (G * NQ) + m + 1)
                        dve.tensor_reduce(q_sum[:, m // NQ, (m % NQ) * (H // NQ):(m % NQ + 1) * (H // NQ)],
                                          squares[:, m % 2, :].rearrange("p (h d) -> p h d", d=HD), AX_X, ALU.add
                                          ).then_inc(n_summed, 1)
                for hp in range(1, HP, 2):
                    dve.wait_ge(q_made, i * HP + hp + 1)
                    dve.tensor_copy(qT[:, :, 2 * hp:2 * hp + 2, :].rearrange("p b h t -> p h b t"),
                                    misc_ps[1][:, :].rearrange("p (h b t) -> p h b t", h=2, t=T)).then_inc(q_kept_dve, 1)
                for s in range(AHEAD):
                    weigh(i, s, link)
                for s in range(EARLY):
                    share_out(i, s, link)
                for s in range(ST):
                    if s % R == 1 and s >= 2 * R:
                        keep_mix(i, s // R - 2)
                    if s + EARLY < ST:
                        share_out(i, s + EARLY, link)
                    if s + AHEAD < ST:
                        weigh(i, s + AHEAD, link)
                    if s == ST // 2:
                        row_stats(i + 1, link)
                    if s == ST // 2 + R:
                        normalize(i + 1)
                keep_mix(i, NB - 2)
                keep_mix(i, NB - 1)
                for t in range(G):
                    dve.wait_ge(projected, i * G + t + 1)
                    tile = x_sb[:, bass.ds(i * G + t, 1), :].rearrange("p a d -> p (a d)")
                    dve.tensor_tensor(tile, tile, misc_ps[t][:, 0:D], ALU.add).then_inc(added, 1)
                assert link.n == LINKS

        @block.gpsimd
        def _(pool):
            pool.memset(minus_half[:, :], -0.5).then_inc(begun, 1)
            pool.wait_ge(begun, 1)
            LINKS = 1 + NB if layer == 0 else 1 + 2

            def norm_scale(g, link):
                pool.wait_ge(var_ready, g + 1)
                apart(pool, passed)
                link(pool.tensor_scalar(rstd[:, :], mv[:, :, 1], LN_EPS, None, ALU.add))
                pool.tensor_tensor(rstd[:, :], rstd[:, :], minus_half[:, 0:G], ALU.pow).then_inc(rstd_ready, 1)

            if layer == 0:
                pool.wait_ge(pre_loaded, 16)
            norm_scale(0, Chain(pool, pool_chain, 0, passed))
            with pool.Fori(0, ITERS) as i:
                link = Chain(pool, pool_chain, i * LINKS + 1, passed)
                if layer == 0:
                    for b in range(NB):
                        if b == NB // 2 + 2:
                            norm_scale(i + 1, link)
                        pool.wait_ge(bias_ready, i * NB + b)
                        pool.wait_ge(shifted, i * ST + max(b - 1, 0) * R)
                        apart(pool, passed)
                        link(pool.tensor_copy(valid[:, :], mask[:, bass.ds(i * NB + b, 1), :].rearrange("p a s -> p (a s)")),
                             alone=True)
                        pool.tensor_scalar(bias[:, b % 2, :], valid[:, :], 1.0, 1e30, ALU.subtract, ALU.mult
                                           ).then_inc(bias_ready, 1)
                else:
                    flat = q_rms[:, :, :].rearrange("p g h -> p (g h)")
                    pool.wait_ge(n_summed, i * (G * NQ) + G * NQ)
                    apart(pool, passed)
                    link(pool.tensor_scalar(flat, q_sum[:, :, :].rearrange("p g h -> p (g h)"), 1.0 / HD, LN_EPS,
                                            ALU.mult, ALU.add))
                    link(pool.tensor_tensor(flat, flat, minus_half[:, :], ALU.pow), alone=True)
                    for b in range(BT):
                        for j in range(HR):
                            ins = pool.tensor_scalar(
                                row_scale[j * T:(j + 1) * T, :, b, :],
                                q_rms[b * T:(b + 1) * T, :, :].rearrange("p g (r j) -> p g r j", j=HR)[:, :, :, j],
                                SCALE, None, ALU.mult)
                    ins.then_inc(rows_ready, 1)
                    norm_scale(i + 1, link)


def row_stats(dve, x_tile, stats, mv, link):
    link(dve.bn_stats(stats[:, :], x_tile), alone=True)
    return dve.bn_aggr(mv[:, :], stats[:, :])


def rstd_of(pool, mv, rstd, minus_half, link):
    link(pool.tensor_scalar(rstd[:, :], mv[:, 1:2], LN_EPS, None, ALU.add))
    return pool.tensor_tensor(rstd[:, :], rstd[:, :], minus_half[:, :], ALU.pow)


def own_scores(act, blocks, score_ps, b):
    q = slice(b * T, (b + 1) * T)
    return act.activation(blocks[q, :, :], score_ps[q, :, q], ACT.Copy)


def per_head(x, n=T):
    return x.unsqueeze(2).broadcast_to([P, H, n])


def self_attention(nc, I, x_sb, ident):
    with ExitStack() as ctx:
        sc = Scope(nc, ctx, "sa0")
        HC = AH // NC
        w_rows, out_rows = sc.sb("w_rows", [P, 3 * NC, D]), sc.sb("out_rows", [P, NC, D])
        wT, outT = sc.sb("wT", [P, NC, 3 * D]), sc.sb("outT", [P, NC, D])
        bias_qk, bias_v, bias_out = sc.sb("bias_qk", [P, 2 * NC]), sc.sb("bias_v", [P, D]), sc.sb("bias_out", [P, D])
        head_mask = sc.sb("head_mask", [P, HC])
        stats, mv, rstd, minus_half = sc.sb("stats", [P, 6]), sc.sb("mv", [P, 2]), sc.sb("rstd", [P, 1]), sc.sb("minus_half", [P, 1])
        xn, xnT = sc.sb("xn", [P, D]), sc.sb("xnT", [P, NC, P])
        qkT, k_heads, v = sc.sb("qkT", [P, 2 * NC, P]), sc.sb("k_heads", [P, AH, P]), sc.sb("v", [P, D])
        blocks, top, total = sc.sb("blocks", [P, AH, T]), sc.sb("top", [P, AH]), sc.sb("total", [P, AH])
        probsT = sc.sb("probsT", [P, AH, P])
        mix, mixT = sc.sb("mix", [P, D]), sc.sb("mixT", [P, NC, P])
        score_ps = sc.ps("score", [P, AH, P])
        turn_ps, qk_ps, v_ps, mix_ps = sc.ps("turn"), sc.ps("qk"), sc.ps("v"), sc.ps("mix")

        loaded, mask_step, mask_ready = sc.sem("loaded"), sc.sem("mask_step"), sc.sem("mask_ready")
        w_turned, w_kept, zeroed, half_set = sc.sem("w_turned"), sc.sem("w_kept"), sc.sem("zeroed"), sc.sem("half_set")
        passed, dve_chain, pool_chain = sc.sem("passed"), sc.sem("dve_chain"), sc.sem("pool_chain")
        var_ready, rstd_ready, normed = sc.sem("var_ready"), sc.sem("rstd_ready"), sc.sem("normed")
        x_turned, xnT_ready = sc.sem("x_turned"), sc.sem("xnT_ready")
        qk_made, qk_kept, heads_ready = sc.sem("qk_made"), sc.sem("qk_kept"), sc.sem("heads_ready")
        v_made, v_kept, scored, blocks_act = sc.sem("v_made"), sc.sem("v_kept"), sc.sem("scored"), sc.sem("blocks_act")
        shifted, exped, probsT_ready = sc.sem("shifted"), sc.sem("exped"), sc.sem("probsT_ready")
        mixed, mix_kept, mix_turned, mixT_ready = sc.sem("mixed"), sc.sem("mix_kept"), sc.sem("mix_turned"), sc.sem("mixT_ready")
        projected, added = sc.sem("projected"), sc.sem("added")
        block = sc.block()

        @block.sync
        def _(sp):
            sp.dma_start(w_rows[:, :, :], I["L0_attn_Wqkv_w"].rearrange("(c p) d -> p c d", p=P)).then_inc(loaded, 16)
            sp.dma_start(out_rows[:, :, :], I["L0_attn_out_w"].rearrange("(c p) d -> p c d", p=P)).then_inc(loaded, 16)
            with nc.allow_non_contiguous_dma(reason="one bias per partition"):
                sp.dma_start(bias_qk[:, :], I["L0_attn_Wqkv_b"][0:2 * D].rearrange("(c p) -> p c", p=P)).then_inc(loaded, 16)
            sp.dma_start(bias_v[:, :], I["L0_attn_Wqkv_b"][2 * D:3 * D].partition_broadcast(P)).then_inc(loaded, 16)
            sp.dma_start(bias_out[:, :], I["L0_attn_out_b"].partition_broadcast(P)).then_inc(loaded, 16)
            sp.wait_ge(loaded, 80)

        @block.tensor
        def _(pe):
            def turn_x(n):
                pe.wait_ge(normed, n + 1)
                pe.wait_ge(mixT_ready, n if isinstance(n, int) and n == 0 else n - 1)
                for c in range(NC):
                    ins = pe.transpose(turn_ps[:, c * P:(c + 1) * P], xn[:, c * P:(c + 1) * P], ident[:, :])
                ins.then_inc(x_turned, 1)

            def project_qk(n):
                pe.wait_ge(xnT_ready, n + 1)
                pe.wait_ge(qk_kept, 2 * NC * n)
                for m in range(2 * NC):
                    for c in range(NC):
                        ins = pe.matmul(qk_ps[:, m * P:(m + 1) * P], wT[:, c, m * P:(m + 1) * P], xnT[:, c, :],
                                        start=(c == 0), stop=(c == NC - 1))
                ins.then_inc(qk_made, 1)

            def project_v(n, added_before):
                pe.wait_ge(added, added_before)
                for c in range(NC):
                    ins = pe.matmul(v_ps[:, 0:D], xnT[:, c, :], wT[:, c, 2 * D:3 * D], start=(c == 0), stop=(c == NC - 1))
                ins.then_inc(v_made, 1)

            def score(n):
                pe.wait_ge(heads_ready, NC * n + NC)
                pe.wait_ge(qk_kept, 2 * NC * (n + 1))
                for m in range(AH // 4):
                    c = m * 4 // HC
                    ins = pe.matmul(score_ps[:, 4 * m:4 * m + 4, :], qkT[:, c, :], k_heads[:, 4 * m:4 * m + 4, :],
                                    start=True, stop=True)
                ins.then_inc(scored, 1)

            def mix_v(n):
                pe.wait_ge(probsT_ready, n + 1)
                pe.wait_ge(v_kept, n + 1)
                for h in range(AH):
                    ins = pe.matmul(mix_ps[:, h * AD:(h + 1) * AD], probsT[:, h, :], v[:, h * AD:(h + 1) * AD],
                                    start=True, stop=True)
                ins.then_inc(mixed, 1)

            def project_out(n):
                pe.wait_ge(mix_kept, n + 1)
                pe.wait_ge(xnT_ready, n + 2)
                for c in range(NC):
                    ins = pe.transpose(turn_ps[:, c * P:(c + 1) * P], mix[:, c * P:(c + 1) * P], ident[:, :])
                ins.then_inc(mix_turned, 1)
                pe.wait_ge(mixT_ready, n + 1)
                pe.wait_ge(v_kept, n + 1)
                for c in range(NC):
                    ins = pe.matmul(v_ps[:, D:2 * D], mixT[:, c, :], outT[:, c, :], start=(c == 0), stop=(c == NC - 1))
                ins.then_inc(projected, 1)

            pe.wait_ge(loaded, 80)
            for m in range(3 * NC + NC):
                if m:
                    pe.wait_ge(w_kept, m)
                src = w_rows[:, m, :] if m < 3 * NC else out_rows[:, m - 3 * NC, :]
                for c in range(NC):
                    ins = pe.transpose(turn_ps[:, c * P:(c + 1) * P], src[:, c * P:(c + 1) * P], ident[:, :])
                ins.then_inc(w_turned, 1)
            pe.wait_ge(w_kept, 4 * NC)
            turn_x(0)
            project_qk(0)
            project_v(0, 0)
            score(0)
            pe.wait_ge(xnT_ready, 1)
            turn_x(1)
            with pe.Fori(0, NT - 1) as i:
                pe.wait_ge(blocks_act, i * BT + BT)
                project_qk(i + 1)
                mix_v(i)
                pe.wait_ge(v_kept, i + 1)
                project_v(i + 1, i)
                score(i + 1)
                pe.wait_ge(v_kept, i + 2)
                project_out(i)
                turn_x(i + 2)
            mix_v(NT - 1)
            project_out(NT - 1)

        @block.scalar
        def _(act):
            def keep_xnT(n):
                act.wait_ge(x_turned, n + 1)
                act.activation(xnT[:, :, :], turn_ps[:, 0:D].rearrange("p (c t) -> p c t", c=NC), ACT.Copy).then_inc(xnT_ready, 1)

            def keep_qk(n):
                act.wait_ge(qk_made, n + 1)
                for m in range(2 * NC):
                    act.activation(qkT[:, m, :], qk_ps[:, m * P:(m + 1) * P], ACT.Identity, bias=bias_qk[:, m:m + 1]
                                   ).then_inc(qk_kept, 1)

            def keep_v(n):
                act.wait_ge(v_made, n + 1)
                act.activation(v[:, :], v_ps[:, 0:D], ACT.Copy).then_inc(v_kept, 1)

            def keep_blocks(n):
                act.wait_ge(scored, n + 1)
                act.wait_ge(probsT_ready, n)
                for b in range(BT):
                    own_scores(act, blocks, score_ps, b).then_inc(blocks_act, 1)

            def exp(n):
                act.wait_ge(shifted, n + 1)
                act.activation(blocks[:, :, :], blocks[:, :, :], ACT.Exp, scale=float(AD) ** -0.5).then_inc(exped, 1)

            def keep_mixT(n):
                act.wait_ge(mix_turned, n + 1)
                act.activation(mixT[:, :, :], turn_ps[:, 0:D].rearrange("p (c t) -> p c t", c=NC), ACT.Copy).then_inc(mixT_ready, 1)

            for m in range(4 * NC):
                act.wait_ge(w_turned, m + 1)
                dst = wT[:, :, m * P:(m + 1) * P] if m < 3 * NC else outT[:, :, (m - 3 * NC) * P:(m - 3 * NC + 1) * P]
                act.activation(dst, turn_ps[:, 0:D].rearrange("p (c t) -> p c t", c=NC), ACT.Copy).then_inc(w_kept, 1)
            keep_xnT(0)
            keep_qk(0)
            keep_v(0)
            keep_blocks(0)
            act.wait_ge(v_made, 1)
            keep_xnT(1)
            with act.Fori(0, NT - 1) as i:
                exp(i)
                keep_qk(i + 1)
                act.wait_ge(mixed, i + 1)
                keep_v(i + 1)
                keep_mixT(i)
                keep_blocks(i + 1)
                keep_xnT(i + 2)
            exp(NT - 1)
            keep_mixT(NT - 1)

        @block.vector
        def _(dve):
            LINKS = 6

            def stats_of(n, link):
                row_stats(dve, x_sb[:, bass.ds(n, 1), :].rearrange("p a d -> p (a d)"), stats, mv, link).then_inc(var_ready, 1)

            def normalize(n):
                dve.wait_ge(rstd_ready, n + 1)
                dve.wait_ge(x_turned, n)
                dve.tensor_scalar(xn[:, :], x_sb[:, bass.ds(n, 1), :].rearrange("p a d -> p (a d)"), mv[:, 0:1], rstd[:, 0:1],
                                  ALU.subtract, ALU.mult).then_inc(normed, 1)

            def softmax(n, link):
                dve.wait_ge(blocks_act, BT * n + BT)
                link(dve.tensor_reduce(top[:, :], blocks[:, :, :], AX_X, ALU.max))
                dve.tensor_tensor(blocks[:, :, :], blocks[:, :, :], per_head(top[:, :]), ALU.subtract).then_inc(shifted, 1)
                dve.wait_ge(exped, n + 1)
                link(dve.tensor_reduce(total[:, :], blocks[:, :, :], AX_X, ALU.add))
                link(dve.reciprocal(total[:, :], total[:, :]))
                link(dve.tensor_tensor(blocks[:, :, :], blocks[:, :, :], per_head(total[:, :]), ALU.mult))
                dve.wait_ge(mixed, n)
                for b in range(BT):
                    q = slice(b * T, (b + 1) * T)
                    ins = dve.transpose(probsT[q, :, q], blocks[q, :, :])
                ins.then_inc(probsT_ready, 1)

            def finish(n, link):
                dve.wait_ge(mixed, n + 1)
                dve.wait_ge(mix_turned, n)
                dve.tensor_tensor(mix[:, :], mix_ps[:, 0:D], bias_v[:, :], ALU.add).then_inc(mix_kept, 1)

            def add(n, link):
                tile = x_sb[:, bass.ds(n, 1), :].rearrange("p a d -> p (a d)")
                link(dve.tensor_tensor(tile, tile, bias_out[:, :], ALU.add))
                dve.wait_ge(projected, n + 1)
                dve.tensor_tensor(tile, tile, v_ps[:, D:2 * D], ALU.add).then_inc(added, 1)

            dve.memset(probsT[:, :, :], 0.0).then_inc(zeroed, 1)
            dve.wait_ge(zeroed, 1)
            dve.wait_ge(loaded, 80)
            link = Chain(dve, dve_chain, 0, passed)
            stats_of(0, link)
            normalize(0)
            stats_of(1, link)
            normalize(1)
            with dve.Fori(0, NT - 1) as i:
                link = Chain(dve, dve_chain, i * LINKS + 2, passed)
                softmax(i, link)
                stats_of(i + 2, link)
                finish(i, link)
                normalize(i + 2)
                add(i, link)
                assert link.n == LINKS
            link = Chain(dve, dve_chain, (NT - 1) * LINKS + 2, passed)
            softmax(NT - 1, link)
            finish(NT - 1, link)
            add(NT - 1, link)

        @block.gpsimd
        def _(pool):
            pool.memset(minus_half[:, :], -0.5).then_inc(half_set, 1)
            pool.memset(head_mask[:, :], 1.0).then_inc(mask_step, 1)
            pool.wait_ge(mask_step, 1)
            pool.affine_select(out=head_mask[:, :], in_=head_mask[:, :], compare_op=ALU.is_ge, fill=0.0, base=0,
                               pattern=[[-AD, HC]], channel_multiplier=1).then_inc(mask_step, 1)
            pool.wait_ge(mask_step, 2)
            pool.affine_select(out=head_mask[:, :], in_=head_mask[:, :], compare_op=ALU.is_ge, fill=0.0, base=AD - 1,
                               pattern=[[AD, HC]], channel_multiplier=-1).then_inc(mask_step, 1)
            pool.wait_ge(mask_step, 3)
            pool.wait_ge(half_set, 1)

            def scale_of(n, base):
                link = Chain(pool, pool_chain, base, passed)
                pool.wait_ge(var_ready, n + 1)
                apart(pool, passed)
                rstd_of(pool, mv, rstd, minus_half, link).then_inc(rstd_ready, 1)

            def mask_keys(n):
                for c in range(NC):
                    pool.wait_ge(scored, n)
                    pool.wait_ge(qk_kept, 2 * NC * n + NC + c + 1)
                    pool.tensor_tensor(k_heads[:, c * HC:(c + 1) * HC, :],
                                       qkT[:, NC + c, :].unsqueeze(1).broadcast_to([P, HC, P]),
                                       head_mask[:, :].unsqueeze(2).broadcast_to([P, HC, P]), ALU.mult).then_inc(heads_ready, 1)

            scale_of(0, 0)
            mask_keys(0)
            scale_of(1, 1)
            with pool.Fori(0, NT - 1) as i:
                mask_keys(i + 1)
                scale_of(i + 2, i + 2)


def route(nc, I, x_sb, ident, slot_rows, slots_all, weights_all):
    with ExitStack() as ctx:
        sc = Scope(nc, ctx, "rt")
        router, routerT = sc.sb("router", [E0, D]), sc.sb("routerT", [P, NC, E0])
        upto, ones, slot_base = sc.sb("upto", [P, P]), sc.sb("ones", [P, P]), sc.sb("slot_base", [P, E0])
        zeros = sc.sb("zeros", [P, 2048])
        stats, mv, rstd, minus_half = sc.sb("stats", [P, 6]), sc.sb("mv", [P, 2]), sc.sb("rstd", [P, 1]), sc.sb("minus_half", [P, 1])
        xn, xnT = sc.sb("xn", [P, 2, D]), sc.sb("xnT", [P, NC, P])
        prob, rest, chosen, before = (sc.sb(n, [P, E0]) for n in ("prob", "rest", "chosen", "before"))
        gate, code, picked = sc.sb("gate", [P, E0]), sc.sb("code", [P, E0]), sc.sb("picked", [P, E0])
        top, best, scale = sc.sb("top", [P, 1]), sc.sb("best", [P, K0]), sc.sb("scale", [P, 2])
        codes = sc.sb("codes", [P, K0])
        places = sc.sb("places", [P, 2, K0], U32)
        turn_ps, logit_ps, place_ps = sc.ps("turn"), sc.ps("logit"), sc.ps("place")
        loaded, w_turned, w_kept = sc.sem("loaded"), sc.sem("w_turned"), sc.sem("w_kept")
        const_step, consts_ready, zeroed, cleared = sc.sem("const_step"), sc.sem("consts_ready"), sc.sem("zeroed"), sc.sem("cleared")
        passed, dve_chain, pool_chain = sc.sem("passed"), sc.sem("dve_chain"), sc.sem("pool_chain")
        var_ready, rstd_ready, normed = sc.sem("var_ready"), sc.sem("rstd_ready"), sc.sem("normed")
        x_turned, xnT_ready, routed = sc.sem("x_turned"), sc.sem("xnT_ready"), sc.sem("routed")
        shifted, exped, chosen_ready, counted = sc.sem("shifted"), sc.sem("exped"), sc.sem("chosen_ready"), sc.sem("counted")
        places_ready = sc.sem("places_ready")
        scattered = [sc.pool_dma_sem(f"scattered{p}") for p in range(2)]
        block = sc.block()
        U = 2
        ITERS = NT // U

        @block.sync
        def _(sp):
            sp.dma_start(router[:, :], I["L0_ffn_router_w"]).then_inc(loaded, 16)
            sp.wait_ge(zeroed, 1)
            per = zeros.shape[1] * P
            flat = slot_rows.rearrange("(n p r) d -> n p (r d)", p=P, r=2048 // D)
            for n in range(SLOTS * D // per):
                sp.dma_start(flat[n], zeros[:, :]).then_inc(cleared, 16)
            sp.wait_ge(cleared, 16 * (SLOTS * D // per))

        @block.tensor
        def _(pe):
            pe.wait_ge(loaded, 16)
            for c in range(NC):
                ins = pe.transpose(turn_ps[:, c * E0:(c + 1) * E0], router[:, c * P:(c + 1) * P], ident[0:E0, 0:E0])
            ins.then_inc(w_turned, 1)
            pe.wait_ge(w_kept, 1)
            pe.wait_ge(consts_ready, 1)
            with pe.Fori(0, ITERS) as i:
                for u in range(U):
                    n = i * U + u
                    pe.wait_ge(normed, n + 1)
                    pe.wait_ge(xnT_ready, n)
                    for c in range(NC):
                        ins = pe.transpose(turn_ps[:, c * P:(c + 1) * P], xn[:, u, c * P:(c + 1) * P], ident[:, :])
                    ins.then_inc(x_turned, 1)
                    pe.wait_ge(xnT_ready, n + 1)
                    pe.wait_ge(exped, n)
                    for c in range(NC):
                        ins = pe.matmul(logit_ps[:, 0:E0], xnT[:, c, :], routerT[:, c, :], start=(c == 0), stop=(c == NC - 1))
                    ins.then_inc(routed, 1)
                    pe.wait_ge(chosen_ready, n + 1)
                    pe.wait_ge(places_ready, n)
                    pe.matmul(place_ps[:, 0:E0], upto[:, :], chosen[:, :], start=True, stop=False)
                    pe.matmul(place_ps[:, 0:E0], ones[:, :], before[:, :], start=False, stop=True).then_inc(counted, 1)

        @block.scalar
        def _(act):
            act.wait_ge(w_turned, 1)
            act.activation(routerT[:, :, :], turn_ps[:, 0:NC * E0].rearrange("p (c e) -> p c e", c=NC), ACT.Copy).then_inc(w_kept, 1)
            with act.Fori(0, ITERS) as i:
                for u in range(U):
                    n = i * U + u
                    act.wait_ge(x_turned, n + 1)
                    act.activation(xnT[:, :, :], turn_ps[:, 0:D].rearrange("p (c t) -> p c t", c=NC), ACT.Copy).then_inc(xnT_ready, 1)
                    act.wait_ge(shifted, n + 1)
                    act.activation(prob[:, :], logit_ps[:, 0:E0], ACT.Exp, bias=top[:, 0:1], accum_out=scale[:, 0:1]).then_inc(exped, 1)

        @block.vector
        def _(dve):
            LINKS = 11 + K0
            dve.memset(before[:, :], 0.0).then_inc(const_step, 1)

            def stats_of(n, link):
                row_stats(dve, x_sb[:, bass.ds(n, 1), :].rearrange("p a d -> p (a d)"), stats, mv, link).then_inc(var_ready, 1)

            def normalize(n, u, uses):
                dve.wait_ge(rstd_ready, n + 1)
                dve.wait_ge(scattered[u], uses)
                dve.tensor_scalar(xn[:, u, :], x_sb[:, bass.ds(n, 1), :].rearrange("p a d -> p (a d)"), mv[:, 0:1], rstd[:, 0:1],
                                  ALU.subtract, ALU.mult).then_inc(normed, 1)

            stats_of(0, Chain(dve, dve_chain, 0, passed))
            dve.wait_ge(consts_ready, 1)
            with dve.Fori(0, ITERS) as i:
                for u in range(U):
                    n = i * U + u
                    link = Chain(dve, dve_chain, n * LINKS + 1, passed)
                    normalize(n, u, i * (16 * K0))
                    stats_of(n + 1, link)
                    dve.wait_ge(routed, n + 1)
                    dve.tensor_reduce(top[:, :], logit_ps[:, 0:E0], AX_X, ALU.max, negate=True).then_inc(shifted, 1)
                    dve.wait_ge(exped, n + 1)
                    link(dve.reciprocal(scale[:, 1:2], scale[:, 0:1]))
                    link(dve.tensor_scalar(prob[:, :], prob[:, :], scale[:, 1:2], None, ALU.mult), alone=True)
                    link(dve.max(best[:, :], prob[:, :]), alone=True)
                    link(dve.match_replace(rest[:, :], best[:, :], prob[:, :], -1.0))
                    dve.tensor_tensor(chosen[:, :], prob[:, :], rest[:, :], ALU.not_equal).then_inc(chosen_ready, 1)
                    link(dve.tensor_reduce(scale[:, 0:1], best[:, :], AX_X, ALU.add))
                    link(dve.tensor_scalar(scale[:, 0:1], scale[:, 0:1], 1e-20, None, ALU.add))
                    link(dve.reciprocal(scale[:, 1:2], scale[:, 0:1]))
                    dve.tensor_scalar(gate[:, :], prob[:, :], scale[:, 1:2], None, ALU.mult)
                    dve.wait_ge(counted, n + 1)
                    dve.tensor_tensor(code[:, :], slot_base[:, :], place_ps[:, 0:E0], ALU.subtract)
                    dve.tensor_tensor(before[:, :], before[:, :], chosen[:, :], ALU.add)
                    link(dve.scalar_tensor_tensor(out=picked[:, :], in0=place_ps[:, 0:E0], scalar=float(CAP), in1=chosen[:, :],
                                                  op0=ALU.is_le, op1=ALU.mult))
                    link(dve.tensor_tensor(code[:, :], code[:, :], picked[:, :], ALU.mult), alone=True)
                    link(dve.max(codes[:, :], code[:, :]))
                    dve.tensor_scalar(slots_all[:, bass.ds(n, 1), :].rearrange("p a k -> p (a k)"), codes[:, :], -1.0,
                                      float(NOWHERE), ALU.mult, ALU.add)
                    for k in range(K0):
                        link(dve.scalar_tensor_tensor(out=picked[:, :], in0=code[:, :], scalar=codes[:, k:k + 1], in1=gate[:, :],
                                                      op0=ALU.is_equal, op1=ALU.mult,
                                                      accum_out=weights_all[:, bass.ds(n * K0 + k, 1)]))
                    dve.tensor_scalar(places[:, u, :], codes[:, :], -1.0, float(NOWHERE), ALU.mult, ALU.add
                                      ).then_inc(places_ready, 1)
                    assert link.n == LINKS, link.n

        @block.gpsimd
        def _(pool):
            pool.memset(zeros[:, :], 0.0).then_inc(zeroed, 1)
            pool.memset(minus_half[:, :], -0.5).then_inc(const_step, 1)
            pool.memset(ones[:, :], 1.0).then_inc(const_step, 1)
            pool.memset(upto[:, :], 1.0).then_inc(const_step, 1)
            pool.iota(slot_base[:, :], pattern=[[-CAP, E0]], base=NOWHERE + 1, channel_multiplier=0,
                      allow_small_or_imprecise_dtypes=True).then_inc(const_step, 1)
            pool.wait_ge(const_step, 5)
            pool.affine_select(out=upto[:, :], in_=upto[:, :], compare_op=ALU.is_ge, fill=0.0, base=0,
                               pattern=[[1, P]], channel_multiplier=-1).then_inc(consts_ready, 1)

            def scale_of(n):
                link = Chain(pool, pool_chain, n, passed)
                pool.wait_ge(var_ready, n + 1)
                apart(pool, passed)
                rstd_of(pool, mv, rstd, minus_half, link).then_inc(rstd_ready, 1)

            scale_of(0)
            pool.wait_ge(cleared, 16 * (SLOTS * D // (2048 * P)))
            with pool.Fori(0, ITERS) as i:
                for u in range(U):
                    n = i * U + u
                    scale_of(n + 1)
                    pool.wait_ge(places_ready, n + 1)
                    apart(pool, passed)
                    for k in range(K0):
                        pool.indirect_dma_start(out=slot_rows, out_offset=bass.IndirectOffsetOnAxis(ap=places[:, u, k:k + 1], axis=0),
                                                in_=xn[:, u, :], in_offset=None, bounds_check=SLOTS - 1, oob_is_err=False
                                                ).then_inc(scattered[u], 16)
            for u in range(U):
                pool.wait_ge(scattered[u], ITERS * 16 * K0)


def experts(nc, I, ident, slot_rows, slot_out):
    with ExitStack() as ctx:
        sc = Scope(nc, ctx, "ex")
        BUF = 4
        TURNS = E0 // 2
        ITERS = TURNS // BUF
        rows = sc.sb("rows", [P, BUF, D])
        w_in = sc.sb("w_in", [P, BUF, 2, 2, NC, F0])
        w_out = sc.sb("w_out", [F0, BUF, 2, D])
        rowsT = sc.sb("rowsT", [P, 2, NC, P])
        gate, hidden = sc.sb("gate", [F0, 2, P]), sc.sb("hidden", [F0, 2, P])
        out_rows = sc.sb("out_rows", [P, 2, D])
        turn_ps = [sc.ps(f"turn{n}") for n in range(2)]
        mid_ps = [sc.ps(f"mid{n}") for n in range(2)]
        out_ps = [sc.ps(f"out{n}") for n in range(2)]
        loaded = [sc.sem(f"loaded{n}") for n in range(BUF)]
        stored = [sc.pool_dma_sem(f"stored{n}") for n in range(2)]
        turned, rowsT_ready, mid_made, gated, hidden_ready = (sc.sem(n) for n in (
            "turned", "rowsT_ready", "mid_made", "gated", "hidden_ready"))
        out_made, out_kept, passed = sc.sem("out_made"), sc.sem("out_kept"), sc.sem("passed")
        block = sc.block()

        @block.sync
        def _(sp):
            with sp.Fori(0, ITERS) as i:
                for u in range(BUF):
                    n = i * BUF + u
                    sp.wait_ge(out_made, i * BUF + max(u - BUF + 1, 0))
                    sp.dma_start(rows[:, u, :], slot_rows[bass.ds(n * P, P), :]).then_inc(loaded[u], 16)
                    for g, name in enumerate(("L0_ffn_w_gate", "L0_ffn_w_up")):
                        sp.dma_start(w_in[:, u, g], I[name].rearrange("e (p j) f -> p e (j f)", j=NC)[:, bass.ds(n * 2, 2), :]
                                     ).then_inc(loaded[u], 16)
                    sp.dma_start(w_out[:, u], I["L0_ffn_w_down"].rearrange("e f d -> f e d")[:, bass.ds(n * 2, 2), :]
                                 ).then_inc(loaded[u], 16)

        @block.tensor
        def _(pe):
            def turn(i, u):
                n = i * BUF + u
                pe.wait_ge(loaded[u], i * 64 + 64)
                pe.wait_ge(rowsT_ready, i * BUF + max(u - 1, 0))
                for j in range(NC):
                    ins = pe.transpose(turn_ps[u % 2][:, j * P:(j + 1) * P], rows[:, u, j:D:NC], ident[:, :])
                ins.then_inc(turned, 1)

            def middle(i, u):
                n = i * BUF + u
                pe.wait_ge(rowsT_ready, n + 1)
                pe.wait_ge(hidden_ready, i * BUF + max(u - 1, 0))
                for g in range(2):
                    for e in range(2):
                        for j in range(NC):
                            ins = pe.matmul(mid_ps[u % 2][0:F0, (2 * g + e) * CAP:(2 * g + e + 1) * CAP], w_in[:, u, g, e, j, :],
                                            rowsT[:, u % 2, j, e * CAP:(e + 1) * CAP], start=(j == 0), stop=(j == NC - 1))
                ins.then_inc(mid_made, 1)

            def finish(i, u):
                n = i * BUF + u
                pe.wait_ge(hidden_ready, n + 1)
                pe.wait_ge(out_kept, i * BUF + max(u - 1, 0))
                for e in range(2):
                    ins = pe.matmul(out_ps[u % 2][e * CAP:(e + 1) * CAP, 0:D], hidden[:, u % 2, e * CAP:(e + 1) * CAP],
                                    w_out[:, u, e, :], start=True, stop=True)
                ins.then_inc(out_made, 1)

            with pe.Fori(0, ITERS) as i:
                turn(i, 0)
                middle(i, 0)
                for u in range(1, BUF):
                    turn(i, u)
                    middle(i, u)
                    finish(i, u - 1)
                finish(i, BUF - 1)

        @block.scalar
        def _(act):
            with act.Fori(0, ITERS) as i:
                for u in range(BUF):
                    n = i * BUF + u
                    act.wait_ge(mid_made, i * BUF + max(u - 1, 0))
                    act.wait_ge(turned, n + 1)
                    act.activation(rowsT[:, u % 2, :, :], turn_ps[u % 2][:, 0:D].rearrange("p (j s) -> p j s", j=NC), ACT.Copy
                                   ).then_inc(rowsT_ready, 1)
                    act.wait_ge(hidden_ready, i * BUF + max(u - 1, 0))
                    act.wait_ge(mid_made, n + 1)
                    act.activation(gate[:, u % 2, :], mid_ps[u % 2][0:F0, 0:P], ACT.Silu).then_inc(gated, 1)

        @block.vector
        def _(dve):
            def keep(i, u):
                n = i * BUF + u
                dve.wait_ge(out_made, n + 1)
                dve.wait_ge(stored[u % 2], i * (16 * BUF // 2) + 16 * (u // 2))
                dve.tensor_copy(out_rows[:, u % 2, :], out_ps[u % 2][:, 0:D]).then_inc(out_kept, 1)

            with dve.Fori(0, ITERS) as i:
                for u in range(BUF):
                    n = i * BUF + u
                    dve.wait_ge(out_made, i * BUF + max(u - 1, 0))
                    dve.wait_ge(gated, n + 1)
                    dve.tensor_tensor(hidden[:, u % 2, :], mid_ps[u % 2][0:F0, P:2 * P], gate[:, u % 2, :], ALU.mult
                                      ).then_inc(hidden_ready, 1)
                    if u:
                        keep(i, u - 1)
                keep(i, BUF - 1)

        @block.gpsimd
        def _(pool):
            with pool.Fori(0, ITERS) as i:
                for u in range(BUF):
                    n = i * BUF + u
                    pool.wait_ge(out_kept, n + 1)
                    apart(pool, passed)
                    pool.dma_start(slot_out[bass.ds(n * P, P), :], out_rows[:, u % 2, :]).then_inc(stored[u % 2], 16)
            for u in range(2):
                pool.wait_ge(stored[u], 16 * TURNS // 2)


def combine(nc, x_sb, slots_all, weights_all, slot_out):
    with ExitStack() as ctx:
        sc = Scope(nc, ctx, "cb")
        U = 2
        ITERS = NT // U
        places = sc.sb("places", [P, U, K0], U32)
        got = sc.sb("got", [P, U, K0, D])
        zeroed, gathered = sc.sem("zeroed"), [sc.pool_dma_sem(f"gathered{u}") for u in range(U)]
        passed, added = sc.sem("passed"), sc.sem("added")
        block = sc.block()

        @block.vector
        def _(dve):
            with dve.Fori(0, ITERS) as i:
                for u in range(U):
                    dve.wait_ge(added, i * (U * K0))
                    dve.tensor_copy(places[:, u, :], slots_all[:, bass.ds(i * U + u, 1), :].rearrange("p a k -> p (a k)"))
                    dve.memset(got[:, u, :, :], 0.0).then_inc(zeroed, 1)
                for u in range(U):
                    dve.wait_ge(gathered[u], i * (16 * K0) + 16 * K0)
                    tile = x_sb[:, bass.ds(i * U + u, 1), :].rearrange("p a d -> p (a d)")
                    for k in range(K0):
                        if k:
                            dve.wait_ge(added, (i * U + u) * K0 + k)
                        dve.scalar_tensor_tensor(out=tile, in0=got[:, u, k, :], scalar=weights_all[:, bass.ds((i * U + u) * K0 + k, 1)],
                                                 in1=tile, op0=ALU.mult, op1=ALU.add).then_inc(added, 1)

        @block.gpsimd
        def _(pool):
            with pool.Fori(0, ITERS) as i:
                for u in range(U):
                    pool.wait_ge(zeroed, i * U + u + 1)
                    apart(pool, passed)
                    for k in range(K0):
                        pool.indirect_dma_start(out=got[:, u, k, :], out_offset=None, in_=slot_out,
                                                in_offset=bass.IndirectOffsetOnAxis(ap=places[:, u, k:k + 1], axis=0),
                                                bounds_check=SLOTS - 1, oob_is_err=False).then_inc(gathered[u], 16)


def routed_experts(nc, I, x_sb, ident):
    with ExitStack() as ctx:
        sc = Scope(nc, ctx, "moe")
        slot_rows = nc.dram_tensor("slot_rows", (SLOTS, D), F32).ap()
        slot_out = nc.dram_tensor("slot_out", (SLOTS, D), F32).ap()
        slots_all, weights_all = sc.sb("slots", [P, NT, K0], U32), sc.sb("weights", [P, NT * K0])
        route(nc, I, x_sb, ident, slot_rows, slots_all, weights_all)
        experts(nc, I, ident, slot_rows, slot_out)
        combine(nc, x_sb, slots_all, weights_all, slot_out)


def fp4_weights(nc, I, wide, narrow):
    with ExitStack() as ctx:
        sc = Scope(nc, ctx, "fp4")
        names = ("wq", "wk", "wv", "wo")
        weights = list(wide) + [narrow]
        scales = [sc.sb(f"scale_{n}", list(w.shape)) for n, w in zip(names, weights)]
        loaded = [sc.sem(f"loaded_{n}") for n in names]
        scaled = sc.sem("scaled")
        block = sc.block()
        DMAS = 1 + P // FP4_ROWS

        def load(eng, j):
            name, w, s = names[j], weights[j], scales[j]
            eng.dma_start(w[:, :, :], I[f"L1_attn_{name}_codes"].rearrange("(c p) n -> p c n", p=P)).then_inc(loaded[j], 16)
            rows = I[f"L1_attn_{name}_scales"].rearrange("(c g) n -> g c n", g=P // FP4_ROWS)
            for g in range(P // FP4_ROWS):
                eng.dma_start(s[g * FP4_ROWS:(g + 1) * FP4_ROWS, :, :], rows[g].partition_broadcast(FP4_ROWS)
                              ).then_inc(loaded[j], 16)

        def scale(eng, j):
            eng.wait_ge(loaded[j], 16 * DMAS)
            eng.tensor_tensor(weights[j][:, :, :], weights[j][:, :, :], scales[j][:, :, :], ALU.mult).then_inc(scaled, 1)

        @block.sync
        def _(sp):
            load(sp, 0)
            load(sp, 2)

        @block.scalar
        def _(act):
            load(act, 1)
            load(act, 3)

        @block.vector
        def _(dve):
            for j in range(4):
                scale(dve, j)
            dve.wait_ge(scaled, 4)


def self_attention_fp4(nc, I, x_sb, ident):
    with ExitStack() as ctx:
        sc = Scope(nc, ctx, "sa1")
        G = 4
        NG = H // G
        wq, wk, wv = (sc.sb(n, [P, NC, H * HD]) for n in ("wq", "wk", "wv"))
        wo = sc.sb("wo", [P, H, D])
        fp4_weights(nc, I, (wq, wk, wv), wo)
        bias_q, bias_k, bias_v = (sc.sb(n, [P, H]) for n in ("bias_q", "bias_k", "bias_v"))
        bias_out = sc.sb("bias_out", [P, D])
        stats, mv, rstd, minus_half = sc.sb("stats", [P, 6]), sc.sb("mv", [P, 2]), sc.sb("rstd", [P, 1]), sc.sb("minus_half", [P, 1])
        xn, xnT = sc.sb("xn", [P, D]), sc.sb("xnT", [P, NC, P])
        qT, kT, v = sc.sb("qT", [P, H, P]), sc.sb("kT", [P, H, P]), sc.sb("v", [P, H * HD])
        blocks, top, total = sc.sb("blocks", [P, H, T]), sc.sb("top", [P, H]), sc.sb("total", [P, H])
        probsT, mixT = sc.sb("probsT", [P, H, P]), sc.sb("mixT", [P, H, P])
        score_ps = sc.ps("score", [P, H, P])
        work_ps = [sc.ps(f"work{b}", [P, G, P]) for b in range(2)]
        turn_ps, out_ps = sc.ps("turn"), sc.ps("out")

        loaded, zeroed, half_set = sc.sem("loaded"), sc.sem("zeroed"), sc.sem("half_set")
        passed, dve_chain, pool_chain = sc.sem("passed"), sc.sem("dve_chain"), sc.sem("pool_chain")
        var_ready, rstd_ready, normed = sc.sem("var_ready"), sc.sem("rstd_ready"), sc.sem("normed")
        x_turned, xnT_ready = sc.sem("x_turned"), sc.sem("xnT_ready")
        q_made, q_kept, k_made, k_kept, v_made, v_kept = (sc.sem(n) for n in (
            "q_made", "q_kept", "k_made", "k_kept", "v_made", "v_kept"))
        scored, blocks_kept, shifted, exped, probsT_ready = (sc.sem(n) for n in (
            "scored", "blocks_kept", "shifted", "exped", "probsT_ready"))
        mixed, mix_kept, projected, added = (sc.sem(n) for n in ("mixed", "mix_kept", "projected", "added"))
        block = sc.block()

        @block.sync
        def _(sp):
            with nc.allow_non_contiguous_dma(reason="one bias per partition"):
                for bias, name in ((bias_q, "bq"), (bias_k, "bk"), (bias_v, "bv")):
                    sp.dma_start(bias[:, :], I["L1_attn_" + name].rearrange("(h d) -> d h", d=HD)).then_inc(loaded, 16)
            sp.dma_start(bias_out[:, :], I["L1_attn_bo"].partition_broadcast(P)).then_inc(loaded, 16)
            sp.wait_ge(loaded, 64)

        @block.tensor
        def _(pe):
            def turn_x(n):
                pe.wait_ge(normed, n + 1)
                pe.wait_ge(xnT_ready, n)
                for c in range(NC):
                    ins = pe.transpose(turn_ps[:, c * P:(c + 1) * P], xn[:, c * P:(c + 1) * P], ident[:, :])
                ins.then_inc(x_turned, 1)

            def project_qk(n):
                pe.wait_ge(xnT_ready, n + 1)
                for g in range(NG):
                    for w, ps, kept, made in ((wq, work_ps[0], q_kept, q_made), (wk, work_ps[1], k_kept, k_made)):
                        if g:
                            pe.wait_ge(kept, NG * n + g)
                        else:
                            pe.wait_ge(v_kept, NG * n)
                        for j in range(G):
                            h = g * G + j
                            for c in range(NC):
                                ins = pe.matmul(ps[:, j, :], w[:, c, h * HD:(h + 1) * HD], xnT[:, c, :],
                                                start=(c == 0), stop=(c == NC - 1))
                        ins.then_inc(made, 1)

            def project_v(n, first):
                for g in range(NG):
                    if g >= 2:
                        pe.wait_ge(v_kept, NG * n + g - 1)
                    elif first:
                        pe.wait_ge(k_kept if g else q_kept, NG)
                    else:
                        pe.wait_ge(mix_kept, NG * n - 1 + g)
                    for c in range(NC):
                        ins = pe.matmul(work_ps[g % 2][:, :, :], xnT[:, c, :], wv[:, c, g * 512:(g + 1) * 512],
                                        start=(c == 0), stop=(c == NC - 1))
                    ins.then_inc(v_made, 1)

            def score(n):
                pe.wait_ge(q_kept, NG * n + NG)
                pe.wait_ge(k_kept, NG * n + NG)
                pe.wait_ge(blocks_kept, n * BT)
                for h in range(H):
                    ins = pe.matmul(score_ps[:, h, :], qT[:, h, :], kT[:, h, :], start=True, stop=True)
                ins.then_inc(scored, 1)

            def mix(n, last):
                pe.wait_ge(probsT_ready, n + 1)
                pe.wait_ge(v_kept, NG * n + NG)
                for g in range(NG):
                    if g >= 2:
                        pe.wait_ge(mix_kept, NG * n + g - 1)
                    elif not last:
                        pe.wait_ge(k_kept if g else q_kept, NG * n + 2 * NG)
                    for j in range(G):
                        h = g * G + j
                        ins = pe.matmul(work_ps[g % 2][:, j, :], v[:, h * HD:(h + 1) * HD], probsT[:, h, :],
                                        start=True, stop=True)
                    ins.then_inc(mixed, 1)

            def project_out(n):
                pe.wait_ge(mix_kept, NG * n + NG)
                pe.wait_ge(added, n)
                for h in range(H):
                    ins = pe.matmul(out_ps[:, 0:D], mixT[:, h, :], wo[:, h, :], start=(h == 0), stop=(h == H - 1))
                ins.then_inc(projected, 1)

            turn_x(0)
            project_qk(0)
            project_v(0, True)
            turn_x(1)
            score(0)
            with pe.Fori(0, NT - 1) as i:
                project_qk(i + 1)
                mix(i, False)
                project_v(i + 1, False)
                turn_x(i + 2)
                project_out(i)
                score(i + 1)
            mix(NT - 1, True)
            project_out(NT - 1)

        @block.scalar
        def _(act):
            def keep_xnT(n):
                act.wait_ge(x_turned, n + 1)
                act.wait_ge(v_made, NG * n)
                act.activation(xnT[:, :, :], turn_ps[:, 0:D].rearrange("p (c t) -> p c t", c=NC), ACT.Copy).then_inc(xnT_ready, 1)

            def keep_k(n, g):
                act.wait_ge(scored, n)
                act.wait_ge(k_made, NG * n + g + 1)
                for j in range(G):
                    h = g * G + j
                    ins = act.activation(kT[:, h, :], work_ps[1][:, j, :], ACT.Identity, bias=bias_k[:, h:h + 1])
                ins.then_inc(k_kept, 1)

            def keep_v(n):
                for g in range(NG):
                    act.wait_ge(mixed, NG * n)
                    act.wait_ge(v_made, NG * n + g + 1)
                    act.activation(v[:, g * 512:(g + 1) * 512].rearrange("p (j d) -> p j d", j=G), work_ps[g % 2][:, :, :],
                                   ACT.Copy).then_inc(v_kept, 1)

            def keep_blocks(n):
                act.wait_ge(scored, n + 1)
                act.wait_ge(probsT_ready, n)
                for b in range(BT):
                    own_scores(act, blocks, score_ps, b).then_inc(blocks_kept, 1)

            def exp(n):
                act.wait_ge(shifted, n + 1)
                act.activation(blocks[:, :, :], blocks[:, :, :], ACT.Exp, scale=SCALE).then_inc(exped, 1)

            act.wait_ge(loaded, 64)
            keep_xnT(0)
            for g in range(NG):
                keep_k(0, g)
            keep_v(0)
            keep_xnT(1)
            keep_blocks(0)
            with act.Fori(0, NT - 1) as i:
                keep_k(i + 1, 0)
                exp(i)
                for g in range(1, NG):
                    keep_k(i + 1, g)
                keep_v(i + 1)
                keep_xnT(i + 2)
                keep_blocks(i + 1)
            exp(NT - 1)

        @block.vector
        def _(dve):
            LINKS = 6

            def tile_of(n):
                return x_sb[:, bass.ds(n, 1), :].rearrange("p a d -> p (a d)")

            def stats_of(n, link):
                row_stats(dve, tile_of(n), stats, mv, link).then_inc(var_ready, 1)

            def normalize(n):
                dve.wait_ge(rstd_ready, n + 1)
                dve.wait_ge(x_turned, n)
                dve.tensor_scalar(xn[:, :], tile_of(n), mv[:, 0:1], rstd[:, 0:1], ALU.subtract, ALU.mult).then_inc(normed, 1)

            def head_bias(bias, g):
                return bias[:, g * G:(g + 1) * G].unsqueeze(2).broadcast_to([P, G, P])

            def keep_q(n, g):
                dve.wait_ge(scored, n)
                dve.wait_ge(q_made, NG * n + g + 1)
                dve.tensor_tensor(qT[:, g * G:(g + 1) * G, :], work_ps[0][:, :, :], head_bias(bias_q, g), ALU.add
                                  ).then_inc(q_kept, 1)

            def shift(n, link):
                dve.wait_ge(blocks_kept, BT * n + BT)
                link(dve.tensor_reduce(top[:, :], blocks[:, :, :], AX_X, ALU.max))
                dve.tensor_tensor(blocks[:, :, :], blocks[:, :, :], per_head(top[:, :]), ALU.subtract).then_inc(shifted, 1)

            def divide(n, link):
                dve.wait_ge(exped, n + 1)
                link(dve.tensor_reduce(total[:, :], blocks[:, :, :], AX_X, ALU.add))
                link(dve.reciprocal(total[:, :], total[:, :]))
                link(dve.tensor_tensor(blocks[:, :, :], blocks[:, :, :], per_head(total[:, :]), ALU.mult))

            def turn_probs(n):
                dve.wait_ge(mixed, NG * n)
                for b in range(BT):
                    q = slice(b * T, (b + 1) * T)
                    ins = dve.transpose(probsT[q, :, q], blocks[q, :, :])
                ins.then_inc(probsT_ready, 1)

            def keep_mix(n, g):
                dve.wait_ge(projected, n)
                dve.wait_ge(mixed, NG * n + g + 1)
                dve.tensor_tensor(mixT[:, g * G:(g + 1) * G, :], work_ps[g % 2][:, :, :], head_bias(bias_v, g), ALU.add
                                  ).then_inc(mix_kept, 1)

            def add(n, link):
                link(dve.tensor_tensor(tile_of(n), tile_of(n), bias_out[:, :], ALU.add))
                dve.wait_ge(projected, n + 1)
                dve.tensor_tensor(tile_of(n), tile_of(n), out_ps[:, 0:D], ALU.add).then_inc(added, 1)

            dve.memset(probsT[:, :, :], 0.0).then_inc(zeroed, 1)
            dve.wait_ge(zeroed, 1)
            dve.wait_ge(loaded, 64)
            link = Chain(dve, dve_chain, 0, passed)
            stats_of(0, link)
            normalize(0)
            for g in range(NG):
                keep_q(0, g)
            stats_of(1, link)
            normalize(1)
            with dve.Fori(0, NT - 1) as i:
                link = Chain(dve, dve_chain, i * LINKS + 2, passed)
                keep_q(i + 1, 0)
                shift(i, link)
                keep_q(i + 1, 1)
                divide(i, link)
                keep_q(i + 1, 2)
                turn_probs(i)
                keep_q(i + 1, 3)
                stats_of(i + 2, link)
                for g in range(NG):
                    keep_mix(i, g)
                normalize(i + 2)
                add(i, link)
                assert link.n == LINKS, link.n
            link = Chain(dve, dve_chain, (NT - 1) * LINKS + 2, passed)
            shift(NT - 1, link)
            divide(NT - 1, link)
            turn_probs(NT - 1)
            for g in range(NG):
                keep_mix(NT - 1, g)
            add(NT - 1, link)

        @block.gpsimd
        def _(pool):
            pool.memset(minus_half[:, :], -0.5).then_inc(half_set, 1)
            pool.wait_ge(half_set, 1)

            def scale_of(n):
                link = Chain(pool, pool_chain, n, passed)
                pool.wait_ge(var_ready, n + 1)
                apart(pool, passed)
                rstd_of(pool, mv, rstd, minus_half, link).then_inc(rstd_ready, 1)

            scale_of(0)
            scale_of(1)
            with pool.Fori(0, NT - 1) as i:
                scale_of(i + 2)


def dense_experts(nc, I, x_sb, ident, out):
    with ExitStack() as ctx:
        sc = Scope(nc, ctx, "ff1")
        GT = 2
        GROUPS = NT // GT
        U = 2
        ITERS = GROUPS // U
        TOP = 2
        W = 8
        STEPS = E1
        FC = F1 // P
        fc1, fc2 = sc.sb("fc1", [P, E1, NC, F1]), sc.sb("fc2", [P, E1, FC, D])
        fc1_b, fc2_b = sc.sb("fc1_b", [P, E1, FC]), sc.sb("fc2_b", [E1, D])
        gate_w, alpha = sc.sb("gate_w", [P, NC, E1]), sc.sb("alpha", [P, E1])
        stats, mv, rstd, minus_half = sc.sb("stats", [P, GT, 6]), sc.sb("mv", [P, GT, 2]), sc.sb("rstd", [P, GT]), sc.sb("minus_half", [P, 1])
        xn, xnT = sc.sb("xn", [P, GT, D]), sc.sb("xnT", [P, U, NC, GT, P])
        prob, top, total = sc.sb("prob", [P, GT, E1]), sc.sb("top", [P, GT]), sc.sb("total", [P, GT])
        best, pair, rest = sc.sb("best", [P, GT, W]), sc.sb("pair", [P, GT, W]), sc.sb("rest", [P, GT, E1])
        weight = sc.sb("weight", [P, U, GT, E1])
        weightT = sc.sb("weightT", [E1, GT, P])
        hidden = sc.sb("hidden", [P, 2, FC, GT * P])
        turn_ps = sc.ps("turn", [P, NC, GT, P])
        route_ps, bias_ps = sc.ps("route"), sc.ps("bias", [P, GT, D])
        mid_ps = [sc.ps(f"mid{b}", [P, FC, GT * P]) for b in range(2)]
        out_ps = [sc.ps(f"out{b}", [P, GT, D]) for b in range(2)]

        loaded, fc1_loaded, fc2_loaded = sc.sem("loaded"), sc.sem("fc1_loaded"), sc.sem("fc2_loaded")
        pair_set, half_set = sc.sem("pair_set"), sc.sem("half_set")
        passed, dve_chain, pool_chain = sc.sem("passed"), sc.sem("dve_chain"), sc.sem("pool_chain")
        var_ready, rstd_ready, normed = sc.sem("var_ready"), sc.sem("rstd_ready"), sc.sem("normed")
        x_turned, xnT_ready, routed, shifted, exped = (sc.sem(n) for n in (
            "x_turned", "xnT_ready", "routed", "shifted", "exped"))
        weighed, weight_turned, weightT_ready, biased, based = (sc.sem(n) for n in (
            "weighed", "weight_turned", "weightT_ready", "biased", "based"))
        mid_made, hidden_ready, out_made, added, stored = (sc.sem(n) for n in (
            "mid_made", "hidden_ready", "out_made", "added", "stored"))
        block = sc.block()
        LOADS = 4

        def tile_of(n):
            return x_sb[:, bass.ds(n, 1), :].rearrange("p a d -> p (a d)")

        @block.sync
        def _(sp):
            with nc.allow_non_contiguous_dma(reason="one bias per partition, small rows"):
                sp.dma_start(gate_w[:, :, :], I["L1_ffn_gate_w"].rearrange("(c p) e -> p c e", p=P)).then_inc(loaded, 16)
                sp.dma_start(fc1_b[:, :, :], I["L1_ffn_fc1_b"].rearrange("e (f p) -> p e f", p=P)).then_inc(loaded, 16)
            sp.dma_start(fc2_b[:, :], I["L1_ffn_fc2_b"]).then_inc(loaded, 16)
            sp.dma_start(alpha[:, :], I["L1_ffn_alpha"].partition_broadcast(P)).then_inc(loaded, 16)
            sp.dma_start(fc1[:, :, :, :], I["L1_ffn_fc1_w"].rearrange("e (c p) f -> p e c f", p=P)).then_inc(fc1_loaded, 16)
            sp.dma_start(fc2[:, :, :, :], I["L1_ffn_fc2_w"].rearrange("e (c p) d -> p e c d", p=P)).then_inc(fc2_loaded, 16)
            result = out.rearrange("(n b) t d -> (b t) n d", b=BT)
            with sp.Fori(0, ITERS) as i:
                for p in range(U):
                    g = i * U + p
                    sp.wait_ge(added, (g + 1) * (STEPS * GT))
                    sp.dma_start(result[:, bass.ds(g * GT, GT), :], x_sb[:, bass.ds(g * GT, GT), :]).then_inc(stored, 16)
            sp.wait_ge(stored, 16 * GROUPS)

        @block.tensor
        def _(pe):
            def turn(g, p):
                pe.wait_ge(normed, (g + 1) * GT)
                pe.wait_ge(xnT_ready, g)
                for c in range(NC):
                    for t in range(GT):
                        ins = pe.transpose(turn_ps[:, c, t, :], xn[:, t, c * P:(c + 1) * P], ident[:, :])
                ins.then_inc(x_turned, 1)

            def route(g, p):
                pe.wait_ge(xnT_ready, g + 1)
                pe.wait_ge(weightT_ready, g)
                for t in range(GT):
                    for c in range(NC):
                        ins = pe.matmul(route_ps[:, t * E1:(t + 1) * E1], xnT[:, p, c, t, :], gate_w[:, c, :],
                                        start=(c == 0), stop=(c == NC - 1))
                ins.then_inc(routed, 1)

            def turn_weights(g, p):
                pe.wait_ge(weighed, g + 1)
                for t in range(GT):
                    ins = pe.transpose(route_ps[0:E1, 256 + t * P:256 + (t + 1) * P], weight[:, p, t, :], ident[:, :])
                ins.then_inc(weight_turned, 1)

            def bias(g, p):
                pe.wait_ge(weightT_ready, g + 1)
                pe.wait_ge(based, g * GT)
                for t in range(GT):
                    ins = pe.matmul(bias_ps[:, t, :], weightT[:, t, :], fc2_b[:, :], start=True, stop=True)
                ins.then_inc(biased, 1)

            prepare = {2: turn, 4: route, 6: turn_weights, 7: bias}

            def first(k, e, p):
                pe.wait_ge(hidden_ready, k if isinstance(k, int) else k - 1)
                for f in range(FC):
                    for c in range(NC):
                        ins = pe.matmul(mid_ps[k_parity(e)][:, f, :], fc1[:, e, c, f * P:(f + 1) * P],
                                        xnT[:, p, c, :, :], start=(c == 0), stop=(c == NC - 1))
                ins.then_inc(mid_made, 1)

            def second(k, e):
                pe.wait_ge(hidden_ready, k + 1)
                pe.wait_ge(added, k * GT - GT if e else k * GT)
                for t in range(GT):
                    for f in range(FC):
                        ins = pe.matmul(out_ps[e % 2][:, t, :], hidden[:, e % 2, f, t * P:(t + 1) * P], fc2[:, e, f, :],
                                        start=(f == 0), stop=(f == FC - 1))
                ins.then_inc(out_made, 1)

            def k_parity(e):
                return e % 2

            pe.wait_ge(loaded, 16 * LOADS)
            for stage in prepare.values():
                stage(0, 0)
            pe.wait_ge(fc1_loaded, 16)
            first(0, 0, 0)
            pe.wait_ge(fc2_loaded, 16)
            with pe.Fori(0, ITERS) as i:
                for p in range(U):
                    g = i * U + p
                    for e in range(STEPS):
                        k = g * STEPS + e
                        if e + 1 < STEPS:
                            first(k + 1, e + 1, p)
                        else:
                            pe.wait_ge(xnT_ready, g + 2)
                            first(k + 1, 0, 1 - p)
                        if e in prepare:
                            prepare[e](g + 1, 1 - p)
                        second(k, e)

        @block.scalar
        def _(act):
            def keep_xnT(g, p):
                act.wait_ge(x_turned, g + 1)
                act.activation(xnT[:, p, :, :, :], turn_ps[:, :, :, :], ACT.Copy).then_inc(xnT_ready, 1)

            def exp(g, p):
                act.wait_ge(shifted, g + 1)
                act.activation(prob[:, :, :], prob[:, :, :], ACT.Exp).then_inc(exped, 1)

            def keep_weights(g, p):
                act.wait_ge(weight_turned, g + 1)
                act.wait_ge(biased, g)
                act.activation(weightT[:, :, :], route_ps[0:E1, 256:512].rearrange("e (t n) -> e t n", t=GT), ACT.Copy
                               ).then_inc(weightT_ready, 1)

            prepare = {2: keep_xnT, 5: exp, 6: keep_weights}

            def gelu(k, e):
                act.wait_ge(out_made, k - 1 if e else k)
                act.wait_ge(mid_made, k + 1)
                for f in range(FC):
                    ins = act.activation(hidden[:, e % 2, f, :], mid_ps[e % 2][:, f, :], ACT.Gelu, bias=fc1_b[:, e, f:f + 1])
                ins.then_inc(hidden_ready, 1)

            act.wait_ge(loaded, 16 * LOADS)
            for stage in prepare.values():
                stage(0, 0)
            with act.Fori(0, ITERS) as i:
                for p in range(U):
                    g = i * U + p
                    for e in range(STEPS):
                        gelu(g * STEPS + e, e)
                        if e in prepare:
                            prepare[e](g + 1, 1 - p)

        @block.vector
        def _(dve):
            LINKS = 13

            def stats_of(g, p, link):
                for t in range(GT):
                    link(dve.bn_stats(stats[:, t, :], tile_of(g * GT + t)), alone=True)
                    dve.bn_aggr(mv[:, t, :], stats[:, t, :]).then_inc(var_ready, 1)

            def normalize(g, p, link):
                dve.wait_ge(x_turned, g)
                for t in range(GT):
                    dve.wait_ge(rstd_ready, g + 1)
                    dve.tensor_scalar(xn[:, t, :], tile_of(g * GT + t), mv[:, t, 0:1], rstd[:, t:t + 1],
                                      ALU.subtract, ALU.mult).then_inc(normed, 1)

            def per_tile(x, n):
                return x.unsqueeze(2).broadcast_to([P, GT, n])

            def shift(g, p, link):
                dve.wait_ge(routed, g + 1)
                logits = route_ps[:, 0:GT * E1].rearrange("q (t e) -> q t e", t=GT)
                link(dve.tensor_reduce(top[:, :], logits, AX_X, ALU.max))
                dve.tensor_tensor(prob[:, :, :], logits, per_tile(top[:, :], E1), ALU.subtract).then_inc(shifted, 1)

            def weigh(g, p, link):
                dve.wait_ge(exped, g + 1)
                link(dve.tensor_reduce(total[:, :], prob[:, :, :], AX_X, ALU.add))
                link(dve.reciprocal(total[:, :], total[:, :]))
                link(dve.tensor_tensor(prob[:, :, :], prob[:, :, :], per_tile(total[:, :], E1), ALU.mult), alone=True)
                dve.max(best[:, 0, :], prob[:, 0, :])
                link(dve.max(best[:, 1, :], prob[:, 1, :]))
                link(dve.tensor_copy(pair[:, :, 0:TOP], best[:, :, 0:TOP]), alone=True)
                for t in range(GT):
                    ins = dve.match_replace(rest[:, t, :], pair[:, t, :], prob[:, t, :], -1.0)
                link(ins)
                link(dve.tensor_tensor(rest[:, :, :], rest[:, :, :], prob[:, :, :], ALU.not_equal))
                dve.tensor_reduce(total[:, :], pair[:, :, 0:TOP], AX_X, ALU.add)
                link(dve.tensor_tensor(rest[:, :, :], rest[:, :, :], prob[:, :, :], ALU.mult))
                link(dve.reciprocal(total[:, :], total[:, :]))
                link(dve.tensor_tensor(rest[:, :, :], rest[:, :, :], per_tile(total[:, :], E1), ALU.mult))
                dve.tensor_tensor(weight[:, p, :, :], rest[:, :, :], alpha[:, :].unsqueeze(1).broadcast_to([P, GT, E1]), ALU.mult
                                  ).then_inc(weighed, 1)

            prepare = {0: stats_of, 1: normalize, 4: shift, 5: weigh}

            def add_bias(g):
                dve.wait_ge(biased, g + 1)
                for t in range(GT):
                    dve.tensor_tensor(tile_of(g * GT + t), tile_of(g * GT + t), bias_ps[:, t, :], ALU.add).then_inc(based, 1)

            def add(g, p, e):
                k = g * STEPS + e
                dve.wait_ge(out_made, k + 1)
                for t in range(GT):
                    if e:
                        dve.wait_ge(added, k * GT + t - 1)
                    else:
                        dve.wait_ge(based, g * GT + t + 1)
                    dve.scalar_tensor_tensor(out=tile_of(g * GT + t), in0=out_ps[e % 2][:, t, :], scalar=weight[:, p, t, e:e + 1],
                                             in1=tile_of(g * GT + t), op0=ALU.mult, op1=ALU.add).then_inc(added, 1)

            dve.memset(pair[:, :, :], -2.0).then_inc(pair_set, 1)
            dve.wait_ge(pair_set, 1)
            dve.wait_ge(loaded, 16 * LOADS)
            link = Chain(dve, dve_chain, 0, passed)
            for stage in prepare.values():
                stage(0, 0, link)
            assert link.n == LINKS, link.n
            with dve.Fori(0, ITERS) as i:
                for p in range(U):
                    g = i * U + p
                    link = Chain(dve, dve_chain, (g + 1) * LINKS, passed)
                    add_bias(g)
                    for e in range(STEPS):
                        if e in prepare:
                            prepare[e](g + 1, 1 - p, link)
                        add(g, p, e)

        @block.gpsimd
        def _(pool):
            pool.memset(minus_half[:, :], -0.5).then_inc(half_set, 1)
            pool.wait_ge(half_set, 1)

            def scale_of(g):
                link = Chain(pool, pool_chain, g, passed)
                pool.wait_ge(var_ready, (g + 1) * GT)
                apart(pool, passed)
                link(pool.tensor_scalar(rstd[:, :], mv[:, :, 1], LN_EPS, None, ALU.add))
                pool.tensor_tensor(rstd[:, :], rstd[:, :], minus_half[:, :].broadcast_to([P, GT]), ALU.pow).then_inc(rstd_ready, 1)

            scale_of(0)
            with pool.Fori(0, GROUPS) as g:
                scale_of(g + 1)


def build(nc, I, out):
    with ExitStack() as ctx:
        sc = Scope(nc, ctx, "all")
        x_sb, ident = sc.sb("x", [P, NT + 2, D]), sc.sb("ident", [P, P])
        load_inputs(nc, I, x_sb, ident)
        with ExitStack() as cross:
            sc = Scope(nc, cross, "cross")
            rk_dram = nc.dram_tensor("rk", (H * RK_COPIES, RK_AHEAD + KEYS), F32).ap()
            folded_dram = nc.dram_tensor("folded1", (P, H, FOLDED), F32).ap()
            ctxT, folded = sc.sb("ctxT", [P, KEYS]), sc.sb("folded", [P, H, FOLDED])
            fold_weights(nc, I, ident, folded, folded_dram)
            context_pass(nc, I, ident, ctxT, rk_dram)
            cross_attention(nc, I, 0, x_sb, ident, ctxT, folded, folded_dram, rk_dram)
            self_attention(nc, I, x_sb, ident)
            routed_experts(nc, I, x_sb, ident)
            cross_attention(nc, I, 1, x_sb, ident, ctxT, folded, folded_dram, rk_dram)
        self_attention_fp4(nc, I, x_sb, ident)
        dense_experts(nc, I, x_sb, ident, out)


OUT_SHAPE = (B, T, D)
NAMES = (
    ["x", "ctx_1024", "mask_BxS2_bf1"]
    + [f"L0_xattn_{n}" for n in ("Wq", "Wk", "Wv", "Wo")]
    + [f"L0_attn_{n}" for n in ("Wqkv_w", "Wqkv_b", "out_w", "out_b")]
    + [f"L0_ffn_{n}" for n in ("router_w", "w_gate", "w_up", "w_down")]
    + [f"L1_xattn_{n}" for n in ("Wq", "Wk", "Wv", "Wo", "gq", "gk")]
    + [f"L1_attn_{w}_{n}" for w in ("wq", "wk", "wv", "wo") for n in ("codes", "scales")]
    + [f"L1_attn_{n}" for n in ("bq", "bk", "bv", "bo")]
    + [f"L1_ffn_{n}" for n in ("gate_w", "fc1_w", "fc1_b", "fc2_w", "fc2_b", "alpha")]
)


def kernel(**inputs):
    import numpy as _np
    import concourse.bacc as _bacc
    from concourse import mybir as _mybir
    from concourse.bass_utils import run_bass_kernel_spmd as _run

    nc = _bacc.Bacc("TRN2", target_bir_lowering=False, num_devices=1)
    arrays, args = {}, {}
    for name in NAMES:
        a = _np.ascontiguousarray(inputs[name])
        if a.dtype == _np.bool_:
            a = a.view(_np.uint8)
        arrays[f"in_{name}_dram"] = a
        args[name] = nc.dram_tensor(f"in_{name}_dram", a.shape, _mybir.dt.from_np(a.dtype), kind="ExternalInput").ap()
    out = nc.dram_tensor("out_0_dram", OUT_SHAPE, F32, kind="ExternalOutput").ap()
    build(nc, args, out)
    r = _run(nc, [arrays], core_ids=[0])
    return r.results[0]["out_0_dram"]
```

```python
from contextlib import ExitStack

import concourse.bass as bass
from concourse import mybir

ALU = mybir.AluOpType
ACT = mybir.ActivationFunctionType
F32 = mybir.dt.float32
U32 = mybir.dt.uint32
AX_X = mybir.AxisListType.X

P = 128
B, T, D = 64, 32, 256
S2, DC = 257, 128
H, HD = 16, 128
KVH = 8
AH, AD = 16, 16
E0, K0, F0, CAP = 64, 8, 96, 64
FP4_ROWS = 32
E1, F1 = 8, 256
NC = D // P
NT = B * T // P
BT = P // T
KEYS = B * S2
LN_EPS = 1e-5
SCALE = float(HD) ** -0.5
SLOTS = E0 * CAP
FOLDED = NC * P + D
GROUP = 512
REST = KEYS % GROUP
RK_AHEAD = GROUP
RK_COPIES = 4
NOWHERE = SLOTS


class Chain:

    def __init__(self, eng, sem, base=0, passed=None):
        self.eng, self.sem, self.base, self.passed, self.n = eng, sem, base, passed, 0

    def __call__(self, ins, alone=False):
        self.n += 1
        ins.then_inc(self.sem, 1)
        self.eng.wait_ge(self.sem, self.base + self.n)
        if alone:
            apart(self.eng, self.passed)


def apart(eng, passed):
    eng.sem_inc(passed, 1)


class Scope:

    def __init__(self, nc, ctx, name):
        self.nc, self.ctx, self.name, self.sems = nc, ctx, name, []

    def sb(self, name, shape, dt=F32):
        return self.ctx.enter_context(self.nc.sbuf_tensor(f"{self.name}_{name}", shape, dt))

    def ps(self, name, shape=(P, 512), dt=F32):
        return self.ctx.enter_context(self.nc.psum_tensor(f"{self.name}_{name}_ps", list(shape), dt))

    def sem(self, name):
        handle = self.ctx.enter_context(self.nc.semaphore(f"{self.name}_{name}"))
        self.sems.append(handle)
        return handle

    def pool_dma_sem(self, name):
        self.sems.append(self.nc.alloc_semaphore(name=f"{self.name}_{name}"))
        return self.sems[-1]

    def block(self):
        with self.nc.Block() as block:
            @block.sync
            def _(sp):
                for handle in self.sems:
                    sp.sem_clear(handle)
        return self.ctx.enter_context(self.nc.Block())


def load_inputs(nc, I, x_sb, ident):
    with ExitStack() as ctx:
        sc = Scope(nc, ctx, "in")
        x_loaded, padded, zeroed, made = sc.sem("x_loaded"), sc.sem("padded"), sc.sem("zeroed"), sc.sem("made")
        block = sc.block()

        @block.sync
        def _(sp):
            sp.dma_start(x_sb[:, 0:NT, :], I["x"].rearrange("(n b) t d -> (b t) n d", b=BT)).then_inc(x_loaded, 16)
            sp.wait_ge(x_loaded, 16)

        @block.vector
        def _(dve):
            dve.memset(x_sb[:, NT:, :], 0.0).then_inc(padded, 1)
            dve.wait_ge(padded, 1)

        @block.gpsimd
        def _(pool):
            pool.memset(ident[:, :], 0.0).then_inc(zeroed, 1)
            pool.wait_ge(zeroed, 1)
            pool.affine_select(out=ident[:, :], in_=ident[:, :], compare_op=ALU.not_equal, fill=1.0, base=0,
                               pattern=[[-1, P]], channel_multiplier=1).then_inc(made, 1)


def fold_weights(nc, I, ident, folded, folded_dram, ctxT):
    with ExitStack() as ctx:
        sc = Scope(nc, ctx, "fold")
        UNITS, SLOT = KVH, 2
        wq = [sc.sb(f"wq{l}", [P, SLOT, NC, 2 * HD]) for l in range(2)]
        wk = [sc.sb(f"wk{l}", [P, SLOT, (l + 1) * HD]) for l in range(2)]
        wv = [sc.sb(f"wv{l}", [P, SLOT, (l + 1) * HD]) for l in range(2)]
        wo = [sc.sb(f"wo{l}", [P, SLOT, 2, D]) for l in range(2)]
        wT = sc.sb("wT", [P, 2, 4 * P])
        stage = sc.sb("stage", [P, 2, FOLDED])
        rows = sc.sb("rows", [P, 4 * SLOT, GROUP // P, DC])
        gains = sc.sb("gains", [P, 2])
        gain = sc.sb("gain", [P, 1])
        turned_ps = [sc.ps(f"turned{n}") for n in range(2)]
        prod_ps = [sc.ps(f"prod{n}") for n in range(2)]
        ctx_ps = [sc.ps(f"ctx{n}") for n in range(2)]
        ctx_turned, ctx_kept = sc.sem("ctx_turned"), sc.sem("ctx_kept")
        rows_loaded = [sc.sem(f"rows_loaded{k}") for k in range(4 * SLOT)]
        loaded = [sc.sem(f"loaded{p}") for p in range(SLOT)]
        gains_loaded, gain_ready = sc.sem("gains_loaded"), sc.sem("gain_ready")
        passed_dve = sc.sem("passed_dve")
        passed, stored = sc.sem("passed"), [sc.pool_dma_sem(f"stored{j}") for j in range(2)]
        turned, wT_ready, multiplied, kept = sc.sem("turned"), sc.sem("wT_ready"), sc.sem("multiplied"), sc.sem("kept")
        block = sc.block()
        DMAS = 8
        ITERS = UNITS // SLOT
        STEPS = 4 * SLOT

        def step(k):
            return k // 4, (k % 4) // 2, k % 2

        names = ["L0_xattn_", "L1_xattn_"]
        assert ITERS * STEPS * GROUP + REST == KEYS and 0 < REST <= P
        ctx_rows = I["ctx_1024"].rearrange("b s d -> (b s) d")

        @block.sync
        def _(sp):
            sp.dma_start(gains[:, 0:1], I["L1_xattn_gq"].rearrange("(d a) -> d a", a=1)).then_inc(gains_loaded, 16)
            sp.dma_start(gains[:, 1:2], I["L1_xattn_gk"].rearrange("(d a) -> d a", a=1)).then_inc(gains_loaded, 16)
            with sp.Fori(0, ITERS) as i:
                for p in range(SLOT):
                    u = i * SLOT + p
                    sp.wait_ge(multiplied, i * STEPS)
                    for l in range(2):
                        n, w = names[l], (l + 1) * HD
                        sp.dma_start(wq[l][:, p], I[n + "Wq"].rearrange("(c p) n -> p c n", p=P)[
                            :, :, bass.ds(u * (2 * HD), 2 * HD)]).then_inc(loaded[p], 16)
                        sp.dma_start(wk[l][:, p], I[n + "Wk"][:, bass.ds(u * w, w)]).then_inc(loaded[p], 16)
                        sp.dma_start(wv[l][:, p], I[n + "Wv"][:, bass.ds(u * w, w)]).then_inc(loaded[p], 16)
                        sp.dma_start(wo[l][:, p], I[n + "Wo"].rearrange("(h d) n -> d h n", d=HD)[
                            :, bass.ds(u * 2, 2), :]).then_inc(loaded[p], 16)
                    for k in range(4 * p, 4 * p + 4):
                        sp.wait_ge(ctx_turned, i * STEPS + k + 1)
                        sp.dma_start(rows[:, k], ctx_rows[bass.ds((i * STEPS + k) * GROUP, GROUP), :].rearrange(
                            "(c p) d -> p c d", p=P)).then_inc(rows_loaded[k], 16)
            sp.wait_ge(ctx_turned, ITERS * STEPS + 1)
            sp.dma_start(rows[0:REST, 0, 0, :], ctx_rows[KEYS - REST:KEYS, :]).then_inc(rows_loaded[0], 16)

        @block.tensor
        def _(pe):
            def turn(i, k):
                p, l, j = step(k)
                kv = j * HD if l else 0
                if k % 4 == 0:
                    pe.wait_ge(loaded[p], i * (16 * DMAS) + 16 * DMAS)
                pe.wait_ge(wT_ready, i * STEPS + max(k - 1, 0))
                ps = turned_ps[k % 2]
                for c in range(NC):
                    pe.transpose(ps[:, c * P:(c + 1) * P], wq[l][:, p, c, j * HD:(j + 1) * HD], ident[:, :])
                pe.transpose(ps[:, 2 * P:3 * P], wk[l][:, p, kv:kv + HD], ident[:, :])
                pe.transpose(ps[:, 3 * P:4 * P], wv[l][:, p, kv:kv + HD], ident[:, :]).then_inc(turned, 1)

            def product(i, k):
                p, l, j = step(k)
                pe.wait_ge(wT_ready, i * STEPS + k + 1)
                pe.wait_ge(kept, i * STEPS + max(k - 1, 0))
                w, ps = wT[:, k % 2], prod_ps[k % 2]
                for c in range(NC):
                    pe.matmul(ps[:, c * P:(c + 1) * P], w[:, c * P:(c + 1) * P], w[:, 2 * P:3 * P], start=True, stop=True)
                pe.matmul(ps[:, 2 * P:2 * P + D], w[:, 3 * P:4 * P], wo[l][:, p, j, :],
                          start=True, stop=True).then_inc(multiplied, 1)

            def turn_ctx(i, k):
                pe.wait_ge(rows_loaded[k], i * 16 + 16)
                pe.wait_ge(ctx_kept, i * STEPS + max(k - 1, 0))
                for c in range(GROUP // P):
                    ins = pe.transpose(ctx_ps[k % 2][:, c * P:(c + 1) * P], rows[:, k, c, :], ident[:, :])
                ins.then_inc(ctx_turned, 1)

            pe.sem_inc(ctx_turned, STEPS)
            with pe.Fori(0, ITERS) as i:
                turn(i, 0)
                for k in range(STEPS):
                    if k + 1 < STEPS:
                        turn(i, k + 1)
                    product(i, k)
                    turn_ctx(i, k)
            pe.wait_ge(rows_loaded[0], ITERS * 16 + 16)
            pe.wait_ge(ctx_kept, ITERS * STEPS)
            pe.transpose(ctx_ps[0][:, 0:REST], rows[0:REST, 0, 0, :], ident[0:REST, 0:REST]).then_inc(ctx_turned, 1)

        @block.vector
        def _(dve):
            dve.wait_ge(gains_loaded, 32)
            dve.tensor_tensor(gain[:, :], gains[:, 0:1], gains[:, 1:2], ALU.mult).then_inc(gain_ready, 1)
            dve.wait_ge(gain_ready, 1)

            def keep_ctx(i, k):
                dve.wait_ge(ctx_turned, i * STEPS + STEPS + k + 1)
                apart(dve, passed_dve)
                dve.tensor_copy(ctxT[:, bass.ds((i * STEPS + k) * GROUP, GROUP)], ctx_ps[k % 2][:, :]).then_inc(ctx_kept, 1)

            with dve.Fori(0, ITERS) as i:
                for k in range(STEPS):
                    _, l, _ = step(k)
                    dve.wait_ge(multiplied, i * STEPS + max(k - 1, 0))
                    dve.wait_ge(turned, i * STEPS + k + 1)
                    w, ps = wT[:, k % 2], turned_ps[k % 2]
                    dve.tensor_scalar(w[:, 0:2 * P], ps[:, 0:2 * P], gain[:, 0:1] if l else -SCALE,
                                      None, ALU.mult)
                    dve.tensor_copy(w[:, 2 * P:4 * P], ps[:, 2 * P:4 * P]).then_inc(wT_ready, 1)
                    if k:
                        keep_ctx(i, k - 1)
                keep_ctx(i, STEPS - 1)
            dve.wait_ge(ctx_turned, (ITERS + 1) * STEPS + 1)
            dve.tensor_copy(ctxT[:, KEYS - REST:KEYS], ctx_ps[0][:, 0:REST]).then_inc(ctx_kept, 1)

        @block.scalar
        def _(act):
            with act.Fori(0, ITERS) as i:
                for k in range(STEPS):
                    p, l, j = step(k)
                    h = i * (2 * SLOT) + (2 * p + j)
                    act.wait_ge(multiplied, i * STEPS + k + 1)
                    if l:
                        act.wait_ge(stored[j], i * (16 * SLOT) + 16 * p)
                        to = stage[:, j, :]
                    else:
                        to = folded[:, bass.ds(h, 1), :].rearrange("p a n -> p (a n)")
                    act.activation(to, prod_ps[k % 2][:, 0:FOLDED], ACT.Copy).then_inc(kept, 1)

        @block.gpsimd
        def _(pool):
            with pool.Fori(0, ITERS) as i:
                for k in range(STEPS):
                    p, l, j = step(k)
                    if l:
                        pool.wait_ge(kept, i * STEPS + k + 1)
                        apart(pool, passed)
                        pool.dma_start(folded_dram[:, bass.ds(i * (2 * SLOT) + (2 * p + j), 1), :],
                                       stage[:, j, :]).then_inc(stored[j], 16)
            for j in range(2):
                pool.wait_ge(stored[j], 16 * UNITS)


class KeyNorms:

    U = GROUP // P
    NQ = H * HD // 512
    HQ = H // NQ
    PER = U * NQ
    SQ = 4

    def __init__(self, sc, I, ident, ctxT, sums, rk_dram, first):
        U, NQ = self.U, self.NQ
        self.I, self.ident, self.ctxT, self.sums, self.rk_dram = I, ident, ctxT, sums, rk_dram
        self.first = first
        self.wk, self.stage = sc.sb("kn_wk", [P, H * HD]), sc.sb("kn_stage", [P, 2, GROUP])
        self.squares = sc.sb("kn_squares", [P, self.SQ, 512])
        self.root, self.rk = sc.sb("kn_root", [P, U, H]), sc.sb("kn_rk", [P, U, H])
        self.rkT, self.eps = sc.sb("kn_rkT", [H, 1, GROUP]), sc.sb("kn_eps", [P, 1])
        self.key_ps = [sc.ps(f"kn_key{n}") for n in range(NQ)]
        self.rk_ps = sc.ps("kn_rk")
        self.wk_loaded, self.eps_set, self.staged = sc.sem("kn_wk_loaded"), sc.sem("kn_eps_set"), sc.sem("kn_staged")
        self.keyed, self.squared, self.summed = (sc.sem("kn_" + n) for n in ("keyed", "squared", "summed"))
        self.rooted, self.rk_ready, self.rk_turned, self.rk_kept, self.rk_stored = (sc.sem("kn_" + n) for n in (
            "rooted", "rk_ready", "rk_turned", "rk_kept", "rk_stored"))
        self.passed = sc.sem("kn_passed")

    def load(self, sp):
        sp.dma_start(self.wk[:, :], self.I["L1_xattn_Wk"]).then_inc(self.wk_loaded, 16)

    def store(self, sp, j, n=GROUP):
        sp.wait_ge(self.rk_kept, j + 1)
        to = self.rk_dram.rearrange("(h c) n -> h c n", c=RK_COPIES)
        sp.dma_start(to[:, :, bass.ds((j + self.first) * GROUP, n)],
                     self.rkT[:, :, 0:n].broadcast_to([H, RK_COPIES, n])).then_inc(self.rk_stored, 16)

    def put(self, pool, j, slot, n=GROUP):
        pool.wait_ge(self.keyed, j * self.PER)
        apart(pool, self.passed)
        pool.tensor_copy(self.stage[:, slot, 0:n], self.ctxT[:, bass.ds((j + self.first) * GROUP, n)]).then_inc(self.staged, 1)

    def begin_pe(self, pe):
        pe.sem_inc(self.keyed, self.PER)
        pe.wait_ge(self.wk_loaded, 16)

    def keys(self, pe, j, slot, u, n=P):
        if u == 0:
            pe.wait_ge(self.staged, j + 1)
        for q in range(self.NQ):
            pe.wait_ge(self.squared, j * self.PER + (u * self.NQ + q + 1))
            pe.matmul(self.key_ps[q][0:n, :], self.stage[:, slot, u * P:u * P + n], self.wk[:, q * 512:(q + 1) * 512],
                      start=True, stop=True).then_inc(self.keyed, 1)

    def turn(self, pe, j):
        pe.wait_ge(self.rk_ready, j + 1)
        pe.wait_ge(self.rk_kept, j)
        for u in range(self.U):
            ins = pe.transpose(self.rk_ps[0:H, u * P:(u + 1) * P], self.rk[:, u, :], self.ident[:, :])
        ins.then_inc(self.rk_turned, 1)

    def begin_act(self, act):
        act.sem_inc(self.squared, self.NQ)
        act.wait_ge(self.eps_set, 1)

    def square(self, act, j, u, n=P):
        for q in range(self.NQ):
            k = u * self.NQ + q
            act.wait_ge(self.summed, j * self.PER + (k + 1))
            act.wait_ge(self.keyed, j * self.PER + (self.PER + k + 1))
            act.activation(self.squares[0:n, q % self.SQ, :], self.key_ps[q][0:n, :], ACT.Square).then_inc(self.squared, 1)

    def take_root(self, act, j, slot, missing=0):
        act.wait_ge(self.rk_ready, j)
        act.wait_ge(self.summed, j * self.PER + (self.SQ - missing))
        act.activation(self.root[:, :, :], self.sums[:, 1 - slot, :, :], ACT.Sqrt, bias=self.eps[:, 0:1],
                       scale=1.0 / HD).then_inc(self.rooted, 1)

    def begin_dve(self, dve):
        dve.sem_inc(self.summed, self.SQ)
        dve.memset(self.eps[:, :], LN_EPS).then_inc(self.eps_set, 1)

    def sum(self, dve, j, slot, u, n=P):
        dve.wait_ge(self.rooted, j)
        for q in range(self.NQ):
            dve.wait_ge(self.squared, j * self.PER + (self.NQ + u * self.NQ + q + 1))
            dve.tensor_reduce(self.sums[0:n, slot, u, q * self.HQ:(q + 1) * self.HQ],
                              self.squares[0:n, q % self.SQ, :].rearrange("p (h d) -> p h d", h=self.HQ), AX_X, ALU.add
                              ).then_inc(self.summed, 1)

    def invert(self, dve, j):
        dve.wait_ge(self.rk_turned, j)
        dve.wait_ge(self.rooted, j + 1)
        dve.reciprocal(self.rk[:, :, :], self.root[:, :, :]).then_inc(self.rk_ready, 1)

    def keep(self, dve, j):
        dve.wait_ge(self.rk_stored, j * 16)
        dve.wait_ge(self.rk_turned, j + 1)
        dve.tensor_copy(self.rkT[:, 0, :], self.rk_ps[0:H, :]).then_inc(self.rk_kept, 1)


def cross_attention(nc, I, layer, x_sb, ident, ctxT, folded, folded_dram, rk_dram):
    with ExitStack() as ctx:
        sc = Scope(nc, ctx, f"xa{layer}")
        G = 2
        NB = G * BT
        R = H * T // P
        HR = H // R
        ST = NB * R
        ITERS = NT // G
        N = G * P
        HP = H // 2
        RING = 4
        SR = 8
        EARLY = 2
        AHEAD = 4
        KB = S2 // P
        assert S2 == KB * P + 1 and KB < R and AHEAD == R and ST % SR == 0
        NQ = H * HD // 512

        stats, mv = sc.sb("stats", [P, G, 6]), sc.sb("mv", [P, G, 2])
        rstd, minus_half = sc.sb("rstd", [P, G]), sc.sb("minus_half", [P, G * H])
        xn, xnT = sc.sb("xn", [P, G, D]), sc.sb("xnT", [P, NC, N])
        qT = sc.sb("qT", [P, NB, H, T])
        keys, last_key = sc.sb("keys", [P, RING, KB, DC]), sc.sb("last_key", [P, RING, DC])
        probs = sc.sb("probs", [P, SR, S2])
        top = sc.sb("top", [P, 8])
        total, share = sc.sb("total", [P, 8]), sc.sb("share", [P, 8])
        probsT = sc.sb("probsT", [P, 2, KB, H * T])
        mixT = sc.sb("mixT", [P, H, N])
        last_ctx = sc.sb("last_ctx", [P, B])
        if layer == 0:
            mask = sc.sb("mask", [P, B, S2], mybir.dt.uint8)
            any_key = sc.sb("any_key", [P, B])
            valid, bias = sc.sb("valid", [P, S2]), sc.sb("bias", [P, 2, S2])
        else:
            wq = sc.sb("wq", [P, NC, H * HD])
            squares = sc.sb("squares", [P, 2, 512])
            q_sum, q_rms = sc.sb("q_sum", [P, G, H]), sc.sb("q_rms", [P, G, H])
            row_scale = sc.sb("row_scale", [P, G, BT, R])
            key_scale = sc.sb("key_scale", [P, 2, R, S2])
            shift = sc.sb("shift", [P, 8])
        misc_ps = [sc.ps(f"misc{n}") for n in range(2)]
        score_ps = [sc.ps(f"score{n}") for n in range(2)]
        probsT_ps = [sc.ps(f"probsT{n}") for n in range(2)]
        mix_ps = [sc.ps(f"mix{n}") for n in range(2)]

        begun, pre_loaded, any_ready, last_ready = sc.sem("begun"), sc.sem("pre_loaded"), sc.sem("any_ready"), sc.sem("last_ready")
        passed, act_passed, pool_passed = sc.sem("passed"), sc.sem("act_passed"), sc.sem("pool_passed")
        keys_loaded = [sc.sem(f"keys_loaded{n}") for n in range(RING)]
        kscale_loaded = [sc.sem(f"kscale_loaded{n}") for n in range(2)]
        keys_ready = sc.sem("keys_ready")
        dve_chain, pool_chain = sc.sem("dve_chain"), sc.sem("pool_chain")
        var_ready, rstd_ready, normed = sc.sem("var_ready"), sc.sem("rstd_ready"), sc.sem("normed")
        x_turned, xnT_ready = sc.sem("x_turned"), sc.sem("xnT_ready")
        q_made, q_kept_act, q_kept_dve = sc.sem("q_made"), sc.sem("q_kept_act"), sc.sem("q_kept_dve")
        n_made, n_squared, n_summed, rows_ready = sc.sem("n_made"), sc.sem("n_squared"), sc.sem("n_summed"), sc.sem("rows_ready")
        bias_ready = sc.sem("bias_ready")
        scored, exped = sc.sem("scored"), sc.sem("exped")
        shifted = sc.sem("shifted")
        probs_ready, turned, turned_kept = sc.sem("probs_ready"), sc.sem("turned"), sc.sem("turned_kept")
        mixed = sc.sem("mixed")
        mix_kept, projected, added = sc.sem("mix_kept"), sc.sem("projected"), sc.sem("added")
        block = sc.block()
        ctx_in = I["ctx_1024"]

        @block.sync
        def _(sp):
            if layer == 0:
                sp.dma_start(mask[:, :, :], I["mask_BxS2_bf1"].partition_broadcast(P)).then_inc(pre_loaded, 16)
            else:
                sp.dma_start(wq[:, :, :], I["L1_xattn_Wq"].rearrange("(c p) n -> p c n", p=P)).then_inc(pre_loaded, 16)
                sp.dma_start(folded[:, :, :], folded_dram).then_inc(pre_loaded, 16)
            with sp.Fori(0, ITERS) as i:
                for b in range(NB):
                    item = i * NB + b
                    sp.wait_ge(mixed, item + 1)
                    sp.dma_start(keys[:, b % RING], ctx_in[bass.ds(item, 1), 0:KB * P, :].rearrange(
                        "a (k p) d -> p (a k) d", p=P)).then_inc(keys_loaded[b % RING], 16)
                    sp.dma_start(last_key[:, b % RING, :], ctx_in[bass.ds(item, 1), KB * P, :].broadcast_to([P, DC])
                                 ).then_inc(keys_loaded[b % RING], 16)
                    if layer == 1:
                        sp.wait_ge(shifted, item * R)
                        for r in range(R):
                            src = rk_dram[r * HR * RK_COPIES:(r + 1) * HR * RK_COPIES,
                                          bass.ds(item * S2 + RK_AHEAD, S2)]
                            sp.dma_start(key_scale[:, b % 2, r, :], src.unsqueeze(1).broadcast_to(
                                [HR * RK_COPIES, T // RK_COPIES, S2])).then_inc(kscale_loaded[b % 2], 16)

        @block.tensor
        def _(pe):
            def turn_x(g):
                pe.wait_ge(normed, g * G + G)
                if not isinstance(g, int) or g > 0:
                    pe.wait_ge(added, (g - 1) * G)
                for t in range(G):
                    for c in range(NC):
                        ins = pe.transpose(misc_ps[0][:, c * N + t * P:c * N + (t + 1) * P],
                                           xn[:, t, c * P:(c + 1) * P], ident[:, :])
                ins.then_inc(x_turned, 1)

            def query_norms(g):
                for m in range(G * NQ):
                    pe.wait_ge(n_squared, g * (G * NQ) + max(m - 1, 0))
                    for c in range(NC):
                        ins = pe.matmul(misc_ps[m % 2][:, :], xnT[:, c, (m // NQ) * P:(m // NQ + 1) * P],
                                        wq[:, c, (m % NQ) * 512:(m % NQ + 1) * 512], start=(c == 0), stop=(c == NC - 1))
                    ins.then_inc(n_made, 1)
                pe.wait_ge(n_squared, g * (G * NQ) + G * NQ)

            def queries(g, hp):
                if hp >= 2:
                    pe.wait_ge(q_kept_dve if hp % 2 else q_kept_act, g * (HP // 2) + hp // 2)
                for j in range(2):
                    for c in range(NC):
                        ins = pe.matmul(misc_ps[hp % 2][:, j * N:(j + 1) * N], folded[:, 2 * hp + j, c * P:(c + 1) * P],
                                        xnT[:, c, :], start=(c == 0), stop=(c == NC - 1))
                ins.then_inc(q_made, 1)

            def score(i, s):
                b, r = s // R, s % R
                pe.wait_ge(shifted, i * ST + (s - 1 + R))
                pe.matmul(score_ps[s % 2][:, 0:S2], qT[:, b, r * HR:(r + 1) * HR, :].rearrange("p h t -> p (h t)"),
                          ctxT[:, bass.ds((i * NB + b) * S2, S2)], start=True, stop=True).then_inc(scored, 1)

            def turn(i, s):
                pe.wait_ge(probs_ready, i * ST + s + 1)
                pe.wait_ge(turned_kept, i * ST + max(s - 1, 0))
                for k in range(KB):
                    ins = pe.transpose(probsT_ps[s % 2][:, k * P:(k + 1) * P], probs[:, s % SR, k * P:(k + 1) * P], ident[:, :])
                ins.then_inc(turned, 1)

            def mix(i, b, k):
                if k == 0:
                    pe.wait_ge(turned_kept, i * ST + (b + 1) * R)
                    pe.wait_ge(mix_kept, i * NB + max(b - 1, 0))
                    pe.wait_ge(keys_ready, i * NB + b + 1)
                ins = pe.matmul(mix_ps[b % 2][:, :], keys[:, b % RING, k, :], probsT[:, b % 2, k, :],
                                start=(k == 0), stop=(k == KB - 1))
                if k == KB - 1:
                    ins.then_inc(mixed, 1)

            def project(i, t, heads):
                if heads.start == 0:
                    pe.wait_ge(mix_kept, i * NB + (t + 1) * BT)
                for h in heads:
                    ins = pe.matmul(misc_ps[t][:, 0:D], mixT[:, h, t * P:(t + 1) * P], folded[:, h, NC * P:FOLDED],
                                    start=(h == 0), stop=(h == H - 1))
                if heads.stop == H:
                    ins.then_inc(projected, 1)

            def queries_kept(g):
                pe.wait_ge(q_kept_act, g * (HP // 2) + HP // 2)
                pe.wait_ge(q_kept_dve, g * (HP // 2) + HP // 2)

            def iteration(i, last):
                for s in range(ST):
                    turn(i, s)
                    if s + AHEAD < ST:
                        score(i, s + AHEAD)
                    if s >= R and s % R >= R - KB:
                        mix(i, s // R - 1, s % R - (R - KB))
                    if s == ST - 3 and not last:
                        turn_x(i + 1)
                if last:
                    for k in range(KB):
                        mix(i, NB - 1, k)
                    for t in range(G):
                        project(i, t, range(H))
                    return
                pe.wait_ge(xnT_ready, i + 2)
                if layer == 1:
                    query_norms(i + 1)
                for hp in range(HP):
                    queries(i + 1, hp)
                    if 1 <= hp <= KB:
                        mix(i, NB - 1, hp - 1)
                queries_kept(i + 1)
                for s in range(AHEAD):
                    score(i + 1, s)
                    if s == 1:
                        project(i, 0, range(H // 2))
                project(i, 0, range(H // 2, H))
                project(i, 1, range(H))

            pe.sem_inc(mixed, RING)
            pe.wait_ge(pre_loaded, 32 if layer else 16)
            turn_x(0)
            pe.wait_ge(xnT_ready, 1)
            if layer == 1:
                query_norms(0)
            for hp in range(HP):
                queries(0, hp)
            queries_kept(0)
            for s in range(AHEAD):
                score(0, s)
            with pe.Fori(0, ITERS - 1) as i:
                iteration(i, False)
            iteration(ITERS - 1, True)

        @block.scalar
        def _(act):
            def keep_xnT(g):
                act.wait_ge(x_turned, g + 1)
                act.activation(xnT[:, :, :], misc_ps[0][:, :].rearrange("p (c n) -> p c n", c=NC), ACT.Copy
                               ).then_inc(xnT_ready, 1)

            def square_queries(g):
                for m in range(G * NQ):
                    act.wait_ge(n_summed, g * (G * NQ) + max(m - 1, 0))
                    act.wait_ge(n_made, g * (G * NQ) + m + 1)
                    act.activation(squares[:, m % 2, :], misc_ps[m % 2][:, :], ACT.Square).then_inc(n_squared, 1)

            def keep_queries(g, hp):
                act.wait_ge(q_made, g * HP + hp + 1)
                act.activation(qT[:, :, 2 * hp:2 * hp + 2, :].rearrange("p b h t -> p h b t"),
                               misc_ps[0][:, :].rearrange("p (h b t) -> p h b t", h=2, t=T), ACT.Copy
                               ).then_inc(q_kept_act, 1)

            def exp(i, s):
                act.wait_ge(shifted, i * ST + s + 1 + R)
                b, col = s // R, slice(s % 8, s % 8 + 1)
                if layer == 0:
                    scale, least = -1.0, top[:, col]
                else:
                    scale, least = row_scale[:, b // BT, b % BT, s % R:s % R + 1], shift[:, col]
                act.activation(probs[:, s % SR, :], probs[:, s % SR, :], ACT.Exp, bias=least,
                               scale=scale, accum_out=total[:, col]).then_inc(exped, 1)

            def keep_turned(i, s):
                b, r = s // R, s % R
                if r == 0:
                    act.wait_ge(mixed, i * NB + max(b - 1, 0) + RING)
                act.wait_ge(turned, i * ST + s + 1)
                act.activation(probsT[:, b % 2, :, r * P:(r + 1) * P],
                               probsT_ps[s % 2][:, 0:KB * P].rearrange("p (k n) -> p k n", k=KB), ACT.Copy
                               ).then_inc(turned_kept, 1)

            def keep_mix(i, b):
                if b == 0:
                    act.wait_ge(projected, i * G)
                act.wait_ge(mixed, i * NB + b + 1 + RING)
                apart(act, act_passed)
                item = bass.ds(i * NB + b, 1)
                act.activation(mixT[:, :, b * T:(b + 1) * T], mix_ps[b % 2][:, :].rearrange("p (h t) -> p h t", h=H),
                               ACT.Identity, bias=last_ctx[:, item], scale=1.0 if layer else any_key[:, item]
                               ).then_inc(mix_kept, 1)

            def iteration(i, last):
                for s in range(ST):
                    keep_turned(i, s)
                    if s + AHEAD < ST:
                        exp(i, s + AHEAD)
                    if s >= 2 * R and s % R == 0:
                        keep_mix(i, s // R - 2)
                    if s == ST - 3 and not last:
                        keep_xnT(i + 1)
                keep_mix(i, NB - 2)
                if last:
                    keep_mix(i, NB - 1)
                    return
                if layer == 1:
                    square_queries(i + 1)
                for hp in range(0, HP, 2):
                    keep_queries(i + 1, hp)
                    if hp == 2:
                        keep_mix(i, NB - 1)
                if layer == 1:
                    act.wait_ge(rows_ready, i + 2)
                for s in range(AHEAD):
                    exp(i + 1, s)

            keep_xnT(0)
            if layer == 1:
                square_queries(0)
            for hp in range(0, HP, 2):
                keep_queries(0, hp)
            if layer == 1:
                act.wait_ge(rows_ready, 1)
            for s in range(AHEAD):
                exp(0, s)
            act.wait_ge(last_ready, 1)
            with act.Fori(0, ITERS - 1) as i:
                iteration(i, False)
            iteration(ITERS - 1, True)

        @block.vector
        def _(dve):
            FIRST = 1 + AHEAD + EARLY
            LINKS = 1 + 2 * ST

            def row_stats(g, link):
                for t in range(G):
                    ins = dve.bn_stats(stats[:, t, :], x_sb[:, bass.ds(g * G + t, 1), :])
                link(ins, alone=True)
                for t in range(G):
                    ins = dve.bn_aggr(mv[:, t, :], stats[:, t, :])
                ins.then_inc(var_ready, 1)

            def normalize(g):
                dve.wait_ge(rstd_ready, g + 1)
                dve.wait_ge(x_turned, g)
                for t in range(G):
                    dve.tensor_scalar(xn[:, t, :], x_sb[:, bass.ds(g * G + t, 1), :], mv[:, t, 0:1], rstd[:, t:t + 1],
                                      ALU.subtract, ALU.mult).then_inc(normed, 1)

            def sum_squares(g):
                for m in range(G * NQ):
                    dve.wait_ge(n_squared, g * (G * NQ) + m + 1)
                    dve.tensor_reduce(q_sum[:, m // NQ, (m % NQ) * (H // NQ):(m % NQ + 1) * (H // NQ)],
                                      squares[:, m % 2, :].rearrange("p (h d) -> p h d", d=HD), AX_X, ALU.add
                                      ).then_inc(n_summed, 1)

            def keep_queries(g):
                for hp in range(1, HP, 2):
                    dve.wait_ge(q_made, g * HP + hp + 1)
                    dve.tensor_copy(qT[:, :, 2 * hp:2 * hp + 2, :].rearrange("p b h t -> p h b t"),
                                    misc_ps[1][:, :].rearrange("p (h b t) -> p h b t", h=2, t=T)).then_inc(q_kept_dve, 1)

            def weigh(i, s, link):
                b, r = s // R, s % R
                col = slice(s % 8, s % 8 + 1)
                if layer == 0:
                    if r == 0:
                        dve.wait_ge(bias_ready, i * NB + b + 1)
                    other, op, pick, start = bias[:, b % 2, :], ALU.add, ALU.min, 3.4e38
                else:
                    if s == 0:
                        dve.wait_ge(rows_ready, i + 1)
                    if r == 0:
                        dve.wait_ge(kscale_loaded[b % 2], i * (16 * R * NB // 2) + 16 * R * (b // 2 + 1))
                    other, op, pick, start = key_scale[:, b % 2, r, :], ALU.mult, ALU.max, -3.4e38
                dve.wait_ge(turned, i * ST + max(s - SR + 1, 0))
                dve.wait_ge(scored, i * ST + s + 1)
                apart(dve, passed)
                ins = dve.tensor_tensor_reduce(out=probs[:, s % SR, :], in0=score_ps[s % 2][:, 0:S2], in1=other, scale=1.0,
                                               scalar=start, op0=op, op1=pick, accum_out=top[:, col])
                if layer == 1:
                    link(ins)
                    ins = dve.tensor_scalar(shift[:, col], top[:, col], row_scale[:, b // BT, b % BT, r:r + 1], -1.0,
                                            ALU.mult, ALU.mult)
                else:
                    link.n += 1
                    dve.sem_inc(dve_chain, 1)
                ins.then_inc(shifted, 1)

            def share_out(i, s, link):
                dve.wait_ge(exped, i * ST + s + 1)
                col = slice(s % 8, s % 8 + 1)
                link(dve.reciprocal(share[:, col], total[:, col]))
                dve.tensor_scalar(probs[:, s % SR, :], probs[:, s % SR, :], share[:, col], None, ALU.mult
                                  ).then_inc(probs_ready, 1)

            def add(i, t):
                dve.wait_ge(projected, i * G + t + 1)
                tile = x_sb[:, bass.ds(i * G + t, 1), :].rearrange("p a d -> p (a d)")
                dve.tensor_tensor(tile, tile, misc_ps[t][:, 0:D], ALU.add).then_inc(added, 1)

            def iteration(i, last):
                link = Chain(dve, dve_chain, i * LINKS + FIRST, passed)
                for s in range(ST):
                    if s + EARLY < ST:
                        share_out(i, s + EARLY, link)
                    if s + AHEAD < ST:
                        weigh(i, s + AHEAD, link)
                    if not last:
                        if s == ST // 2:
                            row_stats(i + 1, link)
                        if s == ST // 2 + R:
                            normalize(i + 1)
                if not last:
                    if layer == 1:
                        sum_squares(i + 1)
                    keep_queries(i + 1)
                    for s in range(AHEAD):
                        weigh(i + 1, s, link)
                    for s in range(EARLY):
                        share_out(i + 1, s, link)
                    assert link.n == LINKS, link.n
                for t in range(G):
                    add(i, t)

            dve.sem_inc(shifted, R)
            every_last = ctxT[:, S2 - 1:KEYS:S2]
            if layer == 0:
                dve.wait_ge(pre_loaded, 16)
                dve.tensor_reduce(any_key[:, :], mask[:, :, :], AX_X, ALU.max).then_inc(any_ready, 1)
                dve.wait_ge(any_ready, 1)
                dve.tensor_tensor(last_ctx[:, :], every_last, any_key[:, :], ALU.mult).then_inc(last_ready, 1)
            else:
                dve.tensor_copy(last_ctx[:, :], every_last).then_inc(last_ready, 1)
            link = Chain(dve, dve_chain, 0, passed)
            row_stats(0, link)
            normalize(0)
            if layer == 1:
                sum_squares(0)
            keep_queries(0)
            for s in range(AHEAD):
                weigh(0, s, link)
            for s in range(EARLY):
                share_out(0, s, link)
            assert link.n == FIRST, link.n
            with dve.Fori(0, ITERS - 1) as i:
                iteration(i, False)
            iteration(ITERS - 1, True)

        @block.gpsimd
        def _(pool):
            LINKS = 1 + NB if layer == 0 else 1 + 2
            FIRST = 1 if layer == 0 else 1 + 2

            def norm_scale(g, link):
                pool.wait_ge(var_ready, g + 1)
                apart(pool, pool_passed)
                link(pool.tensor_scalar(rstd[:, :], mv[:, :, 1], LN_EPS, None, ALU.add))
                pool.tensor_tensor(rstd[:, :], rstd[:, :], minus_half[:, 0:G], ALU.pow).then_inc(rstd_ready, 1)

            def mask_bias(i, b, link):
                pool.wait_ge(bias_ready, i * NB + b)
                pool.wait_ge(shifted, (i * NB + b) * R)
                apart(pool, pool_passed)
                link(pool.tensor_copy(valid[:, :], mask[:, bass.ds(i * NB + b, 1), :].rearrange("p a s -> p (a s)")),
                     alone=True)
                pool.tensor_scalar(bias[:, b % 2, :], valid[:, :], 1.0, -1e30, ALU.subtract, ALU.mult
                                   ).then_inc(bias_ready, 1)

            def less_last(i, b):
                pool.wait_ge(keys_loaded[b % RING], i * (32 * NB // RING) + 32 * (b // RING + 1))
                apart(pool, pool_passed)
                pool.tensor_tensor(keys[:, b % RING], keys[:, b % RING],
                                   last_key[:, b % RING, :].unsqueeze(1).broadcast_to([P, KB, DC]), ALU.subtract
                                   ).then_inc(keys_ready, 1)

            def row_scales(g, link):
                flat = q_rms[:, :, :].rearrange("p g h -> p (g h)")
                pool.wait_ge(n_summed, g * (G * NQ) + G * NQ)
                apart(pool, pool_passed)
                link(pool.tensor_scalar(flat, q_sum[:, :, :].rearrange("p g h -> p (g h)"), 1.0 / HD, LN_EPS,
                                        ALU.mult, ALU.add))
                link(pool.tensor_tensor(flat, flat, minus_half[:, :], ALU.pow), alone=True)
                for b in range(BT):
                    for j in range(HR):
                        ins = pool.tensor_scalar(
                            row_scale[j * T:(j + 1) * T, :, b, :],
                            q_rms[b * T:(b + 1) * T, :, :].rearrange("p g (r j) -> p g r j", j=HR)[:, :, :, j],
                            SCALE, None, ALU.mult)
                ins.then_inc(rows_ready, 1)
                pool.wait_ge(rows_ready, g + 1)
                apart(pool, pool_passed)

            def iteration(i, last):
                link = Chain(pool, pool_chain, i * LINKS + FIRST, pool_passed)
                for b in range(NB):
                    if layer == 0:
                        mask_bias(i, b, link)
                    less_last(i, b)
                    if b == NB // 2 + 1 and not last:
                        norm_scale(i + 1, link)
                if layer == 1 and not last:
                    row_scales(i + 1, link)
                assert last or link.n == LINKS, link.n

            pool.memset(minus_half[:, :], -0.5).then_inc(begun, 1)
            pool.wait_ge(begun, 1)
            if layer == 0:
                pool.wait_ge(pre_loaded, 16)
            link = Chain(pool, pool_chain, 0, pool_passed)
            norm_scale(0, link)
            if layer == 1:
                row_scales(0, link)
            assert link.n == FIRST, link.n
            with pool.Fori(0, ITERS - 1) as i:
                iteration(i, False)
            iteration(ITERS - 1, True)


def row_stats(dve, x_tile, stats, mv, link):
    link(dve.bn_stats(stats[:, :], x_tile), alone=True)
    return dve.bn_aggr(mv[:, :], stats[:, :])


def rstd_of(pool, mv, rstd, minus_half, link):
    link(pool.tensor_scalar(rstd[:, :], mv[:, 1:2], LN_EPS, None, ALU.add))
    return pool.tensor_tensor(rstd[:, :], rstd[:, :], minus_half[:, :], ALU.pow)


def own_scores(act, blocks, score_ps, b):
    q = slice(b * T, (b + 1) * T)
    return act.activation(blocks[q, :, :], score_ps[q, :, q], ACT.Copy)


def per_head(x, n=T):
    return x.unsqueeze(2).broadcast_to([P, H, n])


def self_attention(nc, I, x_sb, ident):
    with ExitStack() as ctx:
        sc = Scope(nc, ctx, "sa0")
        HC = AH // NC
        w_rows, out_rows = sc.sb("w_rows", [P, 3 * NC, D]), sc.sb("out_rows", [P, NC, D])
        wT, outT = sc.sb("wT", [P, NC, 3 * D]), sc.sb("outT", [P, NC, D])
        bias_qk, bias_v, bias_out = sc.sb("bias_qk", [P, 2 * NC]), sc.sb("bias_v", [P, D]), sc.sb("bias_out", [P, D])
        head_mask = sc.sb("head_mask", [P, HC])
        stats, mv, rstd, minus_half = sc.sb("stats", [P, 6]), sc.sb("mv", [P, 2]), sc.sb("rstd", [P, 1]), sc.sb("minus_half", [P, 1])
        xn, xnT = sc.sb("xn", [P, D]), sc.sb("xnT", [P, NC, P])
        qkT, k_heads, v = sc.sb("qkT", [P, 2 * NC, P]), sc.sb("k_heads", [P, AH, P]), sc.sb("v", [P, D])
        blocks, top, total = sc.sb("blocks", [P, AH, T]), sc.sb("top", [P, AH]), sc.sb("total", [P, AH])
        probsT = sc.sb("probsT", [P, AH, P])
        mix, mixT = sc.sb("mix", [P, D]), sc.sb("mixT", [P, NC, P])
        score_ps = sc.ps("score", [P, AH, P])
        turn_ps, qk_ps, v_ps, mix_ps = sc.ps("turn"), sc.ps("qk"), sc.ps("v"), sc.ps("mix")

        loaded, mask_step, mask_ready = sc.sem("loaded"), sc.sem("mask_step"), sc.sem("mask_ready")
        w_turned, w_kept, zeroed, half_set = sc.sem("w_turned"), sc.sem("w_kept"), sc.sem("zeroed"), sc.sem("half_set")
        passed, dve_chain, pool_chain = sc.sem("passed"), sc.sem("dve_chain"), sc.sem("pool_chain")
        var_ready, rstd_ready, normed = sc.sem("var_ready"), sc.sem("rstd_ready"), sc.sem("normed")
        x_turned, xnT_ready = sc.sem("x_turned"), sc.sem("xnT_ready")
        qk_made, qk_kept, heads_ready = sc.sem("qk_made"), sc.sem("qk_kept"), sc.sem("heads_ready")
        v_made, v_kept, scored, blocks_act = sc.sem("v_made"), sc.sem("v_kept"), sc.sem("scored"), sc.sem("blocks_act")
        shifted, exped, probsT_ready = sc.sem("shifted"), sc.sem("exped"), sc.sem("probsT_ready")
        mixed, mix_kept, mix_turned, mixT_ready = sc.sem("mixed"), sc.sem("mix_kept"), sc.sem("mix_turned"), sc.sem("mixT_ready")
        projected, added = sc.sem("projected"), sc.sem("added")
        block = sc.block()

        @block.sync
        def _(sp):
            sp.dma_start(w_rows[:, :, :], I["L0_attn_Wqkv_w"].rearrange("(c p) d -> p c d", p=P)).then_inc(loaded, 16)
            sp.dma_start(out_rows[:, :, :], I["L0_attn_out_w"].rearrange("(c p) d -> p c d", p=P)).then_inc(loaded, 16)
            with nc.allow_non_contiguous_dma(reason="one bias per partition"):
                sp.dma_start(bias_qk[:, :], I["L0_attn_Wqkv_b"][0:2 * D].rearrange("(c p) -> p c", p=P)).then_inc(loaded, 16)
            sp.dma_start(bias_v[:, :], I["L0_attn_Wqkv_b"][2 * D:3 * D].partition_broadcast(P)).then_inc(loaded, 16)
            sp.dma_start(bias_out[:, :], I["L0_attn_out_b"].partition_broadcast(P)).then_inc(loaded, 16)
            sp.wait_ge(loaded, 80)

        @block.tensor
        def _(pe):
            def turn_x(n):
                pe.wait_ge(normed, n + 1)
                pe.wait_ge(mixT_ready, n if isinstance(n, int) and n == 0 else n - 1)
                for c in range(NC):
                    ins = pe.transpose(turn_ps[:, c * P:(c + 1) * P], xn[:, c * P:(c + 1) * P], ident[:, :])
                ins.then_inc(x_turned, 1)

            def project_qk(n):
                pe.wait_ge(xnT_ready, n + 1)
                pe.wait_ge(qk_kept, 2 * NC * n)
                for m in range(2 * NC):
                    for c in range(NC):
                        ins = pe.matmul(qk_ps[:, m * P:(m + 1) * P], wT[:, c, m * P:(m + 1) * P], xnT[:, c, :],
                                        start=(c == 0), stop=(c == NC - 1))
                ins.then_inc(qk_made, 1)

            def project_v(n, added_before):
                pe.wait_ge(added, added_before)
                for c in range(NC):
                    ins = pe.matmul(v_ps[:, 0:D], xnT[:, c, :], wT[:, c, 2 * D:3 * D], start=(c == 0), stop=(c == NC - 1))
                ins.then_inc(v_made, 1)

            def score(n):
                pe.wait_ge(heads_ready, NC * n + NC)
                pe.wait_ge(qk_kept, 2 * NC * (n + 1))
                for m in range(AH // 4):
                    c = m * 4 // HC
                    ins = pe.matmul(score_ps[:, 4 * m:4 * m + 4, :], qkT[:, c, :], k_heads[:, 4 * m:4 * m + 4, :],
                                    start=True, stop=True)
                ins.then_inc(scored, 1)

            def mix_v(n):
                pe.wait_ge(probsT_ready, n + 1)
                pe.wait_ge(v_kept, n + 1)
                for h in range(AH):
                    ins = pe.matmul(mix_ps[:, h * AD:(h + 1) * AD], probsT[:, h, :], v[:, h * AD:(h + 1) * AD],
                                    start=True, stop=True)
                ins.then_inc(mixed, 1)

            def project_out(n):
                pe.wait_ge(mix_kept, n + 1)
                pe.wait_ge(xnT_ready, n + 2)
                for c in range(NC):
                    ins = pe.transpose(turn_ps[:, c * P:(c + 1) * P], mix[:, c * P:(c + 1) * P], ident[:, :])
                ins.then_inc(mix_turned, 1)
                pe.wait_ge(mixT_ready, n + 1)
                pe.wait_ge(v_kept, n + 1)
                for c in range(NC):
                    ins = pe.matmul(v_ps[:, D:2 * D], mixT[:, c, :], outT[:, c, :], start=(c == 0), stop=(c == NC - 1))
                ins.then_inc(projected, 1)

            pe.wait_ge(loaded, 80)
            for m in range(3 * NC + NC):
                if m:
                    pe.wait_ge(w_kept, m)
                src = w_rows[:, m, :] if m < 3 * NC else out_rows[:, m - 3 * NC, :]
                for c in range(NC):
                    ins = pe.transpose(turn_ps[:, c * P:(c + 1) * P], src[:, c * P:(c + 1) * P], ident[:, :])
                ins.then_inc(w_turned, 1)
            pe.wait_ge(w_kept, 4 * NC)
            turn_x(0)
            project_qk(0)
            project_v(0, 0)
            score(0)
            pe.wait_ge(xnT_ready, 1)
            turn_x(1)
            with pe.Fori(0, NT - 1) as i:
                pe.wait_ge(blocks_act, i * BT + BT)
                project_qk(i + 1)
                mix_v(i)
                pe.wait_ge(v_kept, i + 1)
                project_v(i + 1, i)
                score(i + 1)
                pe.wait_ge(v_kept, i + 2)
                project_out(i)
                turn_x(i + 2)
            mix_v(NT - 1)
            project_out(NT - 1)

        @block.scalar
        def _(act):
            def keep_xnT(n):
                act.wait_ge(x_turned, n + 1)
                act.activation(xnT[:, :, :], turn_ps[:, 0:D].rearrange("p (c t) -> p c t", c=NC), ACT.Copy).then_inc(xnT_ready, 1)

            def keep_qk(n):
                act.wait_ge(qk_made, n + 1)
                for m in range(2 * NC):
                    act.activation(qkT[:, m, :], qk_ps[:, m * P:(m + 1) * P], ACT.Identity, bias=bias_qk[:, m:m + 1]
                                   ).then_inc(qk_kept, 1)

            def keep_v(n):
                act.wait_ge(v_made, n + 1)
                act.activation(v[:, :], v_ps[:, 0:D], ACT.Copy).then_inc(v_kept, 1)

            def keep_blocks(n):
                act.wait_ge(scored, n + 1)
                act.wait_ge(probsT_ready, n)
                for b in range(BT):
                    own_scores(act, blocks, score_ps, b).then_inc(blocks_act, 1)

            def exp(n):
                act.wait_ge(shifted, n + 1)
                act.activation(blocks[:, :, :], blocks[:, :, :], ACT.Exp, scale=float(AD) ** -0.5).then_inc(exped, 1)

            def keep_mixT(n):
                act.wait_ge(mix_turned, n + 1)
                act.activation(mixT[:, :, :], turn_ps[:, 0:D].rearrange("p (c t) -> p c t", c=NC), ACT.Copy).then_inc(mixT_ready, 1)

            for m in range(4 * NC):
                act.wait_ge(w_turned, m + 1)
                dst = wT[:, :, m * P:(m + 1) * P] if m < 3 * NC else outT[:, :, (m - 3 * NC) * P:(m - 3 * NC + 1) * P]
                act.activation(dst, turn_ps[:, 0:D].rearrange("p (c t) -> p c t", c=NC), ACT.Copy).then_inc(w_kept, 1)
            keep_xnT(0)
            keep_qk(0)
            keep_v(0)
            keep_blocks(0)
            act.wait_ge(v_made, 1)
            keep_xnT(1)
            with act.Fori(0, NT - 1) as i:
                exp(i)
                keep_qk(i + 1)
                act.wait_ge(mixed, i + 1)
                keep_v(i + 1)
                keep_mixT(i)
                keep_blocks(i + 1)
                keep_xnT(i + 2)
            exp(NT - 1)
            keep_mixT(NT - 1)

        @block.vector
        def _(dve):
            LINKS = 6

            def stats_of(n, link):
                row_stats(dve, x_sb[:, bass.ds(n, 1), :].rearrange("p a d -> p (a d)"), stats, mv, link).then_inc(var_ready, 1)

            def normalize(n):
                dve.wait_ge(rstd_ready, n + 1)
                dve.wait_ge(x_turned, n)
                dve.tensor_scalar(xn[:, :], x_sb[:, bass.ds(n, 1), :].rearrange("p a d -> p (a d)"), mv[:, 0:1], rstd[:, 0:1],
                                  ALU.subtract, ALU.mult).then_inc(normed, 1)

            def softmax(n, link):
                dve.wait_ge(blocks_act, BT * n + BT)
                link(dve.tensor_reduce(top[:, :], blocks[:, :, :], AX_X, ALU.max))
                dve.tensor_tensor(blocks[:, :, :], blocks[:, :, :], per_head(top[:, :]), ALU.subtract).then_inc(shifted, 1)
                dve.wait_ge(exped, n + 1)
                link(dve.tensor_reduce(total[:, :], blocks[:, :, :], AX_X, ALU.add))
                link(dve.reciprocal(total[:, :], total[:, :]))
                link(dve.tensor_tensor(blocks[:, :, :], blocks[:, :, :], per_head(total[:, :]), ALU.mult))
                dve.wait_ge(mixed, n)
                for b in range(BT):
                    q = slice(b * T, (b + 1) * T)
                    ins = dve.transpose(probsT[q, :, q], blocks[q, :, :])
                ins.then_inc(probsT_ready, 1)

            def finish(n, link):
                dve.wait_ge(mixed, n + 1)
                dve.wait_ge(mix_turned, n)
                dve.tensor_tensor(mix[:, :], mix_ps[:, 0:D], bias_v[:, :], ALU.add).then_inc(mix_kept, 1)

            def add(n, link):
                tile = x_sb[:, bass.ds(n, 1), :].rearrange("p a d -> p (a d)")
                link(dve.tensor_tensor(tile, tile, bias_out[:, :], ALU.add))
                dve.wait_ge(projected, n + 1)
                dve.tensor_tensor(tile, tile, v_ps[:, D:2 * D], ALU.add).then_inc(added, 1)

            dve.memset(probsT[:, :, :], 0.0).then_inc(zeroed, 1)
            dve.wait_ge(zeroed, 1)
            dve.wait_ge(loaded, 80)
            link = Chain(dve, dve_chain, 0, passed)
            stats_of(0, link)
            normalize(0)
            stats_of(1, link)
            normalize(1)
            with dve.Fori(0, NT - 1) as i:
                link = Chain(dve, dve_chain, i * LINKS + 2, passed)
                softmax(i, link)
                stats_of(i + 2, link)
                finish(i, link)
                normalize(i + 2)
                add(i, link)
                assert link.n == LINKS
            link = Chain(dve, dve_chain, (NT - 1) * LINKS + 2, passed)
            softmax(NT - 1, link)
            finish(NT - 1, link)
            add(NT - 1, link)

        @block.gpsimd
        def _(pool):
            pool.memset(minus_half[:, :], -0.5).then_inc(half_set, 1)
            pool.memset(head_mask[:, :], 1.0).then_inc(mask_step, 1)
            pool.wait_ge(mask_step, 1)
            pool.affine_select(out=head_mask[:, :], in_=head_mask[:, :], compare_op=ALU.is_ge, fill=0.0, base=0,
                               pattern=[[-AD, HC]], channel_multiplier=1).then_inc(mask_step, 1)
            pool.wait_ge(mask_step, 2)
            pool.affine_select(out=head_mask[:, :], in_=head_mask[:, :], compare_op=ALU.is_ge, fill=0.0, base=AD - 1,
                               pattern=[[AD, HC]], channel_multiplier=-1).then_inc(mask_step, 1)
            pool.wait_ge(mask_step, 3)
            pool.wait_ge(half_set, 1)

            def scale_of(n, base):
                link = Chain(pool, pool_chain, base, passed)
                pool.wait_ge(var_ready, n + 1)
                apart(pool, passed)
                rstd_of(pool, mv, rstd, minus_half, link).then_inc(rstd_ready, 1)

            def mask_keys(n):
                for c in range(NC):
                    pool.wait_ge(scored, n)
                    pool.wait_ge(qk_kept, 2 * NC * n + NC + c + 1)
                    pool.tensor_tensor(k_heads[:, c * HC:(c + 1) * HC, :],
                                       qkT[:, NC + c, :].unsqueeze(1).broadcast_to([P, HC, P]),
                                       head_mask[:, :].unsqueeze(2).broadcast_to([P, HC, P]), ALU.mult).then_inc(heads_ready, 1)

            scale_of(0, 0)
            mask_keys(0)
            scale_of(1, 1)
            with pool.Fori(0, NT - 1) as i:
                mask_keys(i + 1)
                scale_of(i + 2, i + 2)


def route(nc, I, x_sb, ident, slot_rows, slot_out, slots_all, weights_all, ctxT, sums, rk_dram):
    with ExitStack() as ctx:
        sc = Scope(nc, ctx, "rt")
        router, routerT = sc.sb("router", [E0, D]), sc.sb("routerT", [P, NC, E0])
        upto, ones, slot_base = sc.sb("upto", [P, P]), sc.sb("ones", [P, P]), sc.sb("slot_base", [P, E0])
        zeros = sc.sb("zeros", [P, 2048])
        stats, mv, rstd, minus_half = sc.sb("stats", [P, 6]), sc.sb("mv", [P, 2]), sc.sb("rstd", [P, 1]), sc.sb("minus_half", [P, 1])
        xn, xnT = sc.sb("xn", [P, 2, D]), sc.sb("xnT", [P, NC, P])
        prob, rest, chosen, before = (sc.sb(n, [P, E0]) for n in ("prob", "rest", "chosen", "before"))
        gate, code, picked = sc.sb("gate", [P, E0]), sc.sb("code", [P, E0]), sc.sb("picked", [P, K0, E0])
        top, best, scale = sc.sb("top", [P, 1]), sc.sb("best", [P, K0]), sc.sb("scale", [P, 2])
        codes = sc.sb("codes", [P, K0])
        places = sc.sb("places", [P, 2, K0], U32)
        norms = KeyNorms(sc, I, ident, ctxT, sums, rk_dram, 0)
        turn_ps, logit_ps, place_ps = sc.ps("turn"), sc.ps("logit"), sc.ps("place")
        loaded, w_turned, w_kept = sc.sem("loaded"), sc.sem("w_turned"), sc.sem("w_kept")
        const_step, consts_ready, zeroed, cleared = sc.sem("const_step"), sc.sem("consts_ready"), sc.sem("zeroed"), sc.sem("cleared")
        passed, dve_chain, pool_chain = sc.sem("passed"), sc.sem("dve_chain"), sc.sem("pool_chain")
        var_ready, rstd_ready, normed = sc.sem("var_ready"), sc.sem("rstd_ready"), sc.sem("normed")
        x_turned, xnT_ready, routed = sc.sem("x_turned"), sc.sem("xnT_ready"), sc.sem("routed")
        shifted, exped, chosen_ready, counted = sc.sem("shifted"), sc.sem("exped"), sc.sem("chosen_ready"), sc.sem("counted")
        places_ready = sc.sem("places_ready")
        sums_set = sc.sem("sums_set")
        scattered = [sc.pool_dma_sem(f"scattered{p}") for p in range(2)]
        block = sc.block()
        U = 2
        ITERS = NT // U

        @block.sync
        def _(sp):
            sp.dma_start(router[:, :], I["L0_ffn_router_w"]).then_inc(loaded, 16)
            norms.load(sp)
            sp.wait_ge(zeroed, 1)
            per = zeros.shape[1] * P
            flat = slot_rows.rearrange("(n p r) d -> n p (r d)", p=P, r=2048 // D)
            for n in range(SLOTS * D // per):
                sp.dma_start(flat[n], zeros[:, :]).then_inc(cleared, 16)
            sp.dma_start(slot_out[SLOTS:SLOTS + 1, :], zeros[0:1, 0:D]).then_inc(cleared, 16)
            sp.wait_ge(cleared, 16 * (SLOTS * D // per + 1))
            with sp.Fori(0, NT) as n:
                norms.store(sp, n)
            sp.wait_ge(norms.rk_stored, 16 * NT)

        @block.tensor
        def _(pe):
            pe.wait_ge(loaded, 16)
            for c in range(NC):
                ins = pe.transpose(turn_ps[:, c * E0:(c + 1) * E0], router[:, c * P:(c + 1) * P], ident[0:E0, 0:E0])
            ins.then_inc(w_turned, 1)
            pe.wait_ge(w_kept, 1)
            pe.wait_ge(consts_ready, 1)
            norms.begin_pe(pe)
            with pe.Fori(0, ITERS) as i:
                for u in range(U):
                    n = i * U + u
                    pe.wait_ge(normed, n + 1)
                    pe.wait_ge(xnT_ready, n)
                    for c in range(NC):
                        ins = pe.transpose(turn_ps[:, c * P:(c + 1) * P], xn[:, u, c * P:(c + 1) * P], ident[:, :])
                    ins.then_inc(x_turned, 1)
                    norms.keys(pe, n, u, 0)
                    pe.wait_ge(xnT_ready, n + 1)
                    pe.wait_ge(exped, n)
                    for c in range(NC):
                        ins = pe.matmul(logit_ps[:, 0:E0], xnT[:, c, :], routerT[:, c, :], start=(c == 0), stop=(c == NC - 1))
                    ins.then_inc(routed, 1)
                    norms.keys(pe, n, u, 1)
                    pe.wait_ge(chosen_ready, n + 1)
                    pe.wait_ge(places_ready, n)
                    pe.matmul(place_ps[:, 0:E0], upto[:, :], chosen[:, :], start=True, stop=False)
                    pe.matmul(place_ps[:, 0:E0], ones[:, :], before[:, :], start=False, stop=True).then_inc(counted, 1)
                    norms.keys(pe, n, u, 2)
                    norms.turn(pe, n)
                    norms.keys(pe, n, u, 3)

        @block.scalar
        def _(act):
            act.wait_ge(w_turned, 1)
            act.activation(routerT[:, :, :], turn_ps[:, 0:NC * E0].rearrange("p (c e) -> p c e", c=NC), ACT.Copy).then_inc(w_kept, 1)
            norms.begin_act(act)
            with act.Fori(0, ITERS) as i:
                for u in range(U):
                    n = i * U + u
                    act.wait_ge(x_turned, n + 1)
                    act.activation(xnT[:, :, :], turn_ps[:, 0:D].rearrange("p (c t) -> p c t", c=NC), ACT.Copy).then_inc(xnT_ready, 1)
                    norms.square(act, n, 0)
                    act.wait_ge(shifted, n + 1)
                    act.activation(prob[:, :], logit_ps[:, 0:E0], ACT.Exp, bias=top[:, 0:1], accum_out=scale[:, 0:1]).then_inc(exped, 1)
                    norms.square(act, n, 1)
                    norms.take_root(act, n, u)
                    norms.square(act, n, 2)
                    norms.square(act, n, 3)

        @block.vector
        def _(dve):
            LINKS = 12
            dve.memset(before[:, :], 0.0).then_inc(const_step, 1)
            dve.memset(sums[:, 1, :, :], 0.0).then_inc(sums_set, 1)
            dve.wait_ge(sums_set, 1)
            norms.begin_dve(dve)

            def stats_of(n, link):
                row_stats(dve, x_sb[:, bass.ds(n, 1), :].rearrange("p a d -> p (a d)"), stats, mv, link).then_inc(var_ready, 1)

            def normalize(n, u, uses):
                dve.wait_ge(rstd_ready, n + 1)
                dve.wait_ge(scattered[u], uses)
                dve.tensor_scalar(xn[:, u, :], x_sb[:, bass.ds(n, 1), :].rearrange("p a d -> p (a d)"), mv[:, 0:1], rstd[:, 0:1],
                                  ALU.subtract, ALU.mult).then_inc(normed, 1)

            stats_of(0, Chain(dve, dve_chain, 0, passed))
            dve.wait_ge(consts_ready, 1)
            normalize(0, 0, 0)
            with dve.Fori(0, ITERS) as i:
                for u in range(U):
                    n = i * U + u
                    link = Chain(dve, dve_chain, n * LINKS + 1, passed)
                    stats_of(n + 1, link)
                    norms.sum(dve, n, u, 0)
                    dve.wait_ge(routed, n + 1)
                    dve.tensor_reduce(top[:, :], logit_ps[:, 0:E0], AX_X, ALU.max, negate=True).then_inc(shifted, 1)
                    dve.wait_ge(exped, n + 1)
                    link(dve.reciprocal(scale[:, 1:2], scale[:, 0:1]))
                    link(dve.tensor_scalar(prob[:, :], prob[:, :], scale[:, 1:2], None, ALU.mult), alone=True)
                    link(dve.max(best[:, :], prob[:, :]), alone=True)
                    link(dve.match_replace(rest[:, :], best[:, :], prob[:, :], -1.0))
                    dve.tensor_tensor(chosen[:, :], prob[:, :], rest[:, :], ALU.not_equal).then_inc(chosen_ready, 1)
                    norms.sum(dve, n, u, 1)
                    link(dve.tensor_reduce(scale[:, 0:1], best[:, :], AX_X, ALU.add))
                    link(dve.tensor_scalar(scale[:, 0:1], scale[:, 0:1], 1e-20, None, ALU.add))
                    link(dve.reciprocal(scale[:, 1:2], scale[:, 0:1]))
                    dve.tensor_scalar(gate[:, :], prob[:, :], scale[:, 1:2], None, ALU.mult)
                    dve.wait_ge(counted, n + 1)
                    dve.tensor_tensor(code[:, :], slot_base[:, :], place_ps[:, 0:E0], ALU.subtract)
                    dve.tensor_tensor(before[:, :], before[:, :], chosen[:, :], ALU.add)
                    link(dve.scalar_tensor_tensor(out=picked[:, 0, :], in0=place_ps[:, 0:E0], scalar=float(CAP), in1=chosen[:, :],
                                                  op0=ALU.is_le, op1=ALU.mult))
                    link(dve.tensor_tensor(code[:, :], code[:, :], picked[:, 0, :], ALU.mult), alone=True)
                    link(dve.max(codes[:, :], code[:, :]))
                    dve.tensor_scalar(slots_all[:, bass.ds(n, 1), :].rearrange("p a k -> p (a k)"), codes[:, :], -1.0,
                                      float(NOWHERE), ALU.mult, ALU.add)
                    dve.tensor_scalar(places[:, u, :], codes[:, :], -1.0, float(NOWHERE), ALU.mult, ALU.add
                                      ).then_inc(places_ready, 1)
                    for k in range(K0):
                        ins = dve.scalar_tensor_tensor(out=picked[:, k, :], in0=code[:, :], scalar=codes[:, k:k + 1], in1=gate[:, :],
                                                       op0=ALU.is_equal, op1=ALU.mult,
                                                       accum_out=weights_all[:, bass.ds(n * K0 + k, 1)])
                    link(ins)
                    norms.invert(dve, n)
                    norms.sum(dve, n, u, 2)
                    norms.keep(dve, n)
                    norms.sum(dve, n, u, 3)
                    normalize(n + 1, 1 - u, (i + u) * (16 * K0))
                    assert link.n == LINKS, link.n

        @block.gpsimd
        def _(pool):
            pool.memset(zeros[:, :], 0.0).then_inc(zeroed, 1)
            pool.memset(minus_half[:, :], -0.5).then_inc(const_step, 1)
            pool.memset(ones[:, :], 1.0).then_inc(const_step, 1)
            pool.memset(upto[:, :], 1.0).then_inc(const_step, 1)
            pool.iota(slot_base[:, :], pattern=[[-CAP, E0]], base=NOWHERE + 1, channel_multiplier=0,
                      allow_small_or_imprecise_dtypes=True).then_inc(const_step, 1)
            pool.wait_ge(const_step, 5)
            pool.affine_select(out=upto[:, :], in_=upto[:, :], compare_op=ALU.is_ge, fill=0.0, base=0,
                               pattern=[[1, P]], channel_multiplier=-1).then_inc(consts_ready, 1)

            def scale_of(n):
                link = Chain(pool, pool_chain, n, passed)
                pool.wait_ge(var_ready, n + 1)
                apart(pool, passed)
                rstd_of(pool, mv, rstd, minus_half, link).then_inc(rstd_ready, 1)

            scale_of(0)
            norms.put(pool, 0, 0)
            pool.wait_ge(cleared, 16 * (SLOTS * D // (2048 * P) + 1))
            with pool.Fori(0, ITERS) as i:
                for u in range(U):
                    n = i * U + u
                    scale_of(n + 1)
                    norms.put(pool, n + 1, 1 - u)
                    pool.wait_ge(places_ready, n + 1)
                    apart(pool, passed)
                    for k in range(K0):
                        pool.indirect_dma_start(out=slot_rows, out_offset=bass.IndirectOffsetOnAxis(ap=places[:, u, k:k + 1], axis=0),
                                                in_=xn[:, u, :], in_offset=None, bounds_check=SLOTS - 1, oob_is_err=False
                                                ).then_inc(scattered[u], 16)
            for u in range(U):
                pool.wait_ge(scattered[u], ITERS * 16 * K0)


def experts(nc, I, ident, slot_rows, slot_out):
    with ExitStack() as ctx:
        sc = Scope(nc, ctx, "ex")
        BUF = 4
        TURNS = E0 // 2
        ITERS = TURNS // BUF
        rows = sc.sb("rows", [P, BUF, D])
        w_in = sc.sb("w_in", [P, BUF, 2, 2, NC, F0])
        w_out = sc.sb("w_out", [F0, BUF, 2, D])
        rowsT = sc.sb("rowsT", [P, 2, NC, P])
        gate, hidden = sc.sb("gate", [F0, 2, P]), sc.sb("hidden", [F0, 2, P])
        out_rows = sc.sb("out_rows", [P, 2, D])
        turn_ps = [sc.ps(f"turn{n}") for n in range(2)]
        mid_ps = [sc.ps(f"mid{n}") for n in range(2)]
        out_ps = [sc.ps(f"out{n}") for n in range(2)]
        loaded = [sc.sem(f"loaded{n}") for n in range(BUF)]
        stored = [sc.pool_dma_sem(f"stored{n}") for n in range(2)]
        turned, rowsT_ready, mid_made, gated, hidden_ready = (sc.sem(n) for n in (
            "turned", "rowsT_ready", "mid_made", "gated", "hidden_ready"))
        out_made, out_kept, passed = sc.sem("out_made"), sc.sem("out_kept"), sc.sem("passed")
        block = sc.block()

        @block.sync
        def _(sp):
            with sp.Fori(0, ITERS) as i:
                for u in range(BUF):
                    n = i * BUF + u
                    sp.wait_ge(out_made, i * BUF + max(u - BUF + 1, 0))
                    sp.dma_start(rows[:, u, :], slot_rows[bass.ds(n * P, P), :]).then_inc(loaded[u], 16)
                    for g, name in enumerate(("L0_ffn_w_gate", "L0_ffn_w_up")):
                        sp.dma_start(w_in[:, u, g], I[name].rearrange("e (p j) f -> p e (j f)", j=NC)[:, bass.ds(n * 2, 2), :]
                                     ).then_inc(loaded[u], 16)
                    sp.dma_start(w_out[:, u], I["L0_ffn_w_down"].rearrange("e f d -> f e d")[:, bass.ds(n * 2, 2), :]
                                 ).then_inc(loaded[u], 16)

        @block.tensor
        def _(pe):
            def turn(i, u):
                n = i * BUF + u
                pe.wait_ge(loaded[u], i * 64 + 64)
                pe.wait_ge(rowsT_ready, i * BUF + max(u - 1, 0))
                for j in range(NC):
                    ins = pe.transpose(turn_ps[u % 2][:, j * P:(j + 1) * P], rows[:, u, j:D:NC], ident[:, :])
                ins.then_inc(turned, 1)

            def middle(i, u):
                n = i * BUF + u
                pe.wait_ge(rowsT_ready, n + 1)
                pe.wait_ge(hidden_ready, i * BUF + max(u - 1, 0))
                for g in range(2):
                    for e in range(2):
                        for j in range(NC):
                            ins = pe.matmul(mid_ps[u % 2][0:F0, (2 * g + e) * CAP:(2 * g + e + 1) * CAP], w_in[:, u, g, e, j, :],
                                            rowsT[:, u % 2, j, e * CAP:(e + 1) * CAP], start=(j == 0), stop=(j == NC - 1))
                ins.then_inc(mid_made, 1)

            def finish(i, u):
                n = i * BUF + u
                pe.wait_ge(hidden_ready, n + 1)
                pe.wait_ge(out_kept, i * BUF + max(u - 1, 0))
                for e in range(2):
                    ins = pe.matmul(out_ps[u % 2][e * CAP:(e + 1) * CAP, 0:D], hidden[:, u % 2, e * CAP:(e + 1) * CAP],
                                    w_out[:, u, e, :], start=True, stop=True)
                ins.then_inc(out_made, 1)

            with pe.Fori(0, ITERS) as i:
                turn(i, 0)
                middle(i, 0)
                for u in range(1, BUF):
                    turn(i, u)
                    middle(i, u)
                    finish(i, u - 1)
                finish(i, BUF - 1)

        @block.scalar
        def _(act):
            with act.Fori(0, ITERS) as i:
                for u in range(BUF):
                    n = i * BUF + u
                    act.wait_ge(mid_made, i * BUF + max(u - 1, 0))
                    act.wait_ge(turned, n + 1)
                    act.activation(rowsT[:, u % 2, :, :], turn_ps[u % 2][:, 0:D].rearrange("p (j s) -> p j s", j=NC), ACT.Copy
                                   ).then_inc(rowsT_ready, 1)
                    act.wait_ge(hidden_ready, i * BUF + max(u - 1, 0))
                    act.wait_ge(mid_made, n + 1)
                    act.activation(gate[:, u % 2, :], mid_ps[u % 2][0:F0, 0:P], ACT.Silu).then_inc(gated, 1)

        @block.vector
        def _(dve):
            def keep(i, u):
                n = i * BUF + u
                dve.wait_ge(out_made, n + 1)
                dve.wait_ge(stored[u % 2], i * (16 * BUF // 2) + 16 * (u // 2))
                dve.tensor_copy(out_rows[:, u % 2, :], out_ps[u % 2][:, 0:D]).then_inc(out_kept, 1)

            with dve.Fori(0, ITERS) as i:
                for u in range(BUF):
                    n = i * BUF + u
                    dve.wait_ge(out_made, i * BUF + max(u - 1, 0))
                    dve.wait_ge(gated, n + 1)
                    dve.tensor_tensor(hidden[:, u % 2, :], mid_ps[u % 2][0:F0, P:2 * P], gate[:, u % 2, :], ALU.mult
                                      ).then_inc(hidden_ready, 1)
                    if u:
                        keep(i, u - 1)
                keep(i, BUF - 1)

        @block.gpsimd
        def _(pool):
            with pool.Fori(0, ITERS) as i:
                for u in range(BUF):
                    n = i * BUF + u
                    pool.wait_ge(out_kept, n + 1)
                    apart(pool, passed)
                    pool.dma_start(slot_out[bass.ds(n * P, P), :], out_rows[:, u % 2, :]).then_inc(stored[u % 2], 16)
            for u in range(2):
                pool.wait_ge(stored[u], 16 * TURNS // 2)


def combine(nc, I, x_sb, ident, slots_all, weights_all, slot_out, ctxT, sums, rk_dram):
    with ExitStack() as ctx:
        sc = Scope(nc, ctx, "cb")
        U = 2
        ITERS = NT // U
        places = sc.sb("places", [P, U, K0], U32)
        got = sc.sb("got", [P, U, K0, D])
        norms = KeyNorms(sc, I, ident, ctxT, sums, rk_dram, NT)
        assert 2 * NT * GROUP == KEYS - REST and REST <= P
        placed, gathered = sc.sem("placed"), [sc.pool_dma_sem(f"gathered{u}") for u in range(U)]
        passed, added = sc.sem("passed"), sc.sem("added")
        AHEAD = U * K0
        block = sc.block()

        @block.sync
        def _(sp):
            norms.load(sp)
            with sp.Fori(0, NT) as n:
                norms.store(sp, n)
            norms.store(sp, NT)
            norms.store(sp, NT + 1, REST)
            sp.wait_ge(norms.rk_stored, 16 * (NT + 2))

        @block.tensor
        def _(pe):
            norms.begin_pe(pe)
            with pe.Fori(0, ITERS) as i:
                for u in range(U):
                    n = i * U + u
                    for c in range(norms.U):
                        norms.keys(pe, n, u, c)
                        if c == 2:
                            norms.turn(pe, n)
            norms.keys(pe, NT, 0, 0, REST)
            norms.turn(pe, NT)
            norms.turn(pe, NT + 1)

        @block.scalar
        def _(act):
            norms.begin_act(act)
            with act.Fori(0, ITERS) as i:
                for u in range(U):
                    n = i * U + u
                    for c in range(norms.U):
                        norms.square(act, n, c)
                        if c == 1:
                            norms.take_root(act, n, u)
            norms.square(act, NT, 0, REST)
            norms.take_root(act, NT, 0)
            norms.take_root(act, NT + 1, 1, missing=norms.PER - norms.NQ)

        @block.vector
        def _(dve):
            norms.begin_dve(dve)
            dve.sem_inc(added, AHEAD)
            with dve.Fori(0, ITERS) as i:
                for u in range(U):
                    n = i * U + u
                    tile = x_sb[:, bass.ds(n, 1), :].rearrange("p a d -> p (a d)")
                    for c in range(norms.U):
                        norms.sum(dve, n, u, c)
                        if c == 1:
                            norms.invert(dve, n)
                        if c == 2:
                            norms.keep(dve, n)
                        dve.wait_ge(gathered[u], i * (16 * K0) + 16 * K0)
                        for k in range(c * K0 // norms.U, (c + 1) * K0 // norms.U):
                            dve.wait_ge(added, n * K0 + (AHEAD + k))
                            dve.scalar_tensor_tensor(out=tile, in0=got[:, u, k, :], scalar=weights_all[:, bass.ds(n * K0 + k, 1)],
                                                     in1=tile, op0=ALU.mult, op1=ALU.add).then_inc(added, 1)
            norms.sum(dve, NT, 0, 0, REST)
            norms.invert(dve, NT)
            norms.keep(dve, NT)
            norms.invert(dve, NT + 1)
            norms.keep(dve, NT + 1)

        @block.gpsimd
        def _(pool):
            with pool.Fori(0, ITERS) as i:
                for u in range(U):
                    n = i * U + u
                    norms.put(pool, n, u)
                    pool.wait_ge(added, n * K0 + K0)
                    apart(pool, passed)
                    pool.tensor_copy(places[:, u, :], slots_all[:, bass.ds(n, 1), :].rearrange("p a k -> p (a k)")
                                     ).then_inc(placed, 1)
                    pool.wait_ge(placed, n + 1)
                    apart(pool, passed)
                    for k in range(K0):
                        pool.indirect_dma_start(out=got[:, u, k, :], out_offset=None, in_=slot_out,
                                                in_offset=bass.IndirectOffsetOnAxis(ap=places[:, u, k:k + 1], axis=0),
                                                bounds_check=SLOTS, oob_is_err=False).then_inc(gathered[u], 16)
            norms.put(pool, NT, 0, REST)


def routed_experts(nc, I, x_sb, ident, ctxT, sums, rk_dram):
    with ExitStack() as ctx:
        sc = Scope(nc, ctx, "moe")
        slot_rows = nc.dram_tensor("slot_rows", (SLOTS, D), F32).ap()
        slot_out = nc.dram_tensor("slot_out", (SLOTS + 1, D), F32).ap()
        slots_all, weights_all = sc.sb("slots", [P, NT, K0], U32), sc.sb("weights", [P, NT * K0])
        route(nc, I, x_sb, ident, slot_rows, slot_out, slots_all, weights_all, ctxT, sums, rk_dram)
        experts(nc, I, ident, slot_rows, slot_out)
        combine(nc, I, x_sb, ident, slots_all, weights_all, slot_out, ctxT, sums, rk_dram)


def fp4_weights(nc, I, wide, narrow):
    with ExitStack() as ctx:
        sc = Scope(nc, ctx, "fp4")
        names = ("wq", "wk", "wv", "wo")
        weights = list(wide) + [narrow]
        scales = [sc.sb(f"scale_{n}", list(w.shape)) for n, w in zip(names, weights)]
        loaded = [sc.sem(f"loaded_{n}") for n in names]
        scaled = sc.sem("scaled")
        block = sc.block()
        DMAS = 1 + P // FP4_ROWS

        def load(eng, j):
            name, w, s = names[j], weights[j], scales[j]
            eng.dma_start(w[:, :, :], I[f"L1_attn_{name}_codes"].rearrange("(c p) n -> p c n", p=P)).then_inc(loaded[j], 16)
            rows = I[f"L1_attn_{name}_scales"].rearrange("(c g) n -> g c n", g=P // FP4_ROWS)
            for g in range(P // FP4_ROWS):
                eng.dma_start(s[g * FP4_ROWS:(g + 1) * FP4_ROWS, :, :], rows[g].partition_broadcast(FP4_ROWS)
                              ).then_inc(loaded[j], 16)

        def scale(eng, j):
            eng.wait_ge(loaded[j], 16 * DMAS)
            eng.tensor_tensor(weights[j][:, :, :], weights[j][:, :, :], scales[j][:, :, :], ALU.mult).then_inc(scaled, 1)

        @block.sync
        def _(sp):
            load(sp, 0)
            load(sp, 2)

        @block.scalar
        def _(act):
            load(act, 1)
            load(act, 3)

        @block.vector
        def _(dve):
            for j in range(4):
                scale(dve, j)
            dve.wait_ge(scaled, 4)


def self_attention_fp4(nc, I, x_sb, ident):
    with ExitStack() as ctx:
        sc = Scope(nc, ctx, "sa1")
        G = 4
        NG = H // G
        wq, wk, wv = (sc.sb(n, [P, NC, H * HD]) for n in ("wq", "wk", "wv"))
        wo = sc.sb("wo", [P, H, D])
        fp4_weights(nc, I, (wq, wk, wv), wo)
        bias_q, bias_k, bias_v = (sc.sb(n, [P, H]) for n in ("bias_q", "bias_k", "bias_v"))
        bias_out = sc.sb("bias_out", [P, D])
        stats, mv, rstd, minus_half = sc.sb("stats", [P, 6]), sc.sb("mv", [P, 2]), sc.sb("rstd", [P, 1]), sc.sb("minus_half", [P, 1])
        xn, xnT = sc.sb("xn", [P, D]), sc.sb("xnT", [P, NC, P])
        qT, kT, v = sc.sb("qT", [P, H, P]), sc.sb("kT", [P, H, P]), sc.sb("v", [P, H * HD])
        blocks, top, total = sc.sb("blocks", [P, H, T]), sc.sb("top", [P, H]), sc.sb("total", [P, H])
        probsT, mixT = sc.sb("probsT", [P, H, P]), sc.sb("mixT", [P, H, P])
        score_ps = sc.ps("score", [P, H, P])
        work_ps = [sc.ps(f"work{b}", [P, G, P]) for b in range(2)]
        turn_ps, out_ps = sc.ps("turn"), sc.ps("out")

        loaded, zeroed, half_set = sc.sem("loaded"), sc.sem("zeroed"), sc.sem("half_set")
        passed, dve_chain, pool_chain = sc.sem("passed"), sc.sem("dve_chain"), sc.sem("pool_chain")
        var_ready, rstd_ready, normed = sc.sem("var_ready"), sc.sem("rstd_ready"), sc.sem("normed")
        x_turned, xnT_ready = sc.sem("x_turned"), sc.sem("xnT_ready")
        q_made, q_kept, k_made, k_kept, v_made, v_kept = (sc.sem(n) for n in (
            "q_made", "q_kept", "k_made", "k_kept", "v_made", "v_kept"))
        scored, blocks_kept, shifted, exped, probsT_ready = (sc.sem(n) for n in (
            "scored", "blocks_kept", "shifted", "exped", "probsT_ready"))
        mixed, mix_kept, projected, added = (sc.sem(n) for n in ("mixed", "mix_kept", "projected", "added"))
        block = sc.block()

        @block.sync
        def _(sp):
            with nc.allow_non_contiguous_dma(reason="one bias per partition"):
                for bias, name in ((bias_q, "bq"), (bias_k, "bk"), (bias_v, "bv")):
                    sp.dma_start(bias[:, :], I["L1_attn_" + name].rearrange("(h d) -> d h", d=HD)).then_inc(loaded, 16)
            sp.dma_start(bias_out[:, :], I["L1_attn_bo"].partition_broadcast(P)).then_inc(loaded, 16)
            sp.wait_ge(loaded, 64)

        @block.tensor
        def _(pe):
            def turn_x(n):
                pe.wait_ge(normed, n + 1)
                pe.wait_ge(xnT_ready, n)
                for c in range(NC):
                    ins = pe.transpose(turn_ps[:, c * P:(c + 1) * P], xn[:, c * P:(c + 1) * P], ident[:, :])
                ins.then_inc(x_turned, 1)

            def project_qk(n):
                pe.wait_ge(xnT_ready, n + 1)
                for g in range(NG):
                    for w, ps, kept, made in ((wq, work_ps[0], q_kept, q_made), (wk, work_ps[1], k_kept, k_made)):
                        if g:
                            pe.wait_ge(kept, NG * n + g)
                        else:
                            pe.wait_ge(v_kept, NG * n)
                        for j in range(G):
                            h = g * G + j
                            for c in range(NC):
                                ins = pe.matmul(ps[:, j, :], w[:, c, h * HD:(h + 1) * HD], xnT[:, c, :],
                                                start=(c == 0), stop=(c == NC - 1))
                        ins.then_inc(made, 1)

            def project_v(n, first):
                for g in range(NG):
                    if g >= 2:
                        pe.wait_ge(v_kept, NG * n + g - 1)
                    elif first:
                        pe.wait_ge(k_kept if g else q_kept, NG)
                    else:
                        pe.wait_ge(mix_kept, NG * n - 1 + g)
                    for c in range(NC):
                        ins = pe.matmul(work_ps[g % 2][:, :, :], xnT[:, c, :], wv[:, c, g * 512:(g + 1) * 512],
                                        start=(c == 0), stop=(c == NC - 1))
                    ins.then_inc(v_made, 1)

            def score(n):
                pe.wait_ge(q_kept, NG * n + NG)
                pe.wait_ge(k_kept, NG * n + NG)
                pe.wait_ge(blocks_kept, n * BT)
                for h in range(H):
                    ins = pe.matmul(score_ps[:, h, :], qT[:, h, :], kT[:, h, :], start=True, stop=True)
                ins.then_inc(scored, 1)

            def mix(n, last):
                pe.wait_ge(probsT_ready, n + 1)
                pe.wait_ge(v_kept, NG * n + NG)
                for g in range(NG):
                    if g >= 2:
                        pe.wait_ge(mix_kept, NG * n + g - 1)
                    elif not last:
                        pe.wait_ge(k_kept if g else q_kept, NG * n + 2 * NG)
                    for j in range(G):
                        h = g * G + j
                        ins = pe.matmul(work_ps[g % 2][:, j, :], v[:, h * HD:(h + 1) * HD], probsT[:, h, :],
                                        start=True, stop=True)
                    ins.then_inc(mixed, 1)

            def project_out(n):
                pe.wait_ge(mix_kept, NG * n + NG)
                pe.wait_ge(added, n)
                for h in range(H):
                    ins = pe.matmul(out_ps[:, 0:D], mixT[:, h, :], wo[:, h, :], start=(h == 0), stop=(h == H - 1))
                ins.then_inc(projected, 1)

            turn_x(0)
            project_qk(0)
            project_v(0, True)
            turn_x(1)
            score(0)
            with pe.Fori(0, NT - 1) as i:
                project_qk(i + 1)
                mix(i, False)
                project_v(i + 1, False)
                turn_x(i + 2)
                project_out(i)
                score(i + 1)
            mix(NT - 1, True)
            project_out(NT - 1)

        @block.scalar
        def _(act):
            def keep_xnT(n):
                act.wait_ge(x_turned, n + 1)
                act.wait_ge(v_made, NG * n)
                act.activation(xnT[:, :, :], turn_ps[:, 0:D].rearrange("p (c t) -> p c t", c=NC), ACT.Copy).then_inc(xnT_ready, 1)

            def keep_k(n, g):
                act.wait_ge(scored, n)
                act.wait_ge(k_made, NG * n + g + 1)
                for j in range(G):
                    h = g * G + j
                    ins = act.activation(kT[:, h, :], work_ps[1][:, j, :], ACT.Identity, bias=bias_k[:, h:h + 1])
                ins.then_inc(k_kept, 1)

            def keep_v(n):
                for g in range(NG):
                    act.wait_ge(mixed, NG * n)
                    act.wait_ge(v_made, NG * n + g + 1)
                    act.activation(v[:, g * 512:(g + 1) * 512].rearrange("p (j d) -> p j d", j=G), work_ps[g % 2][:, :, :],
                                   ACT.Copy).then_inc(v_kept, 1)

            def keep_blocks(n):
                act.wait_ge(scored, n + 1)
                act.wait_ge(probsT_ready, n)
                for b in range(BT):
                    own_scores(act, blocks, score_ps, b).then_inc(blocks_kept, 1)

            def exp(n):
                act.wait_ge(shifted, n + 1)
                act.activation(blocks[:, :, :], blocks[:, :, :], ACT.Exp, scale=SCALE).then_inc(exped, 1)

            act.wait_ge(loaded, 64)
            keep_xnT(0)
            for g in range(NG):
                keep_k(0, g)
            keep_v(0)
            keep_xnT(1)
            keep_blocks(0)
            with act.Fori(0, NT - 1) as i:
                keep_k(i + 1, 0)
                exp(i)
                for g in range(1, NG):
                    keep_k(i + 1, g)
                keep_v(i + 1)
                keep_xnT(i + 2)
                keep_blocks(i + 1)
            exp(NT - 1)

        @block.vector
        def _(dve):
            LINKS = 6

            def tile_of(n):
                return x_sb[:, bass.ds(n, 1), :].rearrange("p a d -> p (a d)")

            def stats_of(n, link):
                row_stats(dve, tile_of(n), stats, mv, link).then_inc(var_ready, 1)

            def normalize(n):
                dve.wait_ge(rstd_ready, n + 1)
                dve.wait_ge(x_turned, n)
                dve.tensor_scalar(xn[:, :], tile_of(n), mv[:, 0:1], rstd[:, 0:1], ALU.subtract, ALU.mult).then_inc(normed, 1)

            def head_bias(bias, g):
                return bias[:, g * G:(g + 1) * G].unsqueeze(2).broadcast_to([P, G, P])

            def keep_q(n, g):
                dve.wait_ge(scored, n)
                dve.wait_ge(q_made, NG * n + g + 1)
                dve.tensor_tensor(qT[:, g * G:(g + 1) * G, :], work_ps[0][:, :, :], head_bias(bias_q, g), ALU.add
                                  ).then_inc(q_kept, 1)

            def shift(n, link):
                dve.wait_ge(blocks_kept, BT * n + BT)
                link(dve.tensor_reduce(top[:, :], blocks[:, :, :], AX_X, ALU.max))
                dve.tensor_tensor(blocks[:, :, :], blocks[:, :, :], per_head(top[:, :]), ALU.subtract).then_inc(shifted, 1)

            def divide(n, link):
                dve.wait_ge(exped, n + 1)
                link(dve.tensor_reduce(total[:, :], blocks[:, :, :], AX_X, ALU.add))
                link(dve.reciprocal(total[:, :], total[:, :]))
                link(dve.tensor_tensor(blocks[:, :, :], blocks[:, :, :], per_head(total[:, :]), ALU.mult))

            def turn_probs(n):
                dve.wait_ge(mixed, NG * n)
                for b in range(BT):
                    q = slice(b * T, (b + 1) * T)
                    ins = dve.transpose(probsT[q, :, q], blocks[q, :, :])
                ins.then_inc(probsT_ready, 1)

            def keep_mix(n, g):
                dve.wait_ge(projected, n)
                dve.wait_ge(mixed, NG * n + g + 1)
                dve.tensor_tensor(mixT[:, g * G:(g + 1) * G, :], work_ps[g % 2][:, :, :], head_bias(bias_v, g), ALU.add
                                  ).then_inc(mix_kept, 1)

            def add(n, link):
                link(dve.tensor_tensor(tile_of(n), tile_of(n), bias_out[:, :], ALU.add))
                dve.wait_ge(projected, n + 1)
                dve.tensor_tensor(tile_of(n), tile_of(n), out_ps[:, 0:D], ALU.add).then_inc(added, 1)

            dve.memset(probsT[:, :, :], 0.0).then_inc(zeroed, 1)
            dve.wait_ge(zeroed, 1)
            dve.wait_ge(loaded, 64)
            link = Chain(dve, dve_chain, 0, passed)
            stats_of(0, link)
            normalize(0)
            for g in range(NG):
                keep_q(0, g)
            stats_of(1, link)
            normalize(1)
            with dve.Fori(0, NT - 1) as i:
                link = Chain(dve, dve_chain, i * LINKS + 2, passed)
                keep_q(i + 1, 0)
                shift(i, link)
                keep_q(i + 1, 1)
                divide(i, link)
                keep_q(i + 1, 2)
                turn_probs(i)
                keep_q(i + 1, 3)
                stats_of(i + 2, link)
                for g in range(NG):
                    keep_mix(i, g)
                normalize(i + 2)
                add(i, link)
                assert link.n == LINKS, link.n
            link = Chain(dve, dve_chain, (NT - 1) * LINKS + 2, passed)
            shift(NT - 1, link)
            divide(NT - 1, link)
            turn_probs(NT - 1)
            for g in range(NG):
                keep_mix(NT - 1, g)
            add(NT - 1, link)

        @block.gpsimd
        def _(pool):
            pool.memset(minus_half[:, :], -0.5).then_inc(half_set, 1)
            pool.wait_ge(half_set, 1)

            def scale_of(n):
                link = Chain(pool, pool_chain, n, passed)
                pool.wait_ge(var_ready, n + 1)
                apart(pool, passed)
                rstd_of(pool, mv, rstd, minus_half, link).then_inc(rstd_ready, 1)

            scale_of(0)
            scale_of(1)
            with pool.Fori(0, NT - 1) as i:
                scale_of(i + 2)


def dense_experts(nc, I, x_sb, ident, out):
    with ExitStack() as ctx:
        sc = Scope(nc, ctx, "ff1")
        GT = 2
        GROUPS = NT // GT
        U = 2
        ITERS = GROUPS // U
        TOP = 2
        W = 8
        STEPS = E1
        FC = F1 // P
        fc1, fc2 = sc.sb("fc1", [P, E1, NC, F1]), sc.sb("fc2", [P, E1, FC, D])
        fc1_b, fc2_b = sc.sb("fc1_b", [P, E1, FC]), sc.sb("fc2_b", [E1, D])
        gate_w, alpha = sc.sb("gate_w", [P, NC, E1]), sc.sb("alpha", [P, E1])
        stats, mv, rstd, minus_half = sc.sb("stats", [P, GT, 6]), sc.sb("mv", [P, GT, 2]), sc.sb("rstd", [P, GT]), sc.sb("minus_half", [P, 1])
        xn, xnT = sc.sb("xn", [P, GT, D]), sc.sb("xnT", [P, U, NC, GT, P])
        prob, top, total = sc.sb("prob", [P, GT, E1]), sc.sb("top", [P, GT]), sc.sb("total", [P, GT])
        best, pair, rest = sc.sb("best", [P, GT, W]), sc.sb("pair", [P, GT, W]), sc.sb("rest", [P, GT, E1])
        weight = sc.sb("weight", [P, U, GT, E1])
        weightT = sc.sb("weightT", [E1, GT, P])
        hidden = sc.sb("hidden", [P, 2, FC, GT * P])
        turn_ps = sc.ps("turn", [P, NC, GT, P])
        route_ps, bias_ps = sc.ps("route"), sc.ps("bias", [P, GT, D])
        mid_ps = [sc.ps(f"mid{b}", [P, FC, GT * P]) for b in range(2)]
        out_ps = [sc.ps(f"out{b}", [P, GT, D]) for b in range(2)]

        loaded, fc1_loaded, fc2_loaded = sc.sem("loaded"), sc.sem("fc1_loaded"), sc.sem("fc2_loaded")
        pair_set, half_set = sc.sem("pair_set"), sc.sem("half_set")
        passed, dve_chain, pool_chain = sc.sem("passed"), sc.sem("dve_chain"), sc.sem("pool_chain")
        var_ready, rstd_ready, normed = sc.sem("var_ready"), sc.sem("rstd_ready"), sc.sem("normed")
        x_turned, xnT_ready, routed, shifted, exped = (sc.sem(n) for n in (
            "x_turned", "xnT_ready", "routed", "shifted", "exped"))
        weighed, weight_turned, weightT_ready, biased, based = (sc.sem(n) for n in (
            "weighed", "weight_turned", "weightT_ready", "biased", "based"))
        mid_made, hidden_ready, out_made, added, stored = (sc.sem(n) for n in (
            "mid_made", "hidden_ready", "out_made", "added", "stored"))
        block = sc.block()
        LOADS = 4

        def tile_of(n):
            return x_sb[:, bass.ds(n, 1), :].rearrange("p a d -> p (a d)")

        @block.sync
        def _(sp):
            with nc.allow_non_contiguous_dma(reason="one bias per partition, small rows"):
                sp.dma_start(gate_w[:, :, :], I["L1_ffn_gate_w"].rearrange("(c p) e -> p c e", p=P)).then_inc(loaded, 16)
                sp.dma_start(fc1_b[:, :, :], I["L1_ffn_fc1_b"].rearrange("e (f p) -> p e f", p=P)).then_inc(loaded, 16)
            sp.dma_start(fc2_b[:, :], I["L1_ffn_fc2_b"]).then_inc(loaded, 16)
            sp.dma_start(alpha[:, :], I["L1_ffn_alpha"].partition_broadcast(P)).then_inc(loaded, 16)
            sp.dma_start(fc1[:, :, :, :], I["L1_ffn_fc1_w"].rearrange("e (c p) f -> p e c f", p=P)).then_inc(fc1_loaded, 16)
            sp.dma_start(fc2[:, :, :, :], I["L1_ffn_fc2_w"].rearrange("e (c p) d -> p e c d", p=P)).then_inc(fc2_loaded, 16)
            result = out.rearrange("(n b) t d -> (b t) n d", b=BT)
            with sp.Fori(0, ITERS) as i:
                for p in range(U):
                    g = i * U + p
                    sp.wait_ge(added, (g + 1) * (STEPS * GT))
                    sp.dma_start(result[:, bass.ds(g * GT, GT), :], x_sb[:, bass.ds(g * GT, GT), :]).then_inc(stored, 16)
            sp.wait_ge(stored, 16 * GROUPS)

        @block.tensor
        def _(pe):
            def turn(g, p):
                pe.wait_ge(normed, (g + 1) * GT)
                pe.wait_ge(xnT_ready, g)
                for c in range(NC):
                    for t in range(GT):
                        ins = pe.transpose(turn_ps[:, c, t, :], xn[:, t, c * P:(c + 1) * P], ident[:, :])
                ins.then_inc(x_turned, 1)

            def route(g, p):
                pe.wait_ge(xnT_ready, g + 1)
                pe.wait_ge(weightT_ready, g)
                for t in range(GT):
                    for c in range(NC):
                        ins = pe.matmul(route_ps[:, t * E1:(t + 1) * E1], xnT[:, p, c, t, :], gate_w[:, c, :],
                                        start=(c == 0), stop=(c == NC - 1))
                ins.then_inc(routed, 1)

            def turn_weights(g, p):
                pe.wait_ge(weighed, g + 1)
                for t in range(GT):
                    ins = pe.transpose(route_ps[0:E1, 256 + t * P:256 + (t + 1) * P], weight[:, p, t, :], ident[:, :])
                ins.then_inc(weight_turned, 1)

            def bias(g, p):
                pe.wait_ge(weightT_ready, g + 1)
                pe.wait_ge(based, g * GT)
                for t in range(GT):
                    ins = pe.matmul(bias_ps[:, t, :], weightT[:, t, :], fc2_b[:, :], start=True, stop=True)
                ins.then_inc(biased, 1)

            prepare = {2: turn, 4: route, 6: turn_weights, 7: bias}

            def first(k, e, p):
                pe.wait_ge(hidden_ready, k if isinstance(k, int) else k - 1)
                for f in range(FC):
                    for c in range(NC):
                        ins = pe.matmul(mid_ps[k_parity(e)][:, f, :], fc1[:, e, c, f * P:(f + 1) * P],
                                        xnT[:, p, c, :, :], start=(c == 0), stop=(c == NC - 1))
                ins.then_inc(mid_made, 1)

            def second(k, e):
                pe.wait_ge(hidden_ready, k + 1)
                pe.wait_ge(added, k * GT - GT if e else k * GT)
                for t in range(GT):
                    for f in range(FC):
                        ins = pe.matmul(out_ps[e % 2][:, t, :], hidden[:, e % 2, f, t * P:(t + 1) * P], fc2[:, e, f, :],
                                        start=(f == 0), stop=(f == FC - 1))
                ins.then_inc(out_made, 1)

            def k_parity(e):
                return e % 2

            pe.wait_ge(loaded, 16 * LOADS)
            for stage in prepare.values():
                stage(0, 0)
            pe.wait_ge(fc1_loaded, 16)
            first(0, 0, 0)
            pe.wait_ge(fc2_loaded, 16)
            with pe.Fori(0, ITERS) as i:
                for p in range(U):
                    g = i * U + p
                    for e in range(STEPS):
                        k = g * STEPS + e
                        if e + 1 < STEPS:
                            first(k + 1, e + 1, p)
                        else:
                            pe.wait_ge(xnT_ready, g + 2)
                            first(k + 1, 0, 1 - p)
                        if e in prepare:
                            prepare[e](g + 1, 1 - p)
                        second(k, e)

        @block.scalar
        def _(act):
            def keep_xnT(g, p):
                act.wait_ge(x_turned, g + 1)
                act.activation(xnT[:, p, :, :, :], turn_ps[:, :, :, :], ACT.Copy).then_inc(xnT_ready, 1)

            def exp(g, p):
                act.wait_ge(shifted, g + 1)
                act.activation(prob[:, :, :], prob[:, :, :], ACT.Exp).then_inc(exped, 1)

            def keep_weights(g, p):
                act.wait_ge(weight_turned, g + 1)
                act.wait_ge(biased, g)
                act.activation(weightT[:, :, :], route_ps[0:E1, 256:512].rearrange("e (t n) -> e t n", t=GT), ACT.Copy
                               ).then_inc(weightT_ready, 1)

            prepare = {2: keep_xnT, 5: exp, 6: keep_weights}

            def gelu(k, e):
                act.wait_ge(out_made, k - 1 if e else k)
                act.wait_ge(mid_made, k + 1)
                for f in range(FC):
                    ins = act.activation(hidden[:, e % 2, f, :], mid_ps[e % 2][:, f, :], ACT.Gelu, bias=fc1_b[:, e, f:f + 1])
                ins.then_inc(hidden_ready, 1)

            act.wait_ge(loaded, 16 * LOADS)
            for stage in prepare.values():
                stage(0, 0)
            with act.Fori(0, ITERS) as i:
                for p in range(U):
                    g = i * U + p
                    for e in range(STEPS):
                        gelu(g * STEPS + e, e)
                        if e in prepare:
                            prepare[e](g + 1, 1 - p)

        @block.vector
        def _(dve):
            LINKS = 13

            def stats_of(g, p, link):
                for t in range(GT):
                    link(dve.bn_stats(stats[:, t, :], tile_of(g * GT + t)), alone=True)
                    dve.bn_aggr(mv[:, t, :], stats[:, t, :]).then_inc(var_ready, 1)

            def normalize(g, p, link):
                dve.wait_ge(x_turned, g)
                for t in range(GT):
                    dve.wait_ge(rstd_ready, g + 1)
                    dve.tensor_scalar(xn[:, t, :], tile_of(g * GT + t), mv[:, t, 0:1], rstd[:, t:t + 1],
                                      ALU.subtract, ALU.mult).then_inc(normed, 1)

            def per_tile(x, n):
                return x.unsqueeze(2).broadcast_to([P, GT, n])

            def shift(g, p, link):
                dve.wait_ge(routed, g + 1)
                logits = route_ps[:, 0:GT * E1].rearrange("q (t e) -> q t e", t=GT)
                link(dve.tensor_reduce(top[:, :], logits, AX_X, ALU.max))
                dve.tensor_tensor(prob[:, :, :], logits, per_tile(top[:, :], E1), ALU.subtract).then_inc(shifted, 1)

            def weigh(g, p, link):
                dve.wait_ge(exped, g + 1)
                link(dve.tensor_reduce(total[:, :], prob[:, :, :], AX_X, ALU.add))
                link(dve.reciprocal(total[:, :], total[:, :]))
                link(dve.tensor_tensor(prob[:, :, :], prob[:, :, :], per_tile(total[:, :], E1), ALU.mult), alone=True)
                dve.max(best[:, 0, :], prob[:, 0, :])
                link(dve.max(best[:, 1, :], prob[:, 1, :]))
                link(dve.tensor_copy(pair[:, :, 0:TOP], best[:, :, 0:TOP]), alone=True)
                for t in range(GT):
                    ins = dve.match_replace(rest[:, t, :], pair[:, t, :], prob[:, t, :], -1.0)
                link(ins)
                link(dve.tensor_tensor(rest[:, :, :], rest[:, :, :], prob[:, :, :], ALU.not_equal))
                dve.tensor_reduce(total[:, :], pair[:, :, 0:TOP], AX_X, ALU.add)
                link(dve.tensor_tensor(rest[:, :, :], rest[:, :, :], prob[:, :, :], ALU.mult))
                link(dve.reciprocal(total[:, :], total[:, :]))
                link(dve.tensor_tensor(rest[:, :, :], rest[:, :, :], per_tile(total[:, :], E1), ALU.mult))
                dve.tensor_tensor(weight[:, p, :, :], rest[:, :, :], alpha[:, :].unsqueeze(1).broadcast_to([P, GT, E1]), ALU.mult
                                  ).then_inc(weighed, 1)

            prepare = {0: stats_of, 1: normalize, 4: shift, 5: weigh}

            def add_bias(g):
                dve.wait_ge(biased, g + 1)
                for t in range(GT):
                    dve.tensor_tensor(tile_of(g * GT + t), tile_of(g * GT + t), bias_ps[:, t, :], ALU.add).then_inc(based, 1)

            def add(g, p, e):
                k = g * STEPS + e
                dve.wait_ge(out_made, k + 1)
                for t in range(GT):
                    if e:
                        dve.wait_ge(added, k * GT + t - 1)
                    else:
                        dve.wait_ge(based, g * GT + t + 1)
                    dve.scalar_tensor_tensor(out=tile_of(g * GT + t), in0=out_ps[e % 2][:, t, :], scalar=weight[:, p, t, e:e + 1],
                                             in1=tile_of(g * GT + t), op0=ALU.mult, op1=ALU.add).then_inc(added, 1)

            dve.memset(pair[:, :, :], -2.0).then_inc(pair_set, 1)
            dve.wait_ge(pair_set, 1)
            dve.wait_ge(loaded, 16 * LOADS)
            link = Chain(dve, dve_chain, 0, passed)
            for stage in prepare.values():
                stage(0, 0, link)
            assert link.n == LINKS, link.n
            with dve.Fori(0, ITERS) as i:
                for p in range(U):
                    g = i * U + p
                    link = Chain(dve, dve_chain, (g + 1) * LINKS, passed)
                    add_bias(g)
                    for e in range(STEPS):
                        if e in prepare:
                            prepare[e](g + 1, 1 - p, link)
                        add(g, p, e)

        @block.gpsimd
        def _(pool):
            pool.memset(minus_half[:, :], -0.5).then_inc(half_set, 1)
            pool.wait_ge(half_set, 1)

            def scale_of(g):
                link = Chain(pool, pool_chain, g, passed)
                pool.wait_ge(var_ready, (g + 1) * GT)
                apart(pool, passed)
                link(pool.tensor_scalar(rstd[:, :], mv[:, :, 1], LN_EPS, None, ALU.add))
                pool.tensor_tensor(rstd[:, :], rstd[:, :], minus_half[:, :].broadcast_to([P, GT]), ALU.pow).then_inc(rstd_ready, 1)

            scale_of(0)
            with pool.Fori(0, GROUPS) as g:
                scale_of(g + 1)


def build(nc, I, out):
    with ExitStack() as ctx:
        sc = Scope(nc, ctx, "all")
        x_sb, ident = sc.sb("x", [P, NT + 2, D]), sc.sb("ident", [P, P])
        load_inputs(nc, I, x_sb, ident)
        with ExitStack() as cross:
            sc = Scope(nc, cross, "cross")
            rk_dram = nc.dram_tensor("rk", (H * RK_COPIES, RK_AHEAD + KEYS), F32).ap()
            folded_dram = nc.dram_tensor("folded1", (P, H, FOLDED), F32).ap()
            sums = sc.sb("sums", [P, 2, KeyNorms.U, H])
            ctxT, folded = sc.sb("ctxT", [P, KEYS]), sc.sb("folded", [P, H, FOLDED])
            fold_weights(nc, I, ident, folded, folded_dram, ctxT)
            cross_attention(nc, I, 0, x_sb, ident, ctxT, folded, folded_dram, rk_dram)
            self_attention(nc, I, x_sb, ident)
            routed_experts(nc, I, x_sb, ident, ctxT, sums, rk_dram)
            cross_attention(nc, I, 1, x_sb, ident, ctxT, folded, folded_dram, rk_dram)
        self_attention_fp4(nc, I, x_sb, ident)
        dense_experts(nc, I, x_sb, ident, out)


OUT_SHAPE = (B, T, D)
NAMES = (
    ["x", "ctx_1024", "mask_BxS2_bf1"]
    + [f"L0_xattn_{n}" for n in ("Wq", "Wk", "Wv", "Wo")]
    + [f"L0_attn_{n}" for n in ("Wqkv_w", "Wqkv_b", "out_w", "out_b")]
    + [f"L0_ffn_{n}" for n in ("router_w", "w_gate", "w_up", "w_down")]
    + [f"L1_xattn_{n}" for n in ("Wq", "Wk", "Wv", "Wo", "gq", "gk")]
    + [f"L1_attn_{w}_{n}" for w in ("wq", "wk", "wv", "wo") for n in ("codes", "scales")]
    + [f"L1_attn_{n}" for n in ("bq", "bk", "bv", "bo")]
    + [f"L1_ffn_{n}" for n in ("gate_w", "fc1_w", "fc1_b", "fc2_w", "fc2_b", "alpha")]
)


def kernel(**inputs):
    import numpy as _np
    import concourse.bacc as _bacc
    from concourse import mybir as _mybir
    from concourse.bass_utils import run_bass_kernel_spmd as _run

    nc = _bacc.Bacc("TRN2", target_bir_lowering=False, num_devices=1)
    arrays, args = {}, {}
    for name in NAMES:
        a = _np.ascontiguousarray(inputs[name])
        if a.dtype == _np.bool_:
            a = a.view(_np.uint8)
        arrays[f"in_{name}_dram"] = a
        args[name] = nc.dram_tensor(f"in_{name}_dram", a.shape, _mybir.dt.from_np(a.dtype), kind="ExternalInput").ap()
    out = nc.dram_tensor("out_0_dram", OUT_SHAPE, F32, kind="ExternalOutput").ap()
    build(nc, args, out)
    r = _run(nc, [arrays], core_ids=[0])
    return r.results[0]["out_0_dram"]
```

```python
from contextlib import ExitStack

import concourse.bass as bass
from concourse import mybir

ALU = mybir.AluOpType
ACT = mybir.ActivationFunctionType
F32 = mybir.dt.float32
U32 = mybir.dt.uint32
AX_X = mybir.AxisListType.X

P = 128
B, T, D = 64, 32, 256
S2, DC = 257, 128
H, HD = 16, 128
KVH = 8
AH, AD = 16, 16
E0, K0, F0, CAP = 64, 8, 96, 64
FP4_ROWS = 32
E1, F1 = 8, 256
NC = D // P
NT = B * T // P
BT = P // T
KEYS = B * S2
LN_EPS = 1e-5
SCALE = float(HD) ** -0.5
SLOTS = E0 * CAP
FOLDED = NC * P + D
GROUP = 512
REST = KEYS % GROUP
RK_AHEAD = GROUP
RK_COPIES = 4
NOWHERE = SLOTS


class Chain:

    def __init__(self, eng, sem, base=0, passed=None):
        self.eng, self.sem, self.base, self.passed, self.n = eng, sem, base, passed, 0

    def __call__(self, ins, alone=False):
        self.n += 1
        ins.then_inc(self.sem, 1)
        self.eng.wait_ge(self.sem, self.base + self.n)
        if alone:
            apart(self.eng, self.passed)


def apart(eng, passed):
    eng.sem_inc(passed, 1)


class Scope:

    def __init__(self, nc, ctx, name):
        self.nc, self.ctx, self.name, self.sems = nc, ctx, name, []

    def sb(self, name, shape, dt=F32):
        return self.ctx.enter_context(self.nc.sbuf_tensor(f"{self.name}_{name}", shape, dt))

    def ps(self, name, shape=(P, 512), dt=F32):
        return self.ctx.enter_context(self.nc.psum_tensor(f"{self.name}_{name}_ps", list(shape), dt))

    def sem(self, name):
        handle = self.ctx.enter_context(self.nc.semaphore(f"{self.name}_{name}"))
        self.sems.append(handle)
        return handle

    def pool_dma_sem(self, name):
        self.sems.append(self.nc.alloc_semaphore(name=f"{self.name}_{name}"))
        return self.sems[-1]

    def block(self):
        with self.nc.Block() as block:
            @block.sync
            def _(sp):
                for handle in self.sems:
                    sp.sem_clear(handle)
        return self.ctx.enter_context(self.nc.Block())


def load_inputs(nc, I, x_sb, ident):
    with ExitStack() as ctx:
        sc = Scope(nc, ctx, "in")
        x_loaded, padded, zeroed, made = sc.sem("x_loaded"), sc.sem("padded"), sc.sem("zeroed"), sc.sem("made")
        block = sc.block()

        @block.sync
        def _(sp):
            sp.dma_start(x_sb[:, 0:NT, :], I["x"].rearrange("(n b) t d -> (b t) n d", b=BT)).then_inc(x_loaded, 16)
            sp.wait_ge(x_loaded, 16)

        @block.vector
        def _(dve):
            dve.memset(x_sb[:, NT:, :], 0.0).then_inc(padded, 1)
            dve.wait_ge(padded, 1)

        @block.gpsimd
        def _(pool):
            pool.memset(ident[:, :], 0.0).then_inc(zeroed, 1)
            pool.wait_ge(zeroed, 1)
            pool.affine_select(out=ident[:, :], in_=ident[:, :], compare_op=ALU.not_equal, fill=1.0, base=0,
                               pattern=[[-1, P]], channel_multiplier=1).then_inc(made, 1)


def fold_weights(nc, I, ident, folded, folded_dram, ctxT):
    with ExitStack() as ctx:
        sc = Scope(nc, ctx, "fold")
        UNITS, SLOT = KVH, 2
        wq = [sc.sb(f"wq{l}", [P, SLOT, NC, 2 * HD]) for l in range(2)]
        wk = [sc.sb(f"wk{l}", [P, SLOT, (l + 1) * HD]) for l in range(2)]
        wv = [sc.sb(f"wv{l}", [P, SLOT, (l + 1) * HD]) for l in range(2)]
        wo = [sc.sb(f"wo{l}", [P, SLOT, 2, D]) for l in range(2)]
        wT = sc.sb("wT", [P, 2, 4 * P])
        stage = sc.sb("stage", [P, 2, FOLDED])
        rows = sc.sb("rows", [P, 4 * SLOT, GROUP // P, DC])
        gains = sc.sb("gains", [P, 2])
        gain = sc.sb("gain", [P, 1])
        turned_ps = [sc.ps(f"turned{n}") for n in range(2)]
        prod_ps = [sc.ps(f"prod{n}") for n in range(2)]
        ctx_ps = [sc.ps(f"ctx{n}") for n in range(2)]
        ctx_turned, ctx_kept = sc.sem("ctx_turned"), sc.sem("ctx_kept")
        rows_loaded = [sc.sem(f"rows_loaded{k}") for k in range(4 * SLOT)]
        loaded = [sc.sem(f"loaded{p}") for p in range(SLOT)]
        gains_loaded, gain_ready = sc.sem("gains_loaded"), sc.sem("gain_ready")
        passed_dve = sc.sem("passed_dve")
        passed, stored = sc.sem("passed"), [sc.pool_dma_sem(f"stored{j}") for j in range(2)]
        turned, wT_ready, multiplied, kept = sc.sem("turned"), sc.sem("wT_ready"), sc.sem("multiplied"), sc.sem("kept")
        block = sc.block()
        DMAS = 8
        ITERS = UNITS // SLOT
        STEPS = 4 * SLOT

        def step(k):
            return k // 4, (k % 4) // 2, k % 2

        names = ["L0_xattn_", "L1_xattn_"]
        assert ITERS * STEPS * GROUP + REST == KEYS and 0 < REST <= P
        ctx_rows = I["ctx_1024"].rearrange("b s d -> (b s) d")

        @block.sync
        def _(sp):
            sp.dma_start(gains[:, 0:1], I["L1_xattn_gq"].rearrange("(d a) -> d a", a=1)).then_inc(gains_loaded, 16)
            sp.dma_start(gains[:, 1:2], I["L1_xattn_gk"].rearrange("(d a) -> d a", a=1)).then_inc(gains_loaded, 16)
            with sp.Fori(0, ITERS) as i:
                for p in range(SLOT):
                    u = i * SLOT + p
                    sp.wait_ge(multiplied, i * STEPS)
                    for l in range(2):
                        n, w = names[l], (l + 1) * HD
                        sp.dma_start(wq[l][:, p], I[n + "Wq"].rearrange("(c p) n -> p c n", p=P)[
                            :, :, bass.ds(u * (2 * HD), 2 * HD)]).then_inc(loaded[p], 16)
                        sp.dma_start(wk[l][:, p], I[n + "Wk"][:, bass.ds(u * w, w)]).then_inc(loaded[p], 16)
                        sp.dma_start(wv[l][:, p], I[n + "Wv"][:, bass.ds(u * w, w)]).then_inc(loaded[p], 16)
                        sp.dma_start(wo[l][:, p], I[n + "Wo"].rearrange("(h d) n -> d h n", d=HD)[
                            :, bass.ds(u * 2, 2), :]).then_inc(loaded[p], 16)
                    for k in range(4 * p, 4 * p + 4):
                        sp.wait_ge(ctx_turned, i * STEPS + k + 1)
                        sp.dma_start(rows[:, k], ctx_rows[bass.ds((i * STEPS + k) * GROUP, GROUP), :].rearrange(
                            "(c p) d -> p c d", p=P)).then_inc(rows_loaded[k], 16)
            sp.wait_ge(ctx_turned, ITERS * STEPS + 1)
            sp.dma_start(rows[0:REST, 0, 0, :], ctx_rows[KEYS - REST:KEYS, :]).then_inc(rows_loaded[0], 16)

        @block.tensor
        def _(pe):
            def turn(i, k):
                p, l, j = step(k)
                kv = j * HD if l else 0
                if k % 4 == 0:
                    pe.wait_ge(loaded[p], i * (16 * DMAS) + 16 * DMAS)
                pe.wait_ge(wT_ready, i * STEPS + max(k - 1, 0))
                ps = turned_ps[k % 2]
                for c in range(NC):
                    pe.transpose(ps[:, c * P:(c + 1) * P], wq[l][:, p, c, j * HD:(j + 1) * HD], ident[:, :])
                pe.transpose(ps[:, 2 * P:3 * P], wk[l][:, p, kv:kv + HD], ident[:, :])
                pe.transpose(ps[:, 3 * P:4 * P], wv[l][:, p, kv:kv + HD], ident[:, :]).then_inc(turned, 1)

            def product(i, k):
                p, l, j = step(k)
                pe.wait_ge(wT_ready, i * STEPS + k + 1)
                pe.wait_ge(kept, i * STEPS + max(k - 1, 0))
                w, ps = wT[:, k % 2], prod_ps[k % 2]
                for c in range(NC):
                    pe.matmul(ps[:, c * P:(c + 1) * P], w[:, c * P:(c + 1) * P], w[:, 2 * P:3 * P], start=True, stop=True)
                pe.matmul(ps[:, 2 * P:2 * P + D], w[:, 3 * P:4 * P], wo[l][:, p, j, :],
                          start=True, stop=True).then_inc(multiplied, 1)

            def turn_ctx(i, k):
                pe.wait_ge(rows_loaded[k], i * 16 + 16)
                pe.wait_ge(ctx_kept, i * STEPS + max(k - 1, 0))
                for c in range(GROUP // P):
                    ins = pe.transpose(ctx_ps[k % 2][:, c * P:(c + 1) * P], rows[:, k, c, :], ident[:, :])
                ins.then_inc(ctx_turned, 1)

            pe.sem_inc(ctx_turned, STEPS)
            with pe.Fori(0, ITERS) as i:
                turn(i, 0)
                for k in range(STEPS):
                    if k + 1 < STEPS:
                        turn(i, k + 1)
                    product(i, k)
                    turn_ctx(i, k)
            pe.wait_ge(rows_loaded[0], ITERS * 16 + 16)
            pe.wait_ge(ctx_kept, ITERS * STEPS)
            pe.transpose(ctx_ps[0][:, 0:REST], rows[0:REST, 0, 0, :], ident[0:REST, 0:REST]).then_inc(ctx_turned, 1)

        @block.vector
        def _(dve):
            dve.wait_ge(gains_loaded, 32)
            dve.tensor_tensor(gain[:, :], gains[:, 0:1], gains[:, 1:2], ALU.mult).then_inc(gain_ready, 1)
            dve.wait_ge(gain_ready, 1)

            def keep_ctx(i, k):
                dve.wait_ge(ctx_turned, i * STEPS + STEPS + k + 1)
                apart(dve, passed_dve)
                dve.tensor_copy(ctxT[:, bass.ds((i * STEPS + k) * GROUP, GROUP)], ctx_ps[k % 2][:, :]).then_inc(ctx_kept, 1)

            with dve.Fori(0, ITERS) as i:
                for k in range(STEPS):
                    _, l, _ = step(k)
                    dve.wait_ge(multiplied, i * STEPS + max(k - 1, 0))
                    dve.wait_ge(turned, i * STEPS + k + 1)
                    w, ps = wT[:, k % 2], turned_ps[k % 2]
                    dve.tensor_scalar(w[:, 0:2 * P], ps[:, 0:2 * P], gain[:, 0:1] if l else -SCALE,
                                      None, ALU.mult)
                    dve.tensor_copy(w[:, 2 * P:4 * P], ps[:, 2 * P:4 * P]).then_inc(wT_ready, 1)
                    if k:
                        keep_ctx(i, k - 1)
                keep_ctx(i, STEPS - 1)
            dve.wait_ge(ctx_turned, (ITERS + 1) * STEPS + 1)
            dve.tensor_copy(ctxT[:, KEYS - REST:KEYS], ctx_ps[0][:, 0:REST]).then_inc(ctx_kept, 1)

        @block.scalar
        def _(act):
            with act.Fori(0, ITERS) as i:
                for k in range(STEPS):
                    p, l, j = step(k)
                    h = i * (2 * SLOT) + (2 * p + j)
                    act.wait_ge(multiplied, i * STEPS + k + 1)
                    if l:
                        act.wait_ge(stored[j], i * (16 * SLOT) + 16 * p)
                        to = stage[:, j, :]
                    else:
                        to = folded[:, bass.ds(h, 1), :].rearrange("p a n -> p (a n)")
                    act.activation(to, prod_ps[k % 2][:, 0:FOLDED], ACT.Copy).then_inc(kept, 1)

        @block.gpsimd
        def _(pool):
            with pool.Fori(0, ITERS) as i:
                for k in range(STEPS):
                    p, l, j = step(k)
                    if l:
                        pool.wait_ge(kept, i * STEPS + k + 1)
                        apart(pool, passed)
                        pool.dma_start(folded_dram[:, bass.ds(i * (2 * SLOT) + (2 * p + j), 1), :],
                                       stage[:, j, :]).then_inc(stored[j], 16)
            for j in range(2):
                pool.wait_ge(stored[j], 16 * UNITS)


class KeyNorms:

    NQ = H * HD // 512
    HQ = H // NQ
    SQ = 4

    def __init__(self, sc, I, ident, ctxT, wk, sums, rk_dram, first, before=None, banks=NQ):
        self.U = U = sums.shape[2]
        self.PER = U * self.NQ
        NQ = self.NQ
        self.I, self.ident, self.ctxT, self.rk_dram = I, ident, ctxT, rk_dram
        self.wk, self.sums, self.first, self.before = wk, sums, first, before
        self.stage = sc.sb("kn_stage", [P, 2, U * P])
        self.squares = sc.sb("kn_squares", [P, self.SQ, 512])
        self.root, self.rk = sc.sb("kn_root", [P, GROUP // P, H]), sc.sb("kn_rk", [P, GROUP // P, H])
        self.rkT, self.eps = sc.sb("kn_rkT", [H, 1, GROUP]), sc.sb("kn_eps", [P, 1])
        self.banks = banks
        self.key_ps = [sc.ps(f"kn_key{n}") for n in range(banks)]
        self.rk_ps = sc.ps("kn_rk")
        self.wk_loaded, self.eps_set, self.staged = sc.sem("kn_wk_loaded"), sc.sem("kn_eps_set"), sc.sem("kn_staged")
        self.keyed, self.squared, self.summed = (sc.sem("kn_" + n) for n in ("keyed", "squared", "summed"))
        self.rooted, self.rk_ready, self.rk_turned, self.rk_kept, self.rk_stored = (sc.sem("kn_" + n) for n in (
            "rooted", "rk_ready", "rk_turned", "rk_kept", "rk_stored"))
        self.passed = sc.sem("kn_passed")

    def load(self, sp):
        sp.dma_start(self.wk[:, :], self.I["L1_xattn_Wk"]).then_inc(self.wk_loaded, 16)

    def chunks_before(self, j):
        return self.before.shape[1] if self.before is not None and isinstance(j, int) and j == 0 else self.U

    def store(self, sp, j, n=None):
        chunks = self.chunks_before(j)
        n = n or chunks * P
        sp.wait_ge(self.rk_kept, j + 1)
        to = self.rk_dram.rearrange("(h c) n -> h c n", c=RK_COPIES)
        sp.dma_start(to[:, :, bass.ds(j * (self.U * P) + (RK_AHEAD + self.first - chunks * P), n)],
                     self.rkT[:, :, 0:n].broadcast_to([H, RK_COPIES, n])).then_inc(self.rk_stored, 16)

    def put(self, pool, j, slot, n=None):
        n = n or self.U * P
        pool.wait_ge(self.keyed, j * self.PER)
        apart(pool, self.passed)
        pool.tensor_copy(self.stage[:, slot, 0:n], self.ctxT[:, bass.ds(j * (self.U * P) + self.first, n)]).then_inc(self.staged, 1)

    def begin_pe(self, pe):
        pe.sem_inc(self.keyed, self.PER)

    def keys(self, pe, j, slot, u, n=P):
        if u == 0:
            pe.wait_ge(self.staged, j + 1)
        for q in range(self.NQ):
            pe.wait_ge(self.squared, j * self.PER + (u * self.NQ + q + 1))
            pe.matmul(self.key_ps[q % self.banks][0:n, :], self.stage[:, slot, u * P:u * P + n], self.wk[:, q * 512:(q + 1) * 512],
                      start=True, stop=True).then_inc(self.keyed, 1)

    def turn(self, pe, j):
        pe.wait_ge(self.rk_ready, j + 1)
        pe.wait_ge(self.rk_kept, j)
        for u in range(self.chunks_before(j)):
            ins = pe.transpose(self.rk_ps[0:H, u * P:(u + 1) * P], self.rk[:, u, :], self.ident[:, :])
        ins.then_inc(self.rk_turned, 1)

    def begin_act(self, act):
        act.sem_inc(self.squared, self.banks)
        act.wait_ge(self.eps_set, 1)

    def on_act(self, u, q):
        return q == self.NQ - 1

    def square(self, act, j, slot, u, n=P):
        for q in range(self.NQ):
            k = u * self.NQ + q
            act.wait_ge(self.summed, j * self.PER + (k + 1))
            act.wait_ge(self.keyed, j * self.PER + (self.PER + k + 1))
            squares, keys = self.squares[0:n, q % self.SQ, :], self.key_ps[q % self.banks][0:n, :]
            if self.on_act(u, q):
                for h in range(self.HQ):
                    col = slice(h * HD, (h + 1) * HD)
                    ins = act.activation(squares[:, col], keys[:, col], ACT.Square,
                                         accum_out=self.sums[0:n, slot, u, q * self.HQ + h:q * self.HQ + h + 1])
                ins.then_inc(self.squared, 1)
            else:
                act.activation(squares, keys, ACT.Square).then_inc(self.squared, 1)

    def take_root(self, act, j, slot, missing=0):
        act.wait_ge(self.rk_ready, j)
        act.wait_ge(self.summed, j * self.PER + (self.SQ - missing))
        chunks = self.chunks_before(j)
        sums = self.sums[:, 1 - slot, :, :] if chunks == self.U else self.before
        act.activation(self.root[:, 0:chunks, :], sums, ACT.Sqrt, bias=self.eps[:, 0:1],
                       scale=1.0 / HD).then_inc(self.rooted, 1)

    def begin_dve(self, dve):
        dve.sem_inc(self.summed, self.SQ)
        dve.memset(self.eps[:, :], LN_EPS).then_inc(self.eps_set, 1)

    def sum(self, dve, j, slot, u, n=P):
        for q in range(self.NQ):
            self.sum_bank(dve, j, slot, u, q, n)

    def sum_bank(self, dve, j, slot, u, q, n=P):
        if q == 0:
            dve.wait_ge(self.rooted, j)
        dve.wait_ge(self.squared, j * self.PER + (self.banks + u * self.NQ + q + 1))
        if self.on_act(u, q):
            dve.wait_ge(self.summed, j * self.PER + (self.SQ + u * self.NQ + q))
            dve.sem_inc(self.summed, 1)
        else:
            dve.tensor_reduce(self.sums[0:n, slot, u, q * self.HQ:(q + 1) * self.HQ],
                              self.squares[0:n, q % self.SQ, :].rearrange("p (h d) -> p h d", h=self.HQ), AX_X, ALU.add
                              ).then_inc(self.summed, 1)

    def invert(self, dve, j):
        dve.wait_ge(self.rk_turned, j)
        dve.wait_ge(self.rooted, j + 1)
        chunks = self.chunks_before(j)
        dve.reciprocal(self.rk[:, 0:chunks, :], self.root[:, 0:chunks, :]).then_inc(self.rk_ready, 1)

    def keep(self, dve, j):
        dve.wait_ge(self.rk_stored, j * 16)
        dve.wait_ge(self.rk_turned, j + 1)
        n = self.chunks_before(j) * P
        dve.tensor_copy(self.rkT[:, 0, 0:n], self.rk_ps[0:H, 0:n]).then_inc(self.rk_kept, 1)


def cross_attention(nc, I, layer, x_sb, ident, ctxT, folded, wq, rk_dram):
    with ExitStack() as ctx:
        sc = Scope(nc, ctx, f"xa{layer}")
        G = 2
        NB = G * BT
        R = H * T // P
        HR = H // R
        ST = NB * R
        ITERS = NT // G
        N = G * P
        HP = H // 2
        RING = 4
        SR = 8
        EARLY = 2
        AHEAD = 4
        KB = S2 // P
        LAG = 3
        assert S2 == KB * P + 1 and 2 * KB == R and AHEAD == R and ST % SR == 0
        NQ = H * HD // 512

        stats, mv = sc.sb("stats", [P, G, 6]), sc.sb("mv", [P, G, 2])
        rstd, minus_half = sc.sb("rstd", [P, G]), sc.sb("minus_half", [P, G * H])
        xn, xnT = sc.sb("xn", [P, G, D]), sc.sb("xnT", [P, NC, N])
        qT = sc.sb("qT", [P, NB, H, T])
        keys, last_key = sc.sb("keys", [P, RING, KB, DC]), sc.sb("last_key", [P, RING, DC])
        probs = sc.sb("probs", [P, SR, S2])
        top = sc.sb("top", [P, 8])
        total, share = sc.sb("total", [P, 8]), sc.sb("share", [P, 8])
        probsT = sc.sb("probsT", [P, 2, KB, H * T])
        mixT = sc.sb("mixT", [P, H, N])
        last_ctx = sc.sb("last_ctx", [P, B])
        if layer == 0:
            mask = sc.sb("mask", [P, B, S2], mybir.dt.uint8)
            mask_rows, any_row = sc.sb("mask_rows", [B, S2], mybir.dt.uint8), sc.sb("any_row", [B, 1])
            any_diag, ones, any_key = sc.sb("any_diag", [B, B]), sc.sb("ones", [B, P]), sc.sb("any_key", [P, B])
            valid, bias = sc.sb("valid", [P, S2]), sc.sb("bias", [P, 2, S2])
        else:
            squares = sc.sb("squares", [P, 2, 512])
            q_sum, q_rms = sc.sb("q_sum", [P, G, H]), sc.sb("q_rms", [P, G, H])
            row_scale = sc.sb("row_scale", [P, G, BT, R])
            key_scale = sc.sb("key_scale", [P, 2, R, S2])
            shift = sc.sb("shift", [P, 8])
        misc_ps = [sc.ps(f"misc{n}") for n in range(2)]
        score_ps = [sc.ps(f"score{n}") for n in range(2)]
        probsT_ps = [sc.ps(f"probsT{n}") for n in range(2)]
        mix_ps = [sc.ps(f"mix{n}") for n in range(2)]

        begun, pre_loaded, any_ready, any_spread = sc.sem("begun"), sc.sem("pre_loaded"), sc.sem("any_ready"), sc.sem("any_spread")
        last_ready, rows_loaded, ones_set = sc.sem("last_ready"), sc.sem("rows_loaded"), sc.sem("ones_set")
        passed, act_passed, pool_passed = sc.sem("passed"), sc.sem("act_passed"), sc.sem("pool_passed")
        keys_loaded = [sc.sem(f"keys_loaded{n}") for n in range(RING)]
        kscale_loaded = [sc.sem(f"kscale_loaded{n}") for n in range(2)]
        keys_ready = sc.sem("keys_ready")
        dve_chain, pool_chain = sc.sem("dve_chain"), sc.sem("pool_chain")
        var_ready, rstd_ready, normed = sc.sem("var_ready"), sc.sem("rstd_ready"), sc.sem("normed")
        x_turned, xnT_ready = sc.sem("x_turned"), sc.sem("xnT_ready")
        q_made, q_kept_act, q_kept_dve = sc.sem("q_made"), sc.sem("q_kept_act"), sc.sem("q_kept_dve")
        n_made, n_squared, n_summed, rows_ready = sc.sem("n_made"), sc.sem("n_squared"), sc.sem("n_summed"), sc.sem("rows_ready")
        bias_ready = sc.sem("bias_ready")
        scored, exped = sc.sem("scored"), sc.sem("exped")
        shifted = sc.sem("shifted")
        probs_ready, turned, turned_kept = sc.sem("probs_ready"), sc.sem("turned"), sc.sem("turned_kept")
        mixed = sc.sem("mixed")
        mix_kept, projected, added = sc.sem("mix_kept"), sc.sem("projected"), sc.sem("added")
        block = sc.block()
        ctx_in = I["ctx_1024"]

        @block.sync
        def _(sp):
            if layer == 0:
                sp.dma_start(mask_rows[:, :], I["mask_BxS2_bf1"]).then_inc(rows_loaded, 16)
                sp.dma_start(mask[:, :, :], I["mask_BxS2_bf1"].partition_broadcast(P)).then_inc(pre_loaded, 16)
            with sp.Fori(0, ITERS) as i:
                for b in range(NB):
                    item = i * NB + b
                    sp.wait_ge(mixed, item + 1)
                    sp.dma_start(keys[:, b % RING], ctx_in[bass.ds(item, 1), 0:KB * P, :].rearrange(
                        "a (k p) d -> p (a k) d", p=P)).then_inc(keys_loaded[b % RING], 16)
                    sp.dma_start(last_key[:, b % RING, :], ctx_in[bass.ds(item, 1), KB * P, :].broadcast_to([P, DC])
                                 ).then_inc(keys_loaded[b % RING], 16)
                    if layer == 1:
                        sp.wait_ge(shifted, item * R)
                        for r in range(R):
                            src = rk_dram[r * HR * RK_COPIES:(r + 1) * HR * RK_COPIES,
                                          bass.ds(item * S2 + RK_AHEAD, S2)]
                            sp.dma_start(key_scale[:, b % 2, r, :], src.unsqueeze(1).broadcast_to(
                                [HR * RK_COPIES, T // RK_COPIES, S2])).then_inc(kscale_loaded[b % 2], 16)

        @block.tensor
        def _(pe):
            def turn_x(g):
                pe.wait_ge(normed, g * G + G)
                if not isinstance(g, int) or g > 0:
                    pe.wait_ge(added, (g - 1) * G)
                for t in range(G):
                    for c in range(NC):
                        ins = pe.transpose(misc_ps[0][:, c * N + t * P:c * N + (t + 1) * P],
                                           xn[:, t, c * P:(c + 1) * P], ident[:, :])
                ins.then_inc(x_turned, 1)

            def query_norms(g):
                for m in range(G * NQ):
                    pe.wait_ge(n_squared, g * (G * NQ) + max(m - 1, 0))
                    for c in range(NC):
                        ins = pe.matmul(misc_ps[m % 2][:, :], xnT[:, c, (m // NQ) * P:(m // NQ + 1) * P],
                                        wq[:, c, (m % NQ) * 512:(m % NQ + 1) * 512], start=(c == 0), stop=(c == NC - 1))
                    ins.then_inc(n_made, 1)
                pe.wait_ge(n_squared, g * (G * NQ) + G * NQ)

            def queries(g, hp):
                if hp >= 2:
                    pe.wait_ge(q_kept_dve if hp % 2 else q_kept_act, g * (HP // 2) + hp // 2)
                for j in range(2):
                    for c in range(NC):
                        ins = pe.matmul(misc_ps[hp % 2][:, j * N:(j + 1) * N], folded[:, 2 * hp + j, c * P:(c + 1) * P],
                                        xnT[:, c, :], start=(c == 0), stop=(c == NC - 1))
                ins.then_inc(q_made, 1)

            def score(i, s):
                b, r = s // R, s % R
                pe.wait_ge(shifted, i * ST + (s - 1 + R))
                pe.matmul(score_ps[s % 2][:, 0:S2], qT[:, b, r * HR:(r + 1) * HR, :].rearrange("p h t -> p (h t)"),
                          ctxT[:, bass.ds((i * NB + b) * S2, S2)], start=True, stop=True).then_inc(scored, 1)

            def turn(i, s):
                pe.wait_ge(probs_ready, i * ST + s + 1)
                pe.wait_ge(turned_kept, i * ST + max(s - 1, 0))
                for k in range(KB):
                    ins = pe.transpose(probsT_ps[s % 2][:, k * P:(k + 1) * P], probs[:, s % SR, k * P:(k + 1) * P], ident[:, :])
                ins.then_inc(turned, 1)

            def mix(i, m):
                b, half, k = m // (2 * KB), m // KB % 2, m % KB
                if k == 0:
                    pe.wait_ge(turned_kept, i * ST + (b * R + (half + 1) * (R // 2)))
                    if half == 0:
                        pe.wait_ge(mix_kept, i * NB + max(b - 1, 0))
                        pe.wait_ge(keys_ready, i * NB + b + 1)
                cols = slice(half * (H * T // 2), (half + 1) * (H * T // 2))
                ins = pe.matmul(mix_ps[b % 2][:, cols], keys[:, b % RING, k, :], probsT[:, b % 2, k, cols],
                                start=(k == 0), stop=(k == KB - 1))
                if half == 1 and k == KB - 1:
                    ins.then_inc(mixed, 1)

            def project(i, t, heads):
                if heads.start == 0:
                    pe.wait_ge(mix_kept, i * NB + (t + 1) * BT)
                for h in heads:
                    ins = pe.matmul(misc_ps[t][:, 0:D], mixT[:, h, t * P:(t + 1) * P], folded[:, h, NC * P:FOLDED],
                                    start=(h == 0), stop=(h == H - 1))
                if heads.stop == H:
                    ins.then_inc(projected, 1)

            def queries_kept(g):
                pe.wait_ge(q_kept_act, g * (HP // 2) + HP // 2)
                pe.wait_ge(q_kept_dve, g * (HP // 2) + HP // 2)

            def iteration(i, last):
                for s in range(ST):
                    turn(i, s)
                    if s + AHEAD < ST:
                        score(i, s + AHEAD)
                    if s >= LAG:
                        mix(i, s - LAG)
                    if s == ST - 3 and not last:
                        turn_x(i + 1)
                rest = list(range(ST - LAG, ST))
                if last:
                    for m in rest:
                        mix(i, m)
                    for t in range(G):
                        project(i, t, range(H))
                    return
                pe.wait_ge(xnT_ready, i + 2)
                if layer == 1:
                    query_norms(i + 1)
                for hp in range(HP):
                    queries(i + 1, hp)
                    if 1 <= hp <= LAG:
                        mix(i, rest[hp - 1])
                pe.wait_ge(q_kept_act, (i + 1) * (HP // 2) + HP // 2)
                project(i, 0, range(H // 2))
                queries_kept(i + 1)
                for s in range(AHEAD):
                    score(i + 1, s)
                    if s == 1:
                        project(i, 0, range(H // 2, H))
                project(i, 1, range(H))

            pe.sem_inc(mixed, RING)
            if layer == 0:
                pe.wait_ge(any_ready, 2)
                pe.wait_ge(ones_set, 1)
                pe.matmul(misc_ps[1][:, 0:B], ones[:, :], any_diag[:, :], start=True, stop=True).then_inc(any_spread, 1)
                pe.wait_ge(any_ready, 3)
            turn_x(0)
            pe.wait_ge(xnT_ready, 1)
            if layer == 1:
                query_norms(0)
            for hp in range(HP):
                queries(0, hp)
            queries_kept(0)
            for s in range(AHEAD):
                score(0, s)
            with pe.Fori(0, ITERS - 1) as i:
                iteration(i, False)
            iteration(ITERS - 1, True)

        @block.scalar
        def _(act):
            def keep_xnT(g):
                act.wait_ge(x_turned, g + 1)
                act.activation(xnT[:, :, :], misc_ps[0][:, :].rearrange("p (c n) -> p c n", c=NC), ACT.Copy
                               ).then_inc(xnT_ready, 1)

            def square_queries(g):
                for m in range(G * NQ):
                    act.wait_ge(n_summed, g * (G * NQ) + max(m - 1, 0))
                    act.wait_ge(n_made, g * (G * NQ) + m + 1)
                    act.activation(squares[:, m % 2, :], misc_ps[m % 2][:, :], ACT.Square).then_inc(n_squared, 1)

            def keep_queries(g, hp):
                act.wait_ge(q_made, g * HP + hp + 1)
                act.activation(qT[:, :, 2 * hp:2 * hp + 2, :].rearrange("p b h t -> p h b t"),
                               misc_ps[0][:, :].rearrange("p (h b t) -> p h b t", h=2, t=T), ACT.Copy
                               ).then_inc(q_kept_act, 1)

            def exp(i, s):
                act.wait_ge(shifted, i * ST + s + 1 + R)
                b, col = s // R, slice(s % 8, s % 8 + 1)
                if layer == 0:
                    scale, least = -1.0, top[:, col]
                else:
                    scale, least = row_scale[:, b // BT, b % BT, s % R:s % R + 1], shift[:, col]
                act.activation(probs[:, s % SR, :], probs[:, s % SR, :], ACT.Exp, bias=least,
                               scale=scale, accum_out=total[:, col]).then_inc(exped, 1)

            def keep_turned(i, s):
                b, r = s // R, s % R
                if r == 0:
                    act.wait_ge(mixed, i * NB + max(b - 1, 0) + RING)
                act.wait_ge(turned, i * ST + s + 1)
                act.activation(probsT[:, b % 2, :, r * P:(r + 1) * P],
                               probsT_ps[s % 2][:, 0:KB * P].rearrange("p (k n) -> p k n", k=KB), ACT.Copy
                               ).then_inc(turned_kept, 1)

            def keep_mix(i, b):
                if b == 0:
                    act.wait_ge(projected, i * G)
                act.wait_ge(mixed, i * NB + b + 1 + RING)
                apart(act, act_passed)
                item = bass.ds(i * NB + b, 1)
                act.activation(mixT[:, :, b * T:(b + 1) * T], mix_ps[b % 2][:, :].rearrange("p (h t) -> p h t", h=H),
                               ACT.Identity, bias=last_ctx[:, item], scale=1.0 if layer else any_key[:, item]
                               ).then_inc(mix_kept, 1)

            def iteration(i, last):
                for s in range(ST):
                    keep_turned(i, s)
                    if s + AHEAD < ST:
                        exp(i, s + AHEAD)
                    if s >= 2 * R and s % R == 0:
                        keep_mix(i, s // R - 2)
                    if s == ST - 3 and not last:
                        keep_xnT(i + 1)
                keep_mix(i, NB - 2)
                if last:
                    keep_mix(i, NB - 1)
                    return
                if layer == 1:
                    square_queries(i + 1)
                for hp in range(0, HP, 2):
                    keep_queries(i + 1, hp)
                    if hp == 4:
                        keep_mix(i, NB - 1)
                if layer == 1:
                    act.wait_ge(rows_ready, i + 2)
                for s in range(AHEAD):
                    exp(i + 1, s)

            keep_xnT(0)
            if layer == 1:
                square_queries(0)
            for hp in range(0, HP, 2):
                keep_queries(0, hp)
            if layer == 1:
                act.wait_ge(rows_ready, 1)
            for s in range(AHEAD):
                exp(0, s)
            act.wait_ge(last_ready, 1)
            with act.Fori(0, ITERS - 1) as i:
                iteration(i, False)
            iteration(ITERS - 1, True)

        @block.vector
        def _(dve):
            FIRST = 1 + 2 * AHEAD
            LINKS = 1 + 2 * ST

            def row_stats(g, link):
                for t in range(G):
                    ins = dve.bn_stats(stats[:, t, :], x_sb[:, bass.ds(g * G + t, 1), :])
                link(ins, alone=True)
                for t in range(G):
                    ins = dve.bn_aggr(mv[:, t, :], stats[:, t, :])
                ins.then_inc(var_ready, 1)

            def normalize(g):
                dve.wait_ge(rstd_ready, g + 1)
                dve.wait_ge(x_turned, g)
                for t in range(G):
                    dve.tensor_scalar(xn[:, t, :], x_sb[:, bass.ds(g * G + t, 1), :], mv[:, t, 0:1], rstd[:, t:t + 1],
                                      ALU.subtract, ALU.mult).then_inc(normed, 1)

            def sum_squares(g):
                for m in range(G * NQ):
                    dve.wait_ge(n_squared, g * (G * NQ) + m + 1)
                    dve.tensor_reduce(q_sum[:, m // NQ, (m % NQ) * (H // NQ):(m % NQ + 1) * (H // NQ)],
                                      squares[:, m % 2, :].rearrange("p (h d) -> p h d", d=HD), AX_X, ALU.add
                                      ).then_inc(n_summed, 1)

            def keep_queries(g):
                for hp in range(1, HP, 2):
                    dve.wait_ge(q_made, g * HP + hp + 1)
                    dve.tensor_copy(qT[:, :, 2 * hp:2 * hp + 2, :].rearrange("p b h t -> p h b t"),
                                    misc_ps[1][:, :].rearrange("p (h b t) -> p h b t", h=2, t=T)).then_inc(q_kept_dve, 1)

            def weigh(i, s, link):
                b, r = s // R, s % R
                col = slice(s % 8, s % 8 + 1)
                if layer == 0:
                    if r == 0:
                        dve.wait_ge(bias_ready, i * NB + b + 1)
                    other, op, pick, start = bias[:, b % 2, :], ALU.add, ALU.min, 3.4e38
                else:
                    if s == 0:
                        dve.wait_ge(rows_ready, i + 1)
                    if r == 0:
                        dve.wait_ge(kscale_loaded[b % 2], i * (16 * R * NB // 2) + 16 * R * (b // 2 + 1))
                    other, op, pick, start = key_scale[:, b % 2, r, :], ALU.mult, ALU.max, -3.4e38
                dve.wait_ge(turned, i * ST + max(s - SR + 1, 0))
                dve.wait_ge(scored, i * ST + s + 1)
                apart(dve, passed)
                ins = dve.tensor_tensor_reduce(out=probs[:, s % SR, :], in0=score_ps[s % 2][:, 0:S2], in1=other, scale=1.0,
                                               scalar=start, op0=op, op1=pick, accum_out=top[:, col])
                if layer == 1:
                    link(ins)
                    ins = dve.tensor_scalar(shift[:, col], top[:, col], row_scale[:, b // BT, b % BT, r:r + 1], -1.0,
                                            ALU.mult, ALU.mult)
                else:
                    link.n += 1
                    dve.sem_inc(dve_chain, 1)
                ins.then_inc(shifted, 1)

            def share_out(i, s, link):
                dve.wait_ge(exped, i * ST + s + 1)
                col = slice(s % 8, s % 8 + 1)
                link(dve.reciprocal(share[:, col], total[:, col]))
                dve.tensor_scalar(probs[:, s % SR, :], probs[:, s % SR, :], share[:, col], None, ALU.mult
                                  ).then_inc(probs_ready, 1)

            def add(i, t):
                dve.wait_ge(projected, i * G + t + 1)
                tile = x_sb[:, bass.ds(i * G + t, 1), :].rearrange("p a d -> p (a d)")
                dve.tensor_tensor(tile, tile, misc_ps[t][:, 0:D], ALU.add).then_inc(added, 1)

            def iteration(i, last):
                link = Chain(dve, dve_chain, i * LINKS + FIRST, passed)
                for s in range(ST):
                    if AHEAD <= s + EARLY < ST:
                        share_out(i, s + EARLY, link)
                    if s + AHEAD < ST:
                        weigh(i, s + AHEAD, link)
                    if not last:
                        if s == ST // 2:
                            row_stats(i + 1, link)
                        if s == ST // 2 + R:
                            normalize(i + 1)
                if not last:
                    if layer == 1:
                        sum_squares(i + 1)
                    keep_queries(i + 1)
                    for s in range(AHEAD):
                        weigh(i + 1, s, link)
                    for s in range(AHEAD):
                        share_out(i + 1, s, link)
                    assert link.n == LINKS, link.n
                for t in range(G):
                    add(i, t)

            dve.sem_inc(shifted, R)
            every_last = ctxT[:, S2 - 1:KEYS:S2]
            link = Chain(dve, dve_chain, 0, passed)
            row_stats(0, link)
            if layer == 0:
                dve.wait_ge(rows_loaded, 16)
                dve.tensor_reduce(any_row[:, :], mask_rows[:, :], AX_X, ALU.max).then_inc(any_ready, 1)
                dve.wait_ge(any_ready, 1)
                dve.tensor_scalar(any_diag[:, :], ident[0:B, 0:B], any_row[:, 0:1], None, ALU.mult).then_inc(any_ready, 1)
            normalize(0)
            if layer == 0:
                dve.wait_ge(any_spread, 1)
                dve.tensor_copy(any_key[:, :], misc_ps[1][:, 0:B]).then_inc(any_ready, 1)
                dve.wait_ge(any_ready, 3)
                dve.tensor_tensor(last_ctx[:, :], every_last, any_key[:, :], ALU.mult).then_inc(last_ready, 1)
            else:
                dve.tensor_copy(last_ctx[:, :], every_last).then_inc(last_ready, 1)
            if layer == 1:
                sum_squares(0)
            keep_queries(0)
            for s in range(AHEAD):
                weigh(0, s, link)
            for s in range(AHEAD):
                share_out(0, s, link)
            assert link.n == FIRST, link.n
            with dve.Fori(0, ITERS - 1) as i:
                iteration(i, False)
            iteration(ITERS - 1, True)

        @block.gpsimd
        def _(pool):
            LINKS = 1 + NB if layer == 0 else 1 + 2
            FIRST = 1 if layer == 0 else 1 + 2

            def norm_scale(g, link):
                pool.wait_ge(var_ready, g + 1)
                apart(pool, pool_passed)
                link(pool.tensor_scalar(rstd[:, :], mv[:, :, 1], LN_EPS, None, ALU.add))
                pool.tensor_tensor(rstd[:, :], rstd[:, :], minus_half[:, 0:G], ALU.pow).then_inc(rstd_ready, 1)

            def mask_bias(i, b, link):
                pool.wait_ge(bias_ready, i * NB + b)
                pool.wait_ge(shifted, (i * NB + b) * R)
                apart(pool, pool_passed)
                link(pool.tensor_copy(valid[:, :], mask[:, bass.ds(i * NB + b, 1), :].rearrange("p a s -> p (a s)")),
                     alone=True)
                pool.tensor_scalar(bias[:, b % 2, :], valid[:, :], 1.0, -1e30, ALU.subtract, ALU.mult
                                   ).then_inc(bias_ready, 1)

            def less_last(i, b):
                pool.wait_ge(keys_loaded[b % RING], i * (32 * NB // RING) + 32 * (b // RING + 1))
                apart(pool, pool_passed)
                pool.tensor_tensor(keys[:, b % RING], keys[:, b % RING],
                                   last_key[:, b % RING, :].unsqueeze(1).broadcast_to([P, KB, DC]), ALU.subtract
                                   ).then_inc(keys_ready, 1)

            def row_scales(g, link):
                flat = q_rms[:, :, :].rearrange("p g h -> p (g h)")
                pool.wait_ge(n_summed, g * (G * NQ) + G * NQ)
                apart(pool, pool_passed)
                link(pool.tensor_scalar(flat, q_sum[:, :, :].rearrange("p g h -> p (g h)"), 1.0 / HD, LN_EPS,
                                        ALU.mult, ALU.add))
                link(pool.tensor_tensor(flat, flat, minus_half[:, :], ALU.pow), alone=True)
                for b in range(BT):
                    for j in range(HR):
                        ins = pool.tensor_scalar(
                            row_scale[j * T:(j + 1) * T, :, b, :],
                            q_rms[b * T:(b + 1) * T, :, :].rearrange("p g (r j) -> p g r j", j=HR)[:, :, :, j],
                            SCALE, None, ALU.mult)
                ins.then_inc(rows_ready, 1)
                pool.wait_ge(rows_ready, g + 1)
                apart(pool, pool_passed)

            def iteration(i, last):
                link = Chain(pool, pool_chain, i * LINKS + FIRST, pool_passed)
                for b in range(NB):
                    if layer == 0:
                        mask_bias(i, b, link)
                    less_last(i, b)
                    if b == NB // 2 + 1 and not last:
                        norm_scale(i + 1, link)
                if layer == 1 and not last:
                    row_scales(i + 1, link)
                assert last or link.n == LINKS, link.n

            pool.memset(minus_half[:, :], -0.5).then_inc(begun, 1)
            pool.wait_ge(begun, 1)
            link = Chain(pool, pool_chain, 0, pool_passed)
            norm_scale(0, link)
            if layer == 0:
                pool.memset(ones[:, :], 1.0).then_inc(ones_set, 1)
                pool.wait_ge(pre_loaded, 16)
            if layer == 1:
                row_scales(0, link)
            assert link.n == FIRST, link.n
            with pool.Fori(0, ITERS - 1) as i:
                iteration(i, False)
            iteration(ITERS - 1, True)


def row_stats(dve, x_tile, stats, mv, link):
    link(dve.bn_stats(stats[:, :], x_tile), alone=True)
    return dve.bn_aggr(mv[:, :], stats[:, :])


def rstd_of(pool, mv, rstd, minus_half, link):
    link(pool.tensor_scalar(rstd[:, :], mv[:, 1:2], LN_EPS, None, ALU.add))
    return pool.tensor_tensor(rstd[:, :], rstd[:, :], minus_half[:, :], ALU.pow)


def own_scores(act, blocks, score_ps, b):
    q = slice(b * T, (b + 1) * T)
    return act.activation(blocks[q, :, :], score_ps[q, :, q], ACT.Copy)


def per_head(x, n=T):
    return x.unsqueeze(2).broadcast_to([P, H, n])


def self_attention(nc, I, x_sb, ident):
    with ExitStack() as ctx:
        sc = Scope(nc, ctx, "sa0")
        HC = AH // NC
        HEAD_STEP = P + AD
        w_rows, out_rows = sc.sb("w_rows", [P, 3 * NC, D]), sc.sb("out_rows", [P, NC, D])
        wT, outT = sc.sb("wT", [P, NC, 3 * D]), sc.sb("outT", [P, NC, D])
        bias_qkv, bias_out = sc.sb("bias_qkv", [P, 3 * NC]), sc.sb("bias_out", [P, D])
        head_mask = sc.sb("head_mask", [P, HC])
        stats, mv, rstd, minus_half = sc.sb("stats", [P, 6]), sc.sb("mv", [P, 2]), sc.sb("rstd", [P, 1]), sc.sb("minus_half", [P, 1])
        xn, xnT = sc.sb("xn", [P, D]), sc.sb("xnT", [P, 2, NC, P])
        qkT, k_heads = sc.sb("qkT", [P, 2, 2 * NC, P]), sc.sb("k_heads", [P, 2, AH, P])
        v_heads = sc.sb("v_heads", [P, 2, NC, HC * HEAD_STEP])
        blocks, top, total = sc.sb("blocks", [P, AH, T]), sc.sb("top", [P, AH]), sc.sb("total", [P, AH])
        probsT, mixT = sc.sb("probsT", [P, 2, AH, P]), sc.sb("mixT", [P, NC, P])
        score_ps = sc.ps("score", [P, AH, P])
        turn_ps, qk_ps, v_ps, mix_ps = sc.ps("turn"), sc.ps("qk"), sc.ps("v"), sc.ps("mix")

        loaded, mask_step = sc.sem("loaded"), sc.sem("mask_step")
        w_turned, w_kept, zeroed, half_set = sc.sem("w_turned"), sc.sem("w_kept"), sc.sem("zeroed"), sc.sem("half_set")
        passed, dve_chain, pool_chain = sc.sem("passed"), sc.sem("dve_chain"), sc.sem("pool_chain")
        var_ready, rstd_ready, normed = sc.sem("var_ready"), sc.sem("rstd_ready"), sc.sem("normed")
        x_turned, xnT_ready = sc.sem("x_turned"), sc.sem("xnT_ready")
        qk_made, qk_kept, heads_ready = sc.sem("qk_made"), sc.sem("qk_kept"), sc.sem("heads_ready")
        v_made, v_kept, scored, blocks_kept = sc.sem("v_made"), sc.sem("v_kept"), sc.sem("scored"), sc.sem("blocks_kept")
        shifted, exped, probsT_ready = sc.sem("shifted"), sc.sem("exped"), sc.sem("probsT_ready")
        mixed, mixT_ready, projected, added = sc.sem("mixed"), sc.sem("mixT_ready"), sc.sem("projected"), sc.sem("added")
        block = sc.block()
        TURNS = NT - 2
        assert TURNS % 2 == 0

        def turns(eng, turn):
            with eng.Fori(0, TURNS // 2) as i:
                turn(i * 2 + 1, 1)
                turn(i * 2 + 2, 0)

        @block.sync
        def _(sp):
            sp.dma_start(w_rows[:, :, :], I["L0_attn_Wqkv_w"].rearrange("(c p) d -> p c d", p=P)).then_inc(loaded, 16)
            sp.dma_start(out_rows[:, :, :], I["L0_attn_out_w"].rearrange("(c p) d -> p c d", p=P)).then_inc(loaded, 16)
            with nc.allow_non_contiguous_dma(reason="one bias per partition"):
                sp.dma_start(bias_qkv[:, :], I["L0_attn_Wqkv_b"].rearrange("(c p) -> p c", p=P)).then_inc(loaded, 16)
            sp.dma_start(bias_out[:, :], I["L0_attn_out_b"].partition_broadcast(P)).then_inc(loaded, 16)
            sp.wait_ge(loaded, 64)

        @block.tensor
        def _(pe):
            def turn_x(n):
                pe.wait_ge(normed, n + 1)
                pe.wait_ge(xnT_ready, n)
                for c in range(NC):
                    ins = pe.transpose(turn_ps[:, c * P:(c + 1) * P], xn[:, c * P:(c + 1) * P], ident[:, :])
                ins.then_inc(x_turned, 1)

            def project_qk(n, odd):
                pe.wait_ge(xnT_ready, n + 1)
                pe.wait_ge(qk_kept, 2 * NC * n)
                for m in range(2 * NC):
                    for c in range(NC):
                        ins = pe.matmul(qk_ps[:, m * P:(m + 1) * P], wT[:, c, m * P:(m + 1) * P], xnT[:, odd, c, :],
                                        start=(c == 0), stop=(c == NC - 1))
                ins.then_inc(qk_made, 1)

            def project_v(n, odd):
                pe.wait_ge(v_kept, n)
                for c in range(NC):
                    ins = pe.matmul(v_ps[:, 0:D], xnT[:, odd, c, :], wT[:, c, 2 * D:3 * D], start=(c == 0), stop=(c == NC - 1))
                ins.then_inc(v_made, 1)

            def score(n, odd):
                pe.wait_ge(heads_ready, NC * n + NC)
                pe.wait_ge(qk_kept, 2 * NC * (n + 1))
                pe.wait_ge(blocks_kept, BT * n)
                for m in range(AH // 4):
                    ins = pe.matmul(score_ps[:, 4 * m:4 * m + 4, :], qkT[:, odd, m * 4 // HC, :],
                                    k_heads[:, odd, 4 * m:4 * m + 4, :], start=True, stop=True)
                ins.then_inc(scored, 1)

            def mix(n, odd):
                pe.wait_ge(probsT_ready, n + 1)
                pe.wait_ge(v_kept, n + 1)
                pe.wait_ge(added, n)
                for h in range(AH):
                    c, j = h // HC, h % HC
                    ins = pe.matmul(mix_ps[:, c * P:(c + 1) * P], v_heads[:, odd, c, j * P:(j + 1) * P], probsT[:, odd, h, :],
                                    start=(j == 0), stop=(j == HC - 1))
                ins.then_inc(mixed, 1)

            def project_out(n):
                pe.wait_ge(mixT_ready, n + 1)
                for c in range(NC):
                    ins = pe.matmul(mix_ps[:, D:2 * D], mixT[:, c, :], outT[:, c, :], start=(c == 0), stop=(c == NC - 1))
                ins.then_inc(projected, 1)

            pe.wait_ge(loaded, 64)
            for m in range(3 * NC + NC):
                if m > 1:
                    pe.wait_ge(w_kept, m - 1)
                src = w_rows[:, m, :] if m < 3 * NC else out_rows[:, m - 3 * NC, :]
                for c in range(NC):
                    ins = pe.transpose((turn_ps, mix_ps)[m % 2][:, c * P:(c + 1) * P], src[:, c * P:(c + 1) * P], ident[:, :])
                ins.then_inc(w_turned, 1)
            pe.wait_ge(w_kept, 4 * NC)
            pe.wait_ge(zeroed, 2)
            turn_x(0)
            project_qk(0, 0)
            project_v(0, 0)
            turn_x(1)
            project_qk(1, 1)
            score(0, 0)
            turn_x(2)
            project_v(1, 1)

            def turn(n, odd):
                project_qk(n + 1, 1 - odd)
                score(n, odd)
                turn_x(n + 2)
                mix(n - 1, 1 - odd)
                project_v(n + 1, 1 - odd)
                project_out(n - 1)

            turns(pe, turn)
            score(NT - 1, 1)
            for n in (NT - 2, NT - 1):
                mix(n, n % 2)
                project_out(n)

        @block.scalar
        def _(act):
            def keep_xnT(n, odd):
                act.wait_ge(x_turned, n + 1)
                act.activation(xnT[:, odd, :, :], turn_ps[:, 0:D].rearrange("p (c t) -> p c t", c=NC), ACT.Copy).then_inc(xnT_ready, 1)

            def keep_qk(n, odd):
                act.wait_ge(qk_made, n + 1)
                for m in range(2 * NC):
                    act.activation(qkT[:, odd, m, :], qk_ps[:, m * P:(m + 1) * P], ACT.Identity, bias=bias_qkv[:, m:m + 1]
                                   ).then_inc(qk_kept, 1)

            def keep_v(n, odd):
                act.wait_ge(v_made, n + 1)
                ins = act.activation(v_heads[:, odd, :, :].rearrange("p c (j s) -> p c j s", s=HEAD_STEP)[:, :, :, 0:AD],
                                     v_ps[:, 0:D].rearrange("p (c j a) -> p c j a", c=NC, j=HC), ACT.Copy)
                ins.then_inc(v_kept, 1)

            def keep_blocks(n):
                act.wait_ge(scored, n + 1)
                act.wait_ge(probsT_ready, n)
                for b in range(BT):
                    own_scores(act, blocks, score_ps, b).then_inc(blocks_kept, 1)

            def exp(n):
                act.wait_ge(shifted, n + 1)
                act.activation(blocks[:, :, :], blocks[:, :, :], ACT.Exp, scale=float(AD) ** -0.5).then_inc(exped, 1)

            def keep_mixT(n):
                act.wait_ge(projected, n)
                act.wait_ge(mixed, n + 1)
                for c in range(NC):
                    ins = act.activation(mixT[:, c, :], mix_ps[:, c * P:(c + 1) * P], ACT.Identity,
                                         bias=bias_qkv[:, 2 * NC + c:2 * NC + c + 1])
                ins.then_inc(mixT_ready, 1)

            for m in range(4 * NC):
                act.wait_ge(w_turned, m + 1)
                dst = wT[:, :, m * P:(m + 1) * P] if m < 3 * NC else outT[:, :, (m - 3 * NC) * P:(m - 3 * NC + 1) * P]
                act.activation(dst, (turn_ps, mix_ps)[m % 2][:, 0:D].rearrange("p (c t) -> p c t", c=NC), ACT.Copy).then_inc(w_kept, 1)
            act.wait_ge(zeroed, 2)
            keep_xnT(0, 0)
            keep_qk(0, 0)
            keep_v(0, 0)
            keep_xnT(1, 1)
            keep_qk(1, 1)
            keep_blocks(0)
            keep_xnT(2, 0)
            exp(0)
            keep_v(1, 1)

            def turn(n, odd):
                keep_qk(n + 1, 1 - odd)
                keep_blocks(n)
                keep_xnT(n + 2, odd)
                exp(n)
                keep_mixT(n - 1)
                keep_v(n + 1, 1 - odd)

            turns(act, turn)
            keep_blocks(NT - 1)
            exp(NT - 1)
            keep_mixT(NT - 2)
            keep_mixT(NT - 1)

        @block.vector
        def _(dve):
            LINKS = 6
            FIRST = 8

            def tile_of(n):
                return x_sb[:, bass.ds(n, 1), :].rearrange("p a d -> p (a d)")

            def stats_of(n, link):
                row_stats(dve, tile_of(n), stats, mv, link).then_inc(var_ready, 1)

            def normalize(n):
                dve.wait_ge(rstd_ready, n + 1)
                dve.wait_ge(x_turned, n)
                dve.tensor_scalar(xn[:, :], tile_of(n), mv[:, 0:1], rstd[:, 0:1], ALU.subtract, ALU.mult).then_inc(normed, 1)

            def shift(n, link):
                dve.wait_ge(blocks_kept, BT * n + BT)
                link(dve.tensor_reduce(top[:, :], blocks[:, :, :], AX_X, ALU.max))
                dve.tensor_tensor(blocks[:, :, :], blocks[:, :, :], per_head(top[:, :]), ALU.subtract).then_inc(shifted, 1)

            def divide(n, odd, link):
                dve.wait_ge(exped, n + 1)
                link(dve.tensor_reduce(total[:, :], blocks[:, :, :], AX_X, ALU.add))
                link(dve.reciprocal(total[:, :], total[:, :]))
                link(dve.tensor_tensor(blocks[:, :, :], blocks[:, :, :], per_head(total[:, :]), ALU.mult))
                if not isinstance(n, int) or n > 1:
                    dve.wait_ge(mixed, n - 1)
                for b in range(BT):
                    q = slice(b * T, (b + 1) * T)
                    ins = dve.transpose(probsT[q, odd, :, q], blocks[q, :, :])
                ins.then_inc(probsT_ready, 1)

            def add(n, link):
                link(dve.tensor_tensor(tile_of(n), tile_of(n), bias_out[:, :], ALU.add))
                dve.wait_ge(projected, n + 1)
                dve.tensor_tensor(tile_of(n), tile_of(n), mix_ps[:, D:2 * D], ALU.add).then_inc(added, 1)

            dve.memset(probsT[:, :, :, :], 0.0).then_inc(zeroed, 1)
            dve.memset(v_heads[:, :, :, :], 0.0).then_inc(zeroed, 1)
            dve.wait_ge(zeroed, 2)
            dve.wait_ge(loaded, 64)
            link = Chain(dve, dve_chain, 0, passed)
            for n in range(3):
                stats_of(n, link)
                normalize(n)
            shift(0, link)
            stats_of(3, link)
            divide(0, 0, link)
            assert link.n == FIRST, link.n

            def turn(n, odd):
                link = Chain(dve, dve_chain, (n - 1) * LINKS + FIRST, passed)
                normalize(n + 2)
                shift(n, link)
                stats_of(n + 3, link)
                divide(n, odd, link)
                add(n - 1, link)
                assert link.n == LINKS, link.n

            turns(dve, turn)
            link = Chain(dve, dve_chain, TURNS * LINKS + FIRST, passed)
            shift(NT - 1, link)
            divide(NT - 1, 1, link)
            add(NT - 2, link)
            add(NT - 1, link)

        @block.gpsimd
        def _(pool):
            pool.memset(minus_half[:, :], -0.5).then_inc(half_set, 1)
            pool.memset(head_mask[:, :], 1.0).then_inc(mask_step, 1)
            pool.wait_ge(mask_step, 1)
            pool.affine_select(out=head_mask[:, :], in_=head_mask[:, :], compare_op=ALU.is_ge, fill=0.0, base=0,
                               pattern=[[-AD, HC]], channel_multiplier=1).then_inc(mask_step, 1)
            pool.wait_ge(mask_step, 2)
            pool.affine_select(out=head_mask[:, :], in_=head_mask[:, :], compare_op=ALU.is_ge, fill=0.0, base=AD - 1,
                               pattern=[[AD, HC]], channel_multiplier=-1).then_inc(mask_step, 1)
            pool.wait_ge(mask_step, 3)
            pool.wait_ge(half_set, 1)

            def scale_of(n):
                link = Chain(pool, pool_chain, n, passed)
                pool.wait_ge(var_ready, n + 1)
                apart(pool, passed)
                rstd_of(pool, mv, rstd, minus_half, link).then_inc(rstd_ready, 1)

            def mask_keys(n, odd):
                for c in range(NC):
                    if not isinstance(n, int) or n > 1:
                        pool.wait_ge(scored, n - 1)
                    pool.wait_ge(qk_kept, 2 * NC * n + NC + c + 1)
                    pool.tensor_tensor(k_heads[:, odd, c * HC:(c + 1) * HC, :],
                                       qkT[:, odd, NC + c, :].unsqueeze(1).broadcast_to([P, HC, P]),
                                       head_mask[:, :].unsqueeze(2).broadcast_to([P, HC, P]), ALU.mult).then_inc(heads_ready, 1)

            scale_of(0)
            scale_of(1)
            mask_keys(0, 0)
            scale_of(2)
            mask_keys(1, 1)
            scale_of(3)

            def turn(n, odd):
                mask_keys(n + 1, 1 - odd)
                scale_of(n + 3)

            turns(pool, turn)


def route(nc, I, x_sb, ident, slot_rows, slot_out, slots_all, weights_all, ctxT, wk, sums, rk_dram):
    with ExitStack() as ctx:
        sc = Scope(nc, ctx, "rt")
        router, routerT = sc.sb("router", [E0, D]), sc.sb("routerT", [P, NC, E0])
        upto, ones, slot_base = sc.sb("upto", [P, P]), sc.sb("ones", [P, P]), sc.sb("slot_base", [P, E0])
        zeros = sc.sb("zeros", [P, 2048])
        stats, mv, rstd, minus_half = sc.sb("stats", [P, 6]), sc.sb("mv", [P, 2]), sc.sb("rstd", [P, 1]), sc.sb("minus_half", [P, 1])
        xn, xnT = sc.sb("xn", [P, 2, D]), sc.sb("xnT", [P, NC, P])
        prob, rest, chosen, before = (sc.sb(n, [P, E0]) for n in ("prob", "rest", "chosen", "before"))
        gate, code, picked = sc.sb("gate", [P, E0]), sc.sb("code", [P, E0]), sc.sb("picked", [P, K0, E0])
        top, best, scale = sc.sb("top", [P, 1]), sc.sb("best", [P, K0]), sc.sb("scale", [P, 2])
        codes = sc.sb("codes", [P, K0])
        places = sc.sb("places", [P, 2, K0], U32)
        norms = KeyNorms(sc, I, ident, ctxT, wk, sums, rk_dram, 0)
        turn_ps, logit_ps, place_ps = sc.ps("turn"), sc.ps("logit"), sc.ps("place")
        loaded, w_turned, w_kept = sc.sem("loaded"), sc.sem("w_turned"), sc.sem("w_kept")
        const_step, consts_ready, zeroed, cleared = sc.sem("const_step"), sc.sem("consts_ready"), sc.sem("zeroed"), sc.sem("cleared")
        passed, dve_chain, pool_chain = sc.sem("passed"), sc.sem("dve_chain"), sc.sem("pool_chain")
        var_ready, rstd_ready, normed = sc.sem("var_ready"), sc.sem("rstd_ready"), sc.sem("normed")
        x_turned, xnT_ready, routed = sc.sem("x_turned"), sc.sem("xnT_ready"), sc.sem("routed")
        shifted, exped, chosen_ready, counted = sc.sem("shifted"), sc.sem("exped"), sc.sem("chosen_ready"), sc.sem("counted")
        places_ready = sc.sem("places_ready")
        sums_set = sc.sem("sums_set")
        scattered = [sc.pool_dma_sem(f"scattered{p}") for p in range(2)]
        block = sc.block()
        U = 2
        ITERS = NT // U

        @block.sync
        def _(sp):
            sp.dma_start(router[:, :], I["L0_ffn_router_w"]).then_inc(loaded, 16)
            norms.load(sp)
            sp.wait_ge(zeroed, 1)
            per = zeros.shape[1] * P
            flat = slot_rows.rearrange("(n p r) d -> n p (r d)", p=P, r=2048 // D)
            for n in range(SLOTS * D // per):
                sp.dma_start(flat[n], zeros[:, :]).then_inc(cleared, 16)
            sp.dma_start(slot_out[SLOTS:SLOTS + 1, :], zeros[0:1, 0:D]).then_inc(cleared, 16)
            sp.wait_ge(cleared, 16 * (SLOTS * D // per + 1))
            with sp.Fori(0, NT) as n:
                norms.store(sp, n)
            sp.wait_ge(norms.rk_stored, 16 * NT)

        @block.tensor
        def _(pe):
            pe.wait_ge(loaded, 16)
            for c in range(NC):
                ins = pe.transpose(turn_ps[:, c * E0:(c + 1) * E0], router[:, c * P:(c + 1) * P], ident[0:E0, 0:E0])
            ins.then_inc(w_turned, 1)
            pe.wait_ge(w_kept, 1)
            pe.wait_ge(consts_ready, 1)
            norms.begin_pe(pe)
            pe.wait_ge(norms.wk_loaded, 16)

            def turn_x(n, u):
                pe.wait_ge(normed, n + 1)
                pe.wait_ge(xnT_ready, n)
                for c in range(NC):
                    ins = pe.transpose(turn_ps[:, c * P:(c + 1) * P], xn[:, u, c * P:(c + 1) * P], ident[:, :])
                ins.then_inc(x_turned, 1)

            turn_x(0, 0)
            with pe.Fori(0, ITERS) as i:
                for u in range(U):
                    n = i * U + u
                    norms.keys(pe, n, u, 0)
                    pe.wait_ge(xnT_ready, n + 1)
                    pe.wait_ge(exped, n)
                    for c in range(NC):
                        ins = pe.matmul(logit_ps[:, 0:E0], xnT[:, c, :], routerT[:, c, :], start=(c == 0), stop=(c == NC - 1))
                    ins.then_inc(routed, 1)
                    norms.keys(pe, n, u, 1)
                    norms.keys(pe, n, u, 2)
                    pe.wait_ge(chosen_ready, n + 1)
                    pe.wait_ge(places_ready, n)
                    pe.matmul(place_ps[:, 0:E0], upto[:, :], chosen[:, :], start=True, stop=False)
                    pe.matmul(place_ps[:, 0:E0], ones[:, :], before[:, :], start=False, stop=True).then_inc(counted, 1)
                    norms.keys(pe, n, u, 3)
                    turn_x(n + 1, 1 - u)
                    norms.turn(pe, n)

        @block.scalar
        def _(act):
            act.wait_ge(w_turned, 1)
            act.activation(routerT[:, :, :], turn_ps[:, 0:NC * E0].rearrange("p (c e) -> p c e", c=NC), ACT.Copy).then_inc(w_kept, 1)
            norms.begin_act(act)

            def keep_xnT(n):
                act.wait_ge(x_turned, n + 1)
                act.wait_ge(routed, n)
                act.activation(xnT[:, :, :], turn_ps[:, 0:D].rearrange("p (c t) -> p c t", c=NC), ACT.Copy).then_inc(xnT_ready, 1)

            keep_xnT(0)
            with act.Fori(0, ITERS) as i:
                for u in range(U):
                    n = i * U + u
                    norms.square(act, n, u, 0)
                    act.wait_ge(shifted, n + 1)
                    act.activation(prob[:, :], logit_ps[:, 0:E0], ACT.Exp, bias=top[:, 0:1], accum_out=scale[:, 0:1]).then_inc(exped, 1)
                    norms.square(act, n, u, 1)
                    norms.take_root(act, n, u)
                    norms.square(act, n, u, 2)
                    norms.square(act, n, u, 3)
                    keep_xnT(n + 1)

        @block.vector
        def _(dve):
            LINKS = 12
            dve.memset(before[:, :], 0.0).then_inc(const_step, 1)
            dve.memset(sums[:, 1, :, :], 0.0).then_inc(sums_set, 1)
            dve.wait_ge(sums_set, 1)
            norms.begin_dve(dve)

            def stats_of(n, link):
                row_stats(dve, x_sb[:, bass.ds(n, 1), :].rearrange("p a d -> p (a d)"), stats, mv, link).then_inc(var_ready, 1)

            def normalize(n, u, uses):
                dve.wait_ge(rstd_ready, n + 1)
                dve.wait_ge(scattered[u], uses)
                dve.tensor_scalar(xn[:, u, :], x_sb[:, bass.ds(n, 1), :].rearrange("p a d -> p (a d)"), mv[:, 0:1], rstd[:, 0:1],
                                  ALU.subtract, ALU.mult).then_inc(normed, 1)

            stats_of(0, Chain(dve, dve_chain, 0, passed))
            dve.wait_ge(consts_ready, 1)
            normalize(0, 0, 0)
            with dve.Fori(0, ITERS) as i:
                for u in range(U):
                    n = i * U + u
                    link = Chain(dve, dve_chain, n * LINKS + 1, passed)
                    stats_of(n + 1, link)
                    for q in range(norms.NQ):
                        if q == norms.NQ // 2:
                            dve.wait_ge(routed, n + 1)
                            dve.tensor_reduce(top[:, :], logit_ps[:, 0:E0], AX_X, ALU.max, negate=True).then_inc(shifted, 1)
                        norms.sum_bank(dve, n, u, 0, q)
                    dve.wait_ge(exped, n + 1)
                    link(dve.reciprocal(scale[:, 1:2], scale[:, 0:1]))
                    link(dve.tensor_scalar(prob[:, :], prob[:, :], scale[:, 1:2], None, ALU.mult), alone=True)
                    link(dve.max(best[:, :], prob[:, :]), alone=True)
                    link(dve.match_replace(rest[:, :], best[:, :], prob[:, :], -1.0))
                    dve.tensor_tensor(chosen[:, :], prob[:, :], rest[:, :], ALU.not_equal).then_inc(chosen_ready, 1)
                    norms.sum(dve, n, u, 1)
                    link(dve.tensor_reduce(scale[:, 0:1], best[:, :], AX_X, ALU.add))
                    link(dve.tensor_scalar(scale[:, 0:1], scale[:, 0:1], 1e-20, None, ALU.add))
                    link(dve.reciprocal(scale[:, 1:2], scale[:, 0:1]))
                    dve.tensor_scalar(gate[:, :], prob[:, :], scale[:, 1:2], None, ALU.mult)
                    normalize(n + 1, 1 - u, (i + u) * (16 * K0))
                    dve.wait_ge(counted, n + 1)
                    dve.tensor_tensor(code[:, :], slot_base[:, :], place_ps[:, 0:E0], ALU.subtract)
                    dve.tensor_tensor(before[:, :], before[:, :], chosen[:, :], ALU.add)
                    link(dve.scalar_tensor_tensor(out=picked[:, 0, :], in0=place_ps[:, 0:E0], scalar=float(CAP), in1=chosen[:, :],
                                                  op0=ALU.is_le, op1=ALU.mult))
                    link(dve.tensor_tensor(code[:, :], code[:, :], picked[:, 0, :], ALU.mult), alone=True)
                    link(dve.max(codes[:, :], code[:, :]))
                    dve.tensor_scalar(slots_all[:, bass.ds(n, 1), :].rearrange("p a k -> p (a k)"), codes[:, :], -1.0,
                                      float(NOWHERE), ALU.mult, ALU.add)
                    dve.tensor_scalar(places[:, u, :], codes[:, :], -1.0, float(NOWHERE), ALU.mult, ALU.add
                                      ).then_inc(places_ready, 1)
                    norms.invert(dve, n)
                    for k in range(K0):
                        ins = dve.scalar_tensor_tensor(out=picked[:, k, :], in0=code[:, :], scalar=codes[:, k:k + 1], in1=gate[:, :],
                                                       op0=ALU.is_equal, op1=ALU.mult,
                                                       accum_out=weights_all[:, bass.ds(n * K0 + k, 1)])
                    link(ins)
                    norms.sum(dve, n, u, 2)
                    norms.sum(dve, n, u, 3)
                    norms.keep(dve, n)
                    assert link.n == LINKS, link.n

        @block.gpsimd
        def _(pool):
            pool.memset(zeros[:, :], 0.0).then_inc(zeroed, 1)
            pool.memset(minus_half[:, :], -0.5).then_inc(const_step, 1)
            pool.memset(ones[:, :], 1.0).then_inc(const_step, 1)
            pool.memset(upto[:, :], 1.0).then_inc(const_step, 1)
            pool.iota(slot_base[:, :], pattern=[[-CAP, E0]], base=NOWHERE + 1, channel_multiplier=0,
                      allow_small_or_imprecise_dtypes=True).then_inc(const_step, 1)
            pool.wait_ge(const_step, 5)
            pool.affine_select(out=upto[:, :], in_=upto[:, :], compare_op=ALU.is_ge, fill=0.0, base=0,
                               pattern=[[1, P]], channel_multiplier=-1).then_inc(consts_ready, 1)

            def scale_of(n):
                link = Chain(pool, pool_chain, n, passed)
                pool.wait_ge(var_ready, n + 1)
                apart(pool, passed)
                rstd_of(pool, mv, rstd, minus_half, link).then_inc(rstd_ready, 1)

            scale_of(0)
            norms.put(pool, 0, 0)
            pool.wait_ge(cleared, 16 * (SLOTS * D // (2048 * P) + 1))
            with pool.Fori(0, ITERS) as i:
                for u in range(U):
                    n = i * U + u
                    scale_of(n + 1)
                    norms.put(pool, n + 1, 1 - u)
                    pool.wait_ge(places_ready, n + 1)
                    apart(pool, passed)
                    for k in range(K0):
                        pool.indirect_dma_start(out=slot_rows, out_offset=bass.IndirectOffsetOnAxis(ap=places[:, u, k:k + 1], axis=0),
                                                in_=xn[:, u, :], in_offset=None, bounds_check=SLOTS - 1, oob_is_err=False
                                                ).then_inc(scattered[u], 16)
            for u in range(U):
                pool.wait_ge(scattered[u], ITERS * 16 * K0)


def experts(nc, I, ident, slot_rows, slot_out, ctxT, wk, sums, rk_dram):
    with ExitStack() as ctx:
        sc = Scope(nc, ctx, "ex")
        BUF = 8
        TURNS = E0 // 2
        ITERS = TURNS // BUF
        HALF = BUF // 2
        PAIR = 2
        assert PAIR * CAP == P
        rows = sc.sb("rows", [P, BUF, D])
        w_in = sc.sb("w_in", [P, BUF, 2, PAIR, NC, F0])
        w_out = sc.sb("w_out", [F0, BUF, PAIR, D])
        rowsT = sc.sb("rowsT", [P, 2, NC, P])
        gate, hidden = sc.sb("gate", [P, 2, F0]), sc.sb("hidden", [P, 2, F0])
        hiddenT, out_rows = sc.sb("hiddenT", [F0, 2, P]), sc.sb("out_rows", [P, 2, D])
        norms = KeyNorms(sc, I, ident, ctxT, wk, sums[:, 0].rearrange("p (s u) h -> p s u h", s=2), rk_dram, NT * GROUP,
                         before=sums[:, 1], banks=2)
        turn_ps, hidden_ps, out_ps = sc.ps("turn"), sc.ps("hidden"), sc.ps("out")
        mid_ps = [sc.ps(f"mid{n}") for n in range(2)]
        loaded = [sc.sem(f"loaded{n}") for n in range(BUF)]
        stored = [sc.pool_dma_sem(f"stored{n}") for n in range(2)]
        turned, rowsT_ready, mid_made, gated, hidden_ready = (sc.sem(n) for n in (
            "turned", "rowsT_ready", "mid_made", "gated", "hidden_ready"))
        hidden_turned, hiddenT_ready = sc.sem("hidden_turned"), sc.sem("hiddenT_ready")
        out_made, out_kept, passed = sc.sem("out_made"), sc.sem("out_kept"), sc.sem("passed")
        block = sc.block()

        def loop(eng, stages, norm_steps):
            def iteration(i):
                for u in range(BUF):
                    for stage, lag in stages:
                        j, v = (i - 1, u - lag + BUF) if u < lag else (i + 1, u - lag - BUF) if u - lag >= BUF else (i, u - lag)
                        if not isinstance(j, int) or 0 <= j < ITERS:
                            stage(j, v)
                    for step in norm_steps[u % HALF]:
                        step(i * 2 + u // HALF, u // HALF)

            iteration(0)
            with eng.Fori(0, ITERS - 2) as i:
                iteration(i + 1)
            iteration(ITERS - 1)
            for n in range(TURNS, TURNS + 2):
                for stage, lag in stages:
                    if lag > n - TURNS:
                        stage(ITERS - 1, n - lag - TURNS + BUF)

        def after_last(eng, sem, i, u, ahead=0):
            n = i * BUF + u - 1 + ahead
            if not isinstance(n, int) or n > 0:
                eng.wait_ge(sem, n)

        @block.sync
        def _(sp):
            with sp.Fori(0, ITERS) as i:
                for u in range(BUF):
                    n = i * BUF + u
                    sp.wait_ge(out_made, n + 1)
                    sp.dma_start(rows[:, u, :], slot_rows[bass.ds(n * P, P), :]).then_inc(loaded[u], 16)
                    for g, name in enumerate(("L0_ffn_w_gate", "L0_ffn_w_up")):
                        sp.dma_start(w_in[:, u, g], I[name].rearrange("e (p j) f -> p e (j f)", j=NC)[:, bass.ds(n * PAIR, PAIR), :]
                                     ).then_inc(loaded[u], 16)
                    sp.dma_start(w_out[:, u], I["L0_ffn_w_down"].rearrange("e f d -> f e d")[:, bass.ds(n * PAIR, PAIR), :]
                                 ).then_inc(loaded[u], 16)

        @block.tensor
        def _(pe):
            def turn(i, u):
                pe.wait_ge(loaded[u], i * 64 + 64)
                after_last(pe, rowsT_ready, i, u, 1)
                for j in range(NC):
                    ins = pe.transpose(turn_ps[:, j * P:(j + 1) * P], rows[:, u, j:D:NC], ident[:, :])
                ins.then_inc(turned, 1)

            def middle(i, u):
                pe.wait_ge(rowsT_ready, i * BUF + u + 1)
                after_last(pe, hidden_ready, i, u)
                for e in range(PAIR):
                    own = slice(e * CAP, (e + 1) * CAP)
                    for j in range(NC):
                        ins = pe.matmul(mid_ps[u % 2][own, 0:2 * F0].rearrange("s (g f) -> s g f", g=2),
                                        rowsT[:, u % 2, j, own], w_in[:, u, :, e, j, :], start=(j == 0), stop=(j == NC - 1))
                ins.then_inc(mid_made, 1)

            def turn_hidden(i, u):
                pe.wait_ge(hidden_ready, i * BUF + u + 1)
                after_last(pe, hiddenT_ready, i, u, 1)
                pe.transpose(hidden_ps[0:F0, 0:P], hidden[:, u % 2, :], ident[:, :]).then_inc(hidden_turned, 1)

            def finish(i, u):
                pe.wait_ge(hiddenT_ready, i * BUF + u + 1)
                after_last(pe, out_kept, i, u, 1)
                for e in range(PAIR):
                    own = slice(e * CAP, (e + 1) * CAP)
                    ins = pe.matmul(out_ps[own, 0:D], hiddenT[:, u % 2, own], w_out[:, u, e, :], start=True, stop=True)
                ins.then_inc(out_made, 1)

            pe.sem_inc(out_made, BUF)
            norms.begin_pe(pe)
            turn(0, 0)
            loop(pe, ((turn, -1), (middle, 0), (turn_hidden, 1), (finish, 2)), (
                (lambda j, slot: norms.keys(pe, j, slot, 0),),
                (),
                (lambda j, slot: norms.keys(pe, j, slot, 1),),
                (lambda j, slot: norms.turn(pe, j),)))

        @block.scalar
        def _(act):
            def keep_rowsT(i, u):
                after_last(act, mid_made, i, u)
                act.wait_ge(turned, i * BUF + u + 1)
                act.activation(rowsT[:, u % 2, :, :], turn_ps[:, 0:D].rearrange("p (j s) -> p j s", j=NC), ACT.Copy
                               ).then_inc(rowsT_ready, 1)

            def silu(i, u):
                after_last(act, hidden_ready, i, u)
                act.wait_ge(mid_made, i * BUF + u + 1)
                act.activation(gate[:, u % 2, :], mid_ps[u % 2][:, 0:F0], ACT.Silu).then_inc(gated, 1)

            norms.begin_act(act)
            keep_rowsT(0, 0)
            loop(act, ((keep_rowsT, -1), (silu, 0)), (
                (lambda j, slot: norms.square(act, j, slot, 0),),
                (lambda j, slot: norms.take_root(act, j, slot),),
                (lambda j, slot: norms.square(act, j, slot, 1),),
                (lambda j, slot: norms.store(act, j),)))
            act.wait_ge(norms.rk_stored, 16 * 2 * ITERS)

        @block.vector
        def _(dve):
            def multiply(i, u):
                after_last(dve, hidden_turned, i, u)
                dve.wait_ge(gated, i * BUF + u + 1)
                dve.tensor_tensor(hidden[:, u % 2, :], mid_ps[u % 2][:, F0:2 * F0], gate[:, u % 2, :], ALU.mult
                                  ).then_inc(hidden_ready, 1)

            def keep_hiddenT(i, u):
                after_last(dve, out_made, i, u, BUF)
                dve.wait_ge(hidden_turned, i * BUF + u + 1)
                dve.tensor_copy(hiddenT[:, u % 2, :], hidden_ps[0:F0, 0:P]).then_inc(hiddenT_ready, 1)

            def keep_out(i, u):
                dve.wait_ge(out_made, i * BUF + (u + 1 + BUF))
                dve.wait_ge(stored[u % 2], i * (16 * BUF // 2) + 16 * (u // 2))
                dve.tensor_copy(out_rows[:, u % 2, :], out_ps[:, 0:D]).then_inc(out_kept, 1)

            norms.begin_dve(dve)
            loop(dve, ((multiply, 0), (keep_hiddenT, 1), (keep_out, 2)), (
                (lambda j, slot: norms.sum(dve, j, slot, 0),),
                (lambda j, slot: norms.invert(dve, j),),
                (lambda j, slot: norms.sum(dve, j, slot, 1),),
                (lambda j, slot: norms.keep(dve, j),)))

        @block.gpsimd
        def _(pool):
            norms.put(pool, 0, 0)
            with pool.Fori(0, ITERS) as i:
                for u in range(BUF):
                    n = i * BUF + u
                    pool.wait_ge(out_kept, n + 1)
                    apart(pool, passed)
                    pool.dma_start(slot_out[bass.ds(n * P, P), :], out_rows[:, u % 2, :]).then_inc(stored[u % 2], 16)
                    if u % HALF == 0:
                        norms.put(pool, i * 2 + (u // HALF + 1), 1 - u // HALF)
            for u in range(2):
                pool.wait_ge(stored[u], 16 * TURNS // 2)


def combine(nc, I, x_sb, ident, slots_all, weights_all, slot_out, ctxT, wk, sums, rk_dram, folded, folded_dram, wq):
    with ExitStack() as ctx:
        sc = Scope(nc, ctx, "cb")
        U = 2
        TILES = NT // 2
        ITERS = NT // TILES
        first = (NT + 4) * GROUP
        GROUPS = (KEYS - REST - first) // GROUP // ITERS
        LAST = GROUPS * ITERS
        places = sc.sb("places", [P, U, K0], U32)
        got = sc.sb("got", [P, U, K0, D])
        norms = KeyNorms(sc, I, ident, ctxT, wk, sums, rk_dram, first)
        CHUNKS = GROUPS * norms.U // TILES
        assert GROUPS % 2 == 0 and CHUNKS * TILES == GROUPS * norms.U and first + LAST * GROUP == KEYS - REST and REST <= P
        placed, gathered = sc.sem("placed"), [sc.pool_dma_sem(f"gathered{u}") for u in range(U)]
        passed, added, ahead_loaded = sc.sem("passed"), sc.sem("added"), sc.sem("ahead_loaded")
        AHEAD = U * K0
        block = sc.block()

        def chunks(i, t):
            for q in range(t * CHUNKS, (t + 1) * CHUNKS):
                g = q // norms.U
                yield i * GROUPS + g, 1 - g % 2, q % norms.U

        @block.sync
        def _(sp):
            sp.dma_start(folded[:, :, :], folded_dram).then_inc(ahead_loaded, 16)
            sp.dma_start(wq[:, :, :], I["L1_xattn_Wq"].rearrange("(c p) n -> p c n", p=P)).then_inc(ahead_loaded, 16)
            sp.wait_ge(ahead_loaded, 32)
            with sp.Fori(0, LAST) as j:
                norms.store(sp, j)
            norms.store(sp, LAST)
            norms.store(sp, LAST + 1, REST)
            sp.wait_ge(norms.rk_stored, 16 * (LAST + 2))

        @block.tensor
        def _(pe):
            norms.begin_pe(pe)
            with pe.Fori(0, ITERS) as i:
                for t in range(TILES):
                    for j, slot, c in chunks(i, t):
                        norms.keys(pe, j, slot, c)
                        if c == norms.U - 1:
                            norms.turn(pe, j)
            norms.keys(pe, LAST, 1, 0, REST)
            norms.turn(pe, LAST)
            norms.turn(pe, LAST + 1)

        @block.scalar
        def _(act):
            norms.begin_act(act)
            with act.Fori(0, ITERS) as i:
                for t in range(TILES):
                    for j, slot, c in chunks(i, t):
                        norms.square(act, j, slot, c)
                        if c == 1:
                            norms.take_root(act, j, slot)
            norms.square(act, LAST, 1, 0, REST)
            norms.take_root(act, LAST, 1)
            norms.take_root(act, LAST + 1, 0, missing=norms.PER - norms.NQ)

        @block.vector
        def _(dve):
            norms.begin_dve(dve)
            dve.sem_inc(added, AHEAD)
            with dve.Fori(0, ITERS) as i:
                for t in range(TILES):
                    n, u = i * TILES + t, t % U
                    tile = x_sb[:, bass.ds(n, 1), :].rearrange("p a d -> p (a d)")
                    choices = iter(range(K0))
                    for step, (j, slot, c) in enumerate(chunks(i, t)):
                        for q in range(norms.NQ):
                            norms.sum_bank(dve, j, slot, c, q)
                            if step >= CHUNKS - K0 // norms.NQ:
                                k = next(choices)
                                if k == 0:
                                    dve.wait_ge(gathered[u], i * (16 * K0 * TILES // U) + 16 * K0 * (t // U + 1))
                                dve.wait_ge(added, n * K0 + (AHEAD + k))
                                dve.scalar_tensor_tensor(out=tile, in0=got[:, u, k, :],
                                                         scalar=weights_all[:, bass.ds(n * K0 + k, 1)],
                                                         in1=tile, op0=ALU.mult, op1=ALU.add).then_inc(added, 1)
                        if c == 1:
                            norms.invert(dve, j)
                        if c == norms.U - 1:
                            norms.keep(dve, j)
            norms.sum(dve, LAST, 1, 0, REST)
            norms.invert(dve, LAST)
            norms.keep(dve, LAST)
            norms.invert(dve, LAST + 1)
            norms.keep(dve, LAST + 1)

        @block.gpsimd
        def _(pool):
            with pool.Fori(0, ITERS) as i:
                for t in range(TILES):
                    n, u = i * TILES + t, t % U
                    for j, slot, c in chunks(i, t):
                        if c == 0:
                            norms.put(pool, j, slot)
                    pool.wait_ge(added, n * K0 + K0)
                    apart(pool, passed)
                    pool.tensor_copy(places[:, u, :], slots_all[:, bass.ds(n, 1), :].rearrange("p a k -> p (a k)")
                                     ).then_inc(placed, 1)
                    pool.wait_ge(placed, n + 1)
                    apart(pool, passed)
                    for k in range(K0):
                        pool.indirect_dma_start(out=got[:, u, k, :], out_offset=None, in_=slot_out,
                                                in_offset=bass.IndirectOffsetOnAxis(ap=places[:, u, k:k + 1], axis=0),
                                                bounds_check=SLOTS, oob_is_err=False).then_inc(gathered[u], 16)
            norms.put(pool, LAST, 1, REST)


def routed_experts(nc, I, x_sb, ident, ctxT, sums, rk_dram, folded, folded_dram, wq):
    with ExitStack() as ctx:
        sc = Scope(nc, ctx, "moe")
        slot_rows = nc.dram_tensor("slot_rows", (SLOTS, D), F32).ap()
        slot_out = nc.dram_tensor("slot_out", (SLOTS + 1, D), F32).ap()
        slots_all, weights_all = sc.sb("slots", [P, NT, K0], U32), sc.sb("weights", [P, NT * K0])
        wk = sc.sb("wk1", [P, H * HD])
        route(nc, I, x_sb, ident, slot_rows, slot_out, slots_all, weights_all, ctxT, wk, sums, rk_dram)
        experts(nc, I, ident, slot_rows, slot_out, ctxT, wk, sums, rk_dram)
        combine(nc, I, x_sb, ident, slots_all, weights_all, slot_out, ctxT, wk, sums, rk_dram, folded, folded_dram, wq)


def self_attention_fp4(nc, I, x_sb, ident, ahead):
    with ExitStack() as ctx:
        sc = Scope(nc, ctx, "sa1")
        G = 4
        NG = H // G
        wq, wk, wv = (sc.sb(n, [P, NC, H * HD]) for n in ("wq", "wk", "wv"))
        wo = sc.sb("wo", [P, H, D])
        W = G * HD
        scales = sc.sb("scales", [P, 4, NC, W])
        bias_q, bias_k, bias_v = (sc.sb(n, [P, H]) for n in ("bias_q", "bias_k", "bias_v"))
        bias_out = sc.sb("bias_out", [P, D])
        stats, mv, rstd, minus_half = sc.sb("stats", [P, 6]), sc.sb("mv", [P, 2]), sc.sb("rstd", [P, 1]), sc.sb("minus_half", [P, 1])
        xn, xnT = sc.sb("xn", [P, D]), sc.sb("xnT", [P, NC, P])
        qT, kT, v = sc.sb("qT", [P, H, P]), sc.sb("kT", [P, H, P]), sc.sb("v", [P, H * HD])
        blocks, top, total = sc.sb("blocks", [P, H, T]), sc.sb("top", [P, H]), sc.sb("total", [P, H])
        probsT, mixT = sc.sb("probsT", [P, H, P]), sc.sb("mixT", [P, H, P])
        score_ps = sc.ps("score", [P, H, P])
        work_ps = [sc.ps(f"work{b}", [P, G, P]) for b in range(2)]
        turn_ps, out_ps = sc.ps("turn"), sc.ps("out")

        codes_loaded, scaled = [sc.sem(f"codes_loaded{j}") for j in range(4)], sc.sem("scaled")
        loaded, zeroed, half_set, ahead_loaded = sc.sem("loaded"), sc.sem("zeroed"), sc.sem("half_set"), sc.sem("ahead_loaded")
        passed, dve_chain, pool_chain = sc.sem("passed"), sc.sem("dve_chain"), sc.sem("pool_chain")
        var_ready, rstd_ready, normed = sc.sem("var_ready"), sc.sem("rstd_ready"), sc.sem("normed")
        x_turned, xnT_ready = sc.sem("x_turned"), sc.sem("xnT_ready")
        q_made, q_kept, k_made, k_kept, v_made, v_kept = (sc.sem(n) for n in (
            "q_made", "q_kept", "k_made", "k_kept", "v_made", "v_kept"))
        scored, blocks_kept, shifted, exped, probsT_ready = (sc.sem(n) for n in (
            "scored", "blocks_kept", "shifted", "exped", "probsT_ready"))
        mixed, mix_kept, projected, added = (sc.sem(n) for n in ("mixed", "mix_kept", "projected", "added"))
        block = sc.block()

        pieces = [(n, g) for g in range(NG) for n in ("wq", "wk")] + [(n, g) for n in ("wv", "wo") for g in range(NG)]
        weights = {"wq": wq, "wk": wk, "wv": wv, "wo": wo}

        def piece(name, g):
            if name == "wo":
                return wo[:, g * G:(g + 1) * G, :], slice(g * G, (g + 1) * G), slice(0, D)
            return weights[name][:, :, g * W:(g + 1) * W], slice(0, NC), slice(g * W, (g + 1) * W)

        def scale_slot(name, m):
            s = scales[:, m % 4, :, :]
            return s.rearrange("p c n -> p (c n)").rearrange("p (h n) -> p h n", n=D) if name == "wo" else s

        @block.sync
        def _(sp):
            PARTS = P // FP4_ROWS
            for m, (name, g) in enumerate(pieces):
                to, chunks, cols = piece(name, g)
                if m >= 4:
                    sp.wait_ge(scaled, m - 3)
                sp.dma_start(to, I[f"L1_attn_{name}_codes"].rearrange("(c p) n -> p c n", p=P)[:, chunks, cols]
                             ).then_inc(codes_loaded[m % 4], 16)
                rows = I[f"L1_attn_{name}_scales"].rearrange("(c b) n -> b c n", b=PARTS)
                for b in range(PARTS):
                    sp.dma_start(scale_slot(name, m)[b * FP4_ROWS:(b + 1) * FP4_ROWS, :, :],
                                 rows[b][chunks, cols].partition_broadcast(FP4_ROWS)).then_inc(codes_loaded[m % 4], 16)
            with nc.allow_non_contiguous_dma(reason="small rows, one bias per partition"):
                for to, what in ahead:
                    sp.dma_start(to, what).then_inc(ahead_loaded, 16)
            sp.wait_ge(ahead_loaded, 16 * len(ahead))

        @block.tensor
        def _(pe):
            def turn_x(n):
                pe.wait_ge(normed, n + 1)
                pe.wait_ge(xnT_ready, n)
                for c in range(NC):
                    ins = pe.transpose(turn_ps[:, c * P:(c + 1) * P], xn[:, c * P:(c + 1) * P], ident[:, :])
                ins.then_inc(x_turned, 1)

            def project_qk(n, first):
                pe.wait_ge(xnT_ready, n + 1)
                for g in range(NG):
                    if first:
                        pe.wait_ge(scaled, 2 * g + 2)
                    for w, ps, kept, made in ((wq, work_ps[0], q_kept, q_made), (wk, work_ps[1], k_kept, k_made)):
                        if g:
                            pe.wait_ge(kept, NG * n + g)
                        else:
                            pe.wait_ge(v_kept, NG * n)
                        for j in range(G):
                            h = g * G + j
                            for c in range(NC):
                                ins = pe.matmul(ps[:, j, :], w[:, c, h * HD:(h + 1) * HD], xnT[:, c, :],
                                                start=(c == 0), stop=(c == NC - 1))
                        ins.then_inc(made, 1)

            def project_v(n, first):
                for g in range(NG):
                    if first:
                        pe.wait_ge(scaled, 2 * NG + g + 1)
                    if g >= 2:
                        pe.wait_ge(v_kept, NG * n + g - 1)
                    elif first:
                        pe.wait_ge(k_kept if g else q_kept, NG)
                    else:
                        pe.wait_ge(mix_kept, NG * n - 1 + g)
                    for c in range(NC):
                        ins = pe.matmul(work_ps[g % 2][:, :, :], xnT[:, c, :], wv[:, c, g * 512:(g + 1) * 512],
                                        start=(c == 0), stop=(c == NC - 1))
                    ins.then_inc(v_made, 1)

            def score(n):
                pe.wait_ge(q_kept, NG * n + NG)
                pe.wait_ge(k_kept, NG * n + NG)
                pe.wait_ge(blocks_kept, n * BT)
                for h in range(H):
                    ins = pe.matmul(score_ps[:, h, :], qT[:, h, :], kT[:, h, :], start=True, stop=True)
                ins.then_inc(scored, 1)

            def mix(n, last):
                pe.wait_ge(probsT_ready, n + 1)
                pe.wait_ge(v_kept, NG * n + NG)
                for g in range(NG):
                    if g >= 2:
                        pe.wait_ge(mix_kept, NG * n + g - 1)
                    elif not last:
                        pe.wait_ge(k_kept if g else q_kept, NG * n + 2 * NG)
                    for j in range(G):
                        h = g * G + j
                        ins = pe.matmul(work_ps[g % 2][:, j, :], v[:, h * HD:(h + 1) * HD], probsT[:, h, :],
                                        start=True, stop=True)
                    ins.then_inc(mixed, 1)

            def project_out(n):
                pe.wait_ge(mix_kept, NG * n + NG)
                pe.wait_ge(added, n)
                for h in range(H):
                    ins = pe.matmul(out_ps[:, 0:D], mixT[:, h, :], wo[:, h, :], start=(h == 0), stop=(h == H - 1))
                ins.then_inc(projected, 1)

            turn_x(0)
            project_qk(0, True)
            project_v(0, True)
            turn_x(1)
            score(0)
            pe.wait_ge(scaled, len(pieces))
            with pe.Fori(0, NT - 1) as i:
                project_qk(i + 1, False)
                mix(i, False)
                project_v(i + 1, False)
                turn_x(i + 2)
                project_out(i)
                score(i + 1)
            mix(NT - 1, True)
            project_out(NT - 1)

        @block.scalar
        def _(act):
            def keep_xnT(n):
                act.wait_ge(x_turned, n + 1)
                act.wait_ge(v_made, NG * n)
                act.activation(xnT[:, :, :], turn_ps[:, 0:D].rearrange("p (c t) -> p c t", c=NC), ACT.Copy).then_inc(xnT_ready, 1)

            def keep_k(n, g):
                act.wait_ge(scored, n)
                act.wait_ge(k_made, NG * n + g + 1)
                for j in range(G):
                    h = g * G + j
                    ins = act.activation(kT[:, h, :], work_ps[1][:, j, :], ACT.Identity, bias=bias_k[:, h:h + 1])
                ins.then_inc(k_kept, 1)

            def keep_v(n):
                for g in range(NG):
                    act.wait_ge(mixed, NG * n)
                    act.wait_ge(v_made, NG * n + g + 1)
                    act.activation(v[:, g * 512:(g + 1) * 512].rearrange("p (j d) -> p j d", j=G), work_ps[g % 2][:, :, :],
                                   ACT.Copy).then_inc(v_kept, 1)

            def keep_blocks(n):
                act.wait_ge(scored, n + 1)
                act.wait_ge(probsT_ready, n)
                for b in range(BT):
                    own_scores(act, blocks, score_ps, b).then_inc(blocks_kept, 1)

            def exp(n):
                act.wait_ge(shifted, n + 1)
                act.activation(blocks[:, :, :], blocks[:, :, :], ACT.Exp, scale=SCALE).then_inc(exped, 1)

            with nc.allow_non_contiguous_dma(reason="one bias per partition"):
                for bias, name in ((bias_q, "bq"), (bias_k, "bk"), (bias_v, "bv")):
                    act.dma_start(bias[:, :], I["L1_attn_" + name].rearrange("(h d) -> d h", d=HD)).then_inc(loaded, 16)
            act.dma_start(bias_out[:, :], I["L1_attn_bo"].partition_broadcast(P)).then_inc(loaded, 16)
            keep_xnT(0)
            act.wait_ge(loaded, 64)
            for g in range(NG):
                keep_k(0, g)
            keep_v(0)
            keep_xnT(1)
            keep_blocks(0)
            with act.Fori(0, NT - 1) as i:
                keep_k(i + 1, 0)
                exp(i)
                for g in range(1, NG):
                    keep_k(i + 1, g)
                keep_v(i + 1)
                keep_xnT(i + 2)
                keep_blocks(i + 1)
            exp(NT - 1)

        @block.vector
        def _(dve):
            LINKS = 6

            def tile_of(n):
                return x_sb[:, bass.ds(n, 1), :].rearrange("p a d -> p (a d)")

            def stats_of(n, link):
                row_stats(dve, tile_of(n), stats, mv, link).then_inc(var_ready, 1)

            def normalize(n):
                dve.wait_ge(rstd_ready, n + 1)
                dve.wait_ge(x_turned, n)
                dve.tensor_scalar(xn[:, :], tile_of(n), mv[:, 0:1], rstd[:, 0:1], ALU.subtract, ALU.mult).then_inc(normed, 1)

            def head_bias(bias, g):
                return bias[:, g * G:(g + 1) * G].unsqueeze(2).broadcast_to([P, G, P])

            def keep_q(n, g):
                dve.wait_ge(scored, n)
                dve.wait_ge(q_made, NG * n + g + 1)
                dve.tensor_tensor(qT[:, g * G:(g + 1) * G, :], work_ps[0][:, :, :], head_bias(bias_q, g), ALU.add
                                  ).then_inc(q_kept, 1)

            def shift(n, link):
                dve.wait_ge(blocks_kept, BT * n + BT)
                link(dve.tensor_reduce(top[:, :], blocks[:, :, :], AX_X, ALU.max))
                dve.tensor_tensor(blocks[:, :, :], blocks[:, :, :], per_head(top[:, :]), ALU.subtract).then_inc(shifted, 1)

            def divide(n, link):
                dve.wait_ge(exped, n + 1)
                link(dve.tensor_reduce(total[:, :], blocks[:, :, :], AX_X, ALU.add))
                link(dve.reciprocal(total[:, :], total[:, :]))
                link(dve.tensor_tensor(blocks[:, :, :], blocks[:, :, :], per_head(total[:, :]), ALU.mult))

            def turn_probs(n):
                dve.wait_ge(mixed, NG * n)
                for b in range(BT):
                    q = slice(b * T, (b + 1) * T)
                    ins = dve.transpose(probsT[q, :, q], blocks[q, :, :])
                ins.then_inc(probsT_ready, 1)

            def keep_mix(n, g):
                dve.wait_ge(projected, n)
                dve.wait_ge(mixed, NG * n + g + 1)
                dve.tensor_tensor(mixT[:, g * G:(g + 1) * G, :], work_ps[g % 2][:, :, :], head_bias(bias_v, g), ALU.add
                                  ).then_inc(mix_kept, 1)

            def add(n, link):
                link(dve.tensor_tensor(tile_of(n), tile_of(n), bias_out[:, :], ALU.add))
                dve.wait_ge(projected, n + 1)
                dve.tensor_tensor(tile_of(n), tile_of(n), out_ps[:, 0:D], ALU.add).then_inc(added, 1)

            dve.memset(probsT[:, :, :], 0.0).then_inc(zeroed, 1)
            dve.wait_ge(zeroed, 1)
            link = Chain(dve, dve_chain, 0, passed)
            for n in range(2):
                stats_of(n, link)
                normalize(n)
            dve.wait_ge(loaded, 64)
            for g in range(NG):
                keep_q(0, g)
            with dve.Fori(0, NT - 1) as i:
                link = Chain(dve, dve_chain, i * LINKS + 2, passed)
                keep_q(i + 1, 0)
                shift(i, link)
                keep_q(i + 1, 1)
                divide(i, link)
                keep_q(i + 1, 2)
                turn_probs(i)
                keep_q(i + 1, 3)
                stats_of(i + 2, link)
                for g in range(NG):
                    keep_mix(i, g)
                normalize(i + 2)
                add(i, link)
                assert link.n == LINKS, link.n
            link = Chain(dve, dve_chain, (NT - 1) * LINKS + 2, passed)
            shift(NT - 1, link)
            divide(NT - 1, link)
            turn_probs(NT - 1)
            for g in range(NG):
                keep_mix(NT - 1, g)
            add(NT - 1, link)

        @block.gpsimd
        def _(pool):
            pool.memset(minus_half[:, :], -0.5).then_inc(half_set, 1)
            pool.wait_ge(half_set, 1)

            def scale_of(n):
                link = Chain(pool, pool_chain, n, passed)
                pool.wait_ge(var_ready, n + 1)
                apart(pool, passed)
                rstd_of(pool, mv, rstd, minus_half, link).then_inc(rstd_ready, 1)

            scale_of(0)
            scale_of(1)
            for m, (name, g) in enumerate(pieces):
                to = piece(name, g)[0]
                pool.wait_ge(codes_loaded[m % 4], 16 * (1 + P // FP4_ROWS) * (m // 4 + 1))
                pool.tensor_tensor(to, to, scale_slot(name, m), ALU.mult).then_inc(scaled, 1)
            with pool.Fori(0, NT - 1) as i:
                scale_of(i + 2)


def dense_weights(nc, sc, I):
    w = dict(gate_w=sc.sb("gate_w", [P, NC, E1]), fc1_b=sc.sb("fc1_b", [P, E1, F1 // P]), fc2_b=sc.sb("fc2_b", [E1, D]),
             alpha=sc.sb("alpha", [P, E1]), fc1=sc.sb("fc1", [P, E1, NC, F1]))
    loads = [(w["gate_w"][:, :, :], I["L1_ffn_gate_w"].rearrange("(c p) e -> p c e", p=P)),
             (w["fc1_b"][:, :, :], I["L1_ffn_fc1_b"].rearrange("e (f p) -> p e f", p=P)),
             (w["fc2_b"][:, :], I["L1_ffn_fc2_b"]),
             (w["alpha"][:, :], I["L1_ffn_alpha"].partition_broadcast(P)),
             (w["fc1"][:, :, :, :], I["L1_ffn_fc1_w"].rearrange("e (c p) f -> p e c f", p=P))]
    return w, loads


def dense_experts(nc, I, x_sb, ident, out, w):
    with ExitStack() as ctx:
        sc = Scope(nc, ctx, "ff1")
        GT = 2
        GROUPS = NT // GT
        U = 2
        ITERS = GROUPS // U
        TOP = 2
        W = 8
        STEPS = E1
        FC = F1 // P
        fc1, fc2 = w["fc1"], sc.sb("fc2", [P, E1, FC, D])
        fc1_b, fc2_b, gate_w, alpha = w["fc1_b"], w["fc2_b"], w["gate_w"], w["alpha"]
        stats, mv, rstd, minus_half = sc.sb("stats", [P, GT, 6]), sc.sb("mv", [P, GT, 2]), sc.sb("rstd", [P, GT]), sc.sb("minus_half", [P, 1])
        xn, xnT = sc.sb("xn", [P, GT, D]), sc.sb("xnT", [P, U, NC, GT, P])
        prob, top, total = sc.sb("prob", [P, GT, E1]), sc.sb("top", [P, GT]), sc.sb("total", [P, GT])
        best, pair, rest = sc.sb("best", [P, GT, W]), sc.sb("pair", [P, GT, W]), sc.sb("rest", [P, GT, E1])
        weight = sc.sb("weight", [P, U, GT, E1])
        weightT = sc.sb("weightT", [E1, GT, P])
        hidden = sc.sb("hidden", [P, 2, FC, GT * P])
        turn_ps = sc.ps("turn", [P, NC, GT, P])
        route_ps, bias_ps = sc.ps("route"), sc.ps("bias", [P, GT, D])
        mid_ps = [sc.ps(f"mid{b}", [P, FC, GT * P]) for b in range(2)]
        out_ps = [sc.ps(f"out{b}", [P, GT, D]) for b in range(2)]

        fc2_loaded = sc.sem("fc2_loaded")
        pair_set, half_set = sc.sem("pair_set"), sc.sem("half_set")
        passed, dve_chain, pool_chain = sc.sem("passed"), sc.sem("dve_chain"), sc.sem("pool_chain")
        var_ready, rstd_ready, normed = sc.sem("var_ready"), sc.sem("rstd_ready"), sc.sem("normed")
        x_turned, xnT_ready, routed, shifted, exped = (sc.sem(n) for n in (
            "x_turned", "xnT_ready", "routed", "shifted", "exped"))
        weighed, weight_turned, weightT_ready, biased, based = (sc.sem(n) for n in (
            "weighed", "weight_turned", "weightT_ready", "biased", "based"))
        mid_made, hidden_ready, out_made, added, stored = (sc.sem(n) for n in (
            "mid_made", "hidden_ready", "out_made", "added", "stored"))
        block = sc.block()

        def tile_of(n):
            return x_sb[:, bass.ds(n, 1), :].rearrange("p a d -> p (a d)")

        @block.sync
        def _(sp):
            sp.dma_start(fc2[:, :, :, :], I["L1_ffn_fc2_w"].rearrange("e (c p) d -> p e c d", p=P)).then_inc(fc2_loaded, 16)
            result = out.rearrange("(n b) t d -> (b t) n d", b=BT)
            with sp.Fori(0, ITERS) as i:
                for p in range(U):
                    g = i * U + p
                    sp.wait_ge(added, (g + 1) * (STEPS * GT))
                    sp.dma_start(result[:, bass.ds(g * GT, GT), :], x_sb[:, bass.ds(g * GT, GT), :]).then_inc(stored, 16)
            sp.wait_ge(stored, 16 * GROUPS)

        @block.tensor
        def _(pe):
            def turn(g, p):
                pe.wait_ge(normed, (g + 1) * GT)
                pe.wait_ge(xnT_ready, g)
                for c in range(NC):
                    for t in range(GT):
                        ins = pe.transpose(turn_ps[:, c, t, :], xn[:, t, c * P:(c + 1) * P], ident[:, :])
                ins.then_inc(x_turned, 1)

            def route(g, p):
                pe.wait_ge(xnT_ready, g + 1)
                pe.wait_ge(weightT_ready, g)
                for t in range(GT):
                    for c in range(NC):
                        ins = pe.matmul(route_ps[:, t * E1:(t + 1) * E1], xnT[:, p, c, t, :], gate_w[:, c, :],
                                        start=(c == 0), stop=(c == NC - 1))
                ins.then_inc(routed, 1)

            def turn_weights(g, p):
                pe.wait_ge(weighed, g + 1)
                for t in range(GT):
                    ins = pe.transpose(route_ps[0:E1, 256 + t * P:256 + (t + 1) * P], weight[:, p, t, :], ident[:, :])
                ins.then_inc(weight_turned, 1)

            def bias(g, p):
                pe.wait_ge(weightT_ready, g + 1)
                pe.wait_ge(based, g * GT)
                for t in range(GT):
                    ins = pe.matmul(bias_ps[:, t, :], weightT[:, t, :], fc2_b[:, :], start=True, stop=True)
                ins.then_inc(biased, 1)

            prepare = {2: turn, 4: route, 6: turn_weights, 7: bias}

            def first(k, e, p):
                pe.wait_ge(hidden_ready, k if isinstance(k, int) else k - 1)
                for f in range(FC):
                    for c in range(NC):
                        ins = pe.matmul(mid_ps[k_parity(e)][:, f, :], fc1[:, e, c, f * P:(f + 1) * P],
                                        xnT[:, p, c, :, :], start=(c == 0), stop=(c == NC - 1))
                ins.then_inc(mid_made, 1)

            def second(k, e):
                pe.wait_ge(hidden_ready, k + 1)
                pe.wait_ge(added, k * GT - GT if e else k * GT)
                for t in range(GT):
                    for f in range(FC):
                        ins = pe.matmul(out_ps[e % 2][:, t, :], hidden[:, e % 2, f, t * P:(t + 1) * P], fc2[:, e, f, :],
                                        start=(f == 0), stop=(f == FC - 1))
                ins.then_inc(out_made, 1)

            def k_parity(e):
                return e % 2

            for stage in prepare.values():
                stage(0, 0)
            first(0, 0, 0)
            pe.wait_ge(fc2_loaded, 16)
            with pe.Fori(0, ITERS) as i:
                for p in range(U):
                    g = i * U + p
                    for e in range(STEPS):
                        k = g * STEPS + e
                        if e + 1 < STEPS:
                            first(k + 1, e + 1, p)
                        else:
                            pe.wait_ge(xnT_ready, g + 2)
                            first(k + 1, 0, 1 - p)
                        if e in prepare:
                            prepare[e](g + 1, 1 - p)
                        second(k, e)

        @block.scalar
        def _(act):
            def keep_xnT(g, p):
                act.wait_ge(x_turned, g + 1)
                act.activation(xnT[:, p, :, :, :], turn_ps[:, :, :, :], ACT.Copy).then_inc(xnT_ready, 1)

            def exp(g, p):
                act.wait_ge(shifted, g + 1)
                act.activation(prob[:, :, :], prob[:, :, :], ACT.Exp).then_inc(exped, 1)

            def keep_weights(g, p):
                act.wait_ge(weight_turned, g + 1)
                act.wait_ge(biased, g)
                act.activation(weightT[:, :, :], route_ps[0:E1, 256:512].rearrange("e (t n) -> e t n", t=GT), ACT.Copy
                               ).then_inc(weightT_ready, 1)

            prepare = {2: keep_xnT, 5: exp, 6: keep_weights}

            def gelu(k, e):
                act.wait_ge(out_made, k - 1 if e else k)
                act.wait_ge(mid_made, k + 1)
                for f in range(FC):
                    ins = act.activation(hidden[:, e % 2, f, :], mid_ps[e % 2][:, f, :], ACT.Gelu, bias=fc1_b[:, e, f:f + 1])
                ins.then_inc(hidden_ready, 1)

            for stage in prepare.values():
                stage(0, 0)
            with act.Fori(0, ITERS) as i:
                for p in range(U):
                    g = i * U + p
                    for e in range(STEPS):
                        gelu(g * STEPS + e, e)
                        if e in prepare:
                            prepare[e](g + 1, 1 - p)

        @block.vector
        def _(dve):
            LINKS = 13

            def stats_of(g, p, link):
                for t in range(GT):
                    link(dve.bn_stats(stats[:, t, :], tile_of(g * GT + t)), alone=True)
                    dve.bn_aggr(mv[:, t, :], stats[:, t, :]).then_inc(var_ready, 1)

            def normalize(g, p, link):
                dve.wait_ge(x_turned, g)
                for t in range(GT):
                    dve.wait_ge(rstd_ready, g + 1)
                    dve.tensor_scalar(xn[:, t, :], tile_of(g * GT + t), mv[:, t, 0:1], rstd[:, t:t + 1],
                                      ALU.subtract, ALU.mult).then_inc(normed, 1)

            def per_tile(x, n):
                return x.unsqueeze(2).broadcast_to([P, GT, n])

            def shift(g, p, link):
                dve.wait_ge(routed, g + 1)
                logits = route_ps[:, 0:GT * E1].rearrange("q (t e) -> q t e", t=GT)
                link(dve.tensor_reduce(top[:, :], logits, AX_X, ALU.max))
                dve.tensor_tensor(prob[:, :, :], logits, per_tile(top[:, :], E1), ALU.subtract).then_inc(shifted, 1)

            def weigh(g, p, link):
                dve.wait_ge(exped, g + 1)
                link(dve.tensor_reduce(total[:, :], prob[:, :, :], AX_X, ALU.add))
                link(dve.reciprocal(total[:, :], total[:, :]))
                link(dve.tensor_tensor(prob[:, :, :], prob[:, :, :], per_tile(total[:, :], E1), ALU.mult), alone=True)
                dve.max(best[:, 0, :], prob[:, 0, :])
                link(dve.max(best[:, 1, :], prob[:, 1, :]))
                link(dve.tensor_copy(pair[:, :, 0:TOP], best[:, :, 0:TOP]), alone=True)
                for t in range(GT):
                    ins = dve.match_replace(rest[:, t, :], pair[:, t, :], prob[:, t, :], -1.0)
                link(ins)
                link(dve.tensor_tensor(rest[:, :, :], rest[:, :, :], prob[:, :, :], ALU.not_equal))
                dve.tensor_reduce(total[:, :], pair[:, :, 0:TOP], AX_X, ALU.add)
                link(dve.tensor_tensor(rest[:, :, :], rest[:, :, :], prob[:, :, :], ALU.mult))
                link(dve.reciprocal(total[:, :], total[:, :]))
                link(dve.tensor_tensor(rest[:, :, :], rest[:, :, :], per_tile(total[:, :], E1), ALU.mult))
                dve.tensor_tensor(weight[:, p, :, :], rest[:, :, :], alpha[:, :].unsqueeze(1).broadcast_to([P, GT, E1]), ALU.mult
                                  ).then_inc(weighed, 1)

            prepare = {0: stats_of, 1: normalize, 4: shift, 5: weigh}

            def add_bias(g):
                dve.wait_ge(biased, g + 1)
                for t in range(GT):
                    dve.tensor_tensor(tile_of(g * GT + t), tile_of(g * GT + t), bias_ps[:, t, :], ALU.add).then_inc(based, 1)

            def add(g, p, e):
                k = g * STEPS + e
                dve.wait_ge(out_made, k + 1)
                for t in range(GT):
                    if e:
                        dve.wait_ge(added, k * GT + t - 1)
                    else:
                        dve.wait_ge(based, g * GT + t + 1)
                    dve.scalar_tensor_tensor(out=tile_of(g * GT + t), in0=out_ps[e % 2][:, t, :], scalar=weight[:, p, t, e:e + 1],
                                             in1=tile_of(g * GT + t), op0=ALU.mult, op1=ALU.add).then_inc(added, 1)

            dve.memset(pair[:, :, :], -2.0).then_inc(pair_set, 1)
            dve.wait_ge(pair_set, 1)
            link = Chain(dve, dve_chain, 0, passed)
            for stage in prepare.values():
                stage(0, 0, link)
            assert link.n == LINKS, link.n
            with dve.Fori(0, ITERS) as i:
                for p in range(U):
                    g = i * U + p
                    link = Chain(dve, dve_chain, (g + 1) * LINKS, passed)
                    add_bias(g)
                    for e in range(STEPS):
                        if e in prepare:
                            prepare[e](g + 1, 1 - p, link)
                        add(g, p, e)

        @block.gpsimd
        def _(pool):
            pool.memset(minus_half[:, :], -0.5).then_inc(half_set, 1)
            pool.wait_ge(half_set, 1)

            def scale_of(g):
                link = Chain(pool, pool_chain, g, passed)
                pool.wait_ge(var_ready, (g + 1) * GT)
                apart(pool, passed)
                link(pool.tensor_scalar(rstd[:, :], mv[:, :, 1], LN_EPS, None, ALU.add))
                pool.tensor_tensor(rstd[:, :], rstd[:, :], minus_half[:, :].broadcast_to([P, GT]), ALU.pow).then_inc(rstd_ready, 1)

            scale_of(0)
            with pool.Fori(0, GROUPS) as g:
                scale_of(g + 1)


def build(nc, I, out):
    with ExitStack() as ctx:
        sc = Scope(nc, ctx, "all")
        x_sb, ident = sc.sb("x", [P, NT + 2, D]), sc.sb("ident", [P, P])
        load_inputs(nc, I, x_sb, ident)
        with ExitStack() as cross:
            sc = Scope(nc, cross, "cross")
            rk_dram = nc.dram_tensor("rk", (H * RK_COPIES, RK_AHEAD + KEYS), F32).ap()
            folded_dram = nc.dram_tensor("folded1", (P, H, FOLDED), F32).ap()
            sums = sc.sb("sums", [P, 2, GROUP // P, H])
            ctxT, folded = sc.sb("ctxT", [P, KEYS]), sc.sb("folded", [P, H, FOLDED])
            fold_weights(nc, I, ident, folded, folded_dram, ctxT)
            cross_attention(nc, I, 0, x_sb, ident, ctxT, folded, None, None)
            self_attention(nc, I, x_sb, ident)
            wq = sc.sb("wq1", [P, NC, H * HD])
            routed_experts(nc, I, x_sb, ident, ctxT, sums, rk_dram, folded, folded_dram, wq)
            cross_attention(nc, I, 1, x_sb, ident, ctxT, folded, wq, rk_dram)
        w, loads = dense_weights(nc, Scope(nc, ctx, "ff1"), I)
        self_attention_fp4(nc, I, x_sb, ident, loads)
        dense_experts(nc, I, x_sb, ident, out, w)


OUT_SHAPE = (B, T, D)
NAMES = (
    ["x", "ctx_1024", "mask_BxS2_bf1"]
    + [f"L0_xattn_{n}" for n in ("Wq", "Wk", "Wv", "Wo")]
    + [f"L0_attn_{n}" for n in ("Wqkv_w", "Wqkv_b", "out_w", "out_b")]
    + [f"L0_ffn_{n}" for n in ("router_w", "w_gate", "w_up", "w_down")]
    + [f"L1_xattn_{n}" for n in ("Wq", "Wk", "Wv", "Wo", "gq", "gk")]
    + [f"L1_attn_{w}_{n}" for w in ("wq", "wk", "wv", "wo") for n in ("codes", "scales")]
    + [f"L1_attn_{n}" for n in ("bq", "bk", "bv", "bo")]
    + [f"L1_ffn_{n}" for n in ("gate_w", "fc1_w", "fc1_b", "fc2_w", "fc2_b", "alpha")]
)


def kernel(**inputs):
    import numpy as _np
    import concourse.bacc as _bacc
    from concourse import mybir as _mybir
    from concourse.bass_utils import run_bass_kernel_spmd as _run

    nc = _bacc.Bacc("TRN2", target_bir_lowering=False, num_devices=1)
    arrays, args = {}, {}
    for name in NAMES:
        a = _np.ascontiguousarray(inputs[name])
        if a.dtype == _np.bool_:
            a = a.view(_np.uint8)
        arrays[f"in_{name}_dram"] = a
        args[name] = nc.dram_tensor(f"in_{name}_dram", a.shape, _mybir.dt.from_np(a.dtype), kind="ExternalInput").ap()
    out = nc.dram_tensor("out_0_dram", OUT_SHAPE, F32, kind="ExternalOutput").ap()
    build(nc, args, out)
    r = _run(nc, [arrays], core_ids=[0])
    return r.results[0]["out_0_dram"]
```
